# Optimizing a Trainium2 kernel written in Bass

```python
import numpy as np
import jax
import jax.numpy as jnp

def _softmax(x, axis=-1):
    return jax.nn.softmax(x, axis=axis)

def _gelu(x):
    return jax.nn.gelu(x, approximate=True)

def _silu(x):
    return jax.nn.silu(x)

def _sigmoid(x):
    return jax.nn.sigmoid(x)

def _layernorm(x, axis=-1, eps=1e-05):
    m = jnp.mean(x, axis=axis, keepdims=True)
    v = jnp.var(x, axis=axis, keepdims=True)
    return (x - m) / jnp.sqrt(v + eps)

def _scatter_add(tgt, idx, src, axis=0):
    return tgt.at[idx].add(src)

def _segment_sum(src, seg, n):
    return jax.ops.segment_sum(src, seg, n)
kernel_name = 'mk_macaron_d2_jaxref_r4_11d449'

def setup_inputs(seed: int=0):
    np.random.seed(seed)
    _w = jnp.asarray

    def _L0_attn_setup():
        import jax, jax.numpy as jnp
        import numpy as np
        B, L, E, H = (1, 1024, 256, 16)
        D = E // H
        EPS = 1e-06
        key = jax.random.key(seed)
        k1, k2, k3 = jax.random.split(key, 3)
        x = jax.random.normal(k1, (B, L, E), dtype=jnp.float32)
        qkv_w = jax.random.normal(k2, (E, 3 * E), dtype=jnp.float32) / np.sqrt(E)
        qkv_b = jnp.zeros((3 * E,), dtype=jnp.float32)
        out_w = jax.random.normal(k3, (E, E), dtype=jnp.float32) / np.sqrt(E)
        out_b = jnp.zeros((E,), dtype=jnp.float32)
        return {'x': x, 'qkv_w': qkv_w, 'qkv_b': qkv_b, 'out_w': out_w, 'out_b': out_b}
    _L0_attn_in = _L0_attn_setup()

    def _L0_ffn_setup():
        import jax, jax.numpy as jnp
        import numpy as np
        import math
        E = 32
        K = 2
        CF = 1.2
        D = 256
        F = 1024
        key = jax.random.key(seed)
        ks = jax.random.split(key, 7)
        s = 0.02
        return {'x': jax.random.normal(ks[0], (4, 512, D), jnp.float32), 'gate_w': jax.random.normal(ks[1], (D, E), jnp.float32) * s, 'gate_b': jnp.zeros((E,), jnp.float32), 'w1': jax.random.normal(ks[2], (E, D, F), jnp.float32) * s, 'b1': jnp.zeros((E, F), jnp.float32), 'w2': jax.random.normal(ks[3], (E, F, D), jnp.float32) * s, 'b2': jnp.zeros((E, D), jnp.float32)}
    _L0_ffn_in = _L0_ffn_setup()

    def _L1_attn_setup():
        import jax, jax.numpy as jnp
        import numpy as np
        B, T, C = (2, 512, 256)
        NH = 16
        HS = C // NH
        BD = max(HS // 4, 16)
        HORIZON = 64
        key = jax.random.key(seed)
        ks = jax.random.split(key, 10)
        s = 0.02
        return {'x': jax.random.normal(ks[0], (B, T, C), dtype=jnp.float32), 'W_disp': jax.random.normal(ks[1], (NH * BD, C), dtype=jnp.float32) * s, 'W_val': jax.random.normal(ks[2], (C, C), dtype=jnp.float32) * s, 'rel_pos_emb': jax.random.normal(ks[3], (HORIZON, BD), dtype=jnp.float32) * s, 'strain_fused_w': jax.random.normal(ks[4], (2 * BD, BD), dtype=jnp.float32) * s, 'strain_fused_b': jnp.zeros((2 * BD,), dtype=jnp.float32), 'pos_proj_w': jax.random.normal(ks[5], (BD, BD), dtype=jnp.float32) * s, 'bond_out_w': jax.random.normal(ks[6], (1, BD), dtype=jnp.float32) * s, 'damage_out_w': jax.random.normal(ks[7], (1, BD), dtype=jnp.float32) * s, 'damage_out_b': jnp.full((1,), -3.0, dtype=jnp.float32), 'c_proj_w': jax.random.normal(ks[8], (C, C), dtype=jnp.float32) * s}
    _L1_attn_in = _L1_attn_setup()

    def _L1_ffn_setup():
        import jax, jax.numpy as jnp
        import numpy as np
        D_MODEL = 256
        EXPANSION = 4
        D_HIDDEN = D_MODEL * EXPANSION
        NUM_STAGES = int(np.log2(D_HIDDEN))

        def butterfly(y, weights, dim):
            lead = y.shape[:-1]
            for stage in range(weights.shape[0]):
                s = 2 ** stage
                nb = dim // (2 * s)
                yr = y.reshape(*lead, nb, 2, s)
                a = yr[..., 0, :]
                b = yr[..., 1, :]
                w = weights[stage].reshape(nb, s, 2, 2)
                na = w[..., 0, 0] * a + w[..., 0, 1] * b
                nb2 = w[..., 1, 0] * a + w[..., 1, 1] * b
                y = jnp.stack([na, nb2], axis=-2).reshape(*lead, dim)
            return y
        key = jax.random.key(seed)
        ks = jax.random.split(key, 6)
        B, S = (4, 512)
        x = jax.random.normal(ks[0], (B, S, D_MODEL), jnp.float32)
        W_exp = jax.random.normal(ks[1], (D_MODEL, D_HIDDEN), jnp.float32) * 0.02
        b_exp = jnp.zeros((D_HIDDEN,), jnp.float32)
        up_weights = jax.random.normal(ks[2], (NUM_STAGES, D_HIDDEN // 2, 2, 2), jnp.float32) * 0.02
        up_bias = jnp.zeros((D_HIDDEN,), jnp.float32)
        down_weights = jax.random.normal(ks[3], (NUM_STAGES, D_HIDDEN // 2, 2, 2), jnp.float32) * 0.02
        W_con = jax.random.normal(ks[4], (D_HIDDEN, D_MODEL), jnp.float32) * 0.02
        b_con = jnp.zeros((D_MODEL,), jnp.float32)
        down_bias = jnp.zeros((D_MODEL,), jnp.float32)
        return dict(x=x, W_exp=W_exp, b_exp=b_exp, up_weights=up_weights, up_bias=up_bias, down_weights=down_weights, W_con=W_con, b_con=b_con, down_bias=down_bias)
    _L1_ffn_in = _L1_ffn_setup()
    _d = {'L0_attn_x': _L0_attn_in['x'], 'L0_attn_qkv_w': _L0_attn_in['qkv_w'], 'L0_attn_qkv_b': _L0_attn_in['qkv_b'], 'L0_attn_out_w': _L0_attn_in['out_w'], 'L0_attn_out_b': _L0_attn_in['out_b'], 'L0_ffn_gate_w': _L0_ffn_in['gate_w'], 'L0_ffn_gate_b': _L0_ffn_in['gate_b'], 'L0_ffn_w1': _L0_ffn_in['w1'], 'L0_ffn_b1': _L0_ffn_in['b1'], 'L0_ffn_w2': _L0_ffn_in['w2'], 'L0_ffn_b2': _L0_ffn_in['b2'], 'L1_attn_W_disp': _L1_attn_in['W_disp'], 'L1_attn_W_val': _L1_attn_in['W_val'], 'L1_attn_rel_pos_emb': _L1_attn_in['rel_pos_emb'], 'L1_attn_strain_fused_w': _L1_attn_in['strain_fused_w'], 'L1_attn_strain_fused_b': _L1_attn_in['strain_fused_b'], 'L1_attn_pos_proj_w': _L1_attn_in['pos_proj_w'], 'L1_attn_bond_out_w': _L1_attn_in['bond_out_w'], 'L1_attn_damage_out_w': _L1_attn_in['damage_out_w'], 'L1_attn_damage_out_b': _L1_attn_in['damage_out_b'], 'L1_attn_c_proj_w': _L1_attn_in['c_proj_w'], 'L1_ffn_W_exp': _L1_ffn_in['W_exp'], 'L1_ffn_b_exp': _L1_ffn_in['b_exp'], 'L1_ffn_up_weights': _L1_ffn_in['up_weights'], 'L1_ffn_up_bias': _L1_ffn_in['up_bias'], 'L1_ffn_down_weights': _L1_ffn_in['down_weights'], 'L1_ffn_W_con': _L1_ffn_in['W_con'], 'L1_ffn_b_con': _L1_ffn_in['b_con'], 'L1_ffn_down_bias': _L1_ffn_in['down_bias']}
    _x0 = _d['L0_attn_x']
    _d['L0_attn_x'] = jax.random.normal(jax.random.fold_in(jax.random.key(seed), 1), (1, 4096, 256), dtype=_x0.dtype)
    del _x0
    return _d

def reference(L0_attn_x, L0_attn_qkv_w, L0_attn_qkv_b, L0_attn_out_w, L0_attn_out_b, L0_ffn_gate_w, L0_ffn_gate_b, L0_ffn_w1, L0_ffn_b1, L0_ffn_w2, L0_ffn_b2, L1_attn_W_disp, L1_attn_W_val, L1_attn_rel_pos_emb, L1_attn_strain_fused_w, L1_attn_strain_fused_b, L1_attn_pos_proj_w, L1_attn_bond_out_w, L1_attn_damage_out_w, L1_attn_damage_out_b, L1_attn_c_proj_w, L1_ffn_W_exp, L1_ffn_b_exp, L1_ffn_up_weights, L1_ffn_up_bias, L1_ffn_down_weights, L1_ffn_W_con, L1_ffn_b_con, L1_ffn_down_bias):

    def _L0_attn_ref(x, qkv_w, qkv_b, out_w, out_b):
        import jax, jax.numpy as jnp
        import numpy as np
        B, L, E, H = (1, 1024, 256, 16)
        D = E // H
        EPS = 1e-06
        b, l, e = x.shape
        qkv = x @ qkv_w + qkv_b
        q, k, v = jnp.split(qkv, 3, axis=-1)
        q = q.reshape(b, l, H, D).transpose(0, 2, 1, 3)
        k = k.reshape(b, l, H, D).transpose(0, 2, 1, 3)
        v = v.reshape(b, l, H, D).transpose(0, 2, 1, 3)
        q_prime = jax.nn.elu(q) + 1.0
        k_prime = jax.nn.elu(k) + 1.0
        kv_prod = jnp.einsum('bhld,bhle->bhlde', k_prime, v)
        kv_cumsum = jnp.cumsum(kv_prod, axis=2)
        context = jnp.einsum('bhld,bhlde->bhle', q_prime, kv_cumsum)
        k_cumsum = jnp.cumsum(k_prime, axis=2)
        norm = jnp.einsum('bhld,bhld->bhl', q_prime, k_cumsum)
        output = context / (norm[..., None] + EPS)
        output = output.transpose(0, 2, 1, 3).reshape(b, l, e)
        return output @ out_w + out_b

    def _L0_ffn_ref(x, gate_w, gate_b, w1, b1, w2, b2):
        import jax, jax.numpy as jnp
        import numpy as np
        import math
        E = 32
        K = 2
        CF = 1.2
        D = 256
        F = 1024
        orig_shape = x.shape
        xt = x.reshape(-1, D)
        T = xt.shape[0]
        C = int(math.ceil(T * K / E * CF))
        logits = xt @ gate_w + gate_b
        probs = jax.nn.softmax(logits, axis=-1)
        top_w, top_i = jax.lax.top_k(probs, K)
        w = top_w / jnp.sum(top_w, axis=-1, keepdims=True)
        flat_e = top_i.reshape(-1)
        oh = jax.nn.one_hot(flat_e, E, dtype=jnp.int32)
        pos_all = jnp.cumsum(oh, axis=0) - 1
        pos = jnp.take_along_axis(pos_all, flat_e[:, None], axis=1)[:, 0]
        valid = pos < C
        pos_d = jnp.where(valid, pos, C)
        x_rep = jnp.repeat(xt, K, axis=0)
        xe = jnp.zeros((E, C, D), x.dtype).at[flat_e, pos_d].add(x_rep, mode='drop')
        he = jax.nn.gelu(jnp.einsum('ecd,edf->ecf', xe, w1) + b1[:, None, :], approximate=False)
        ye = jnp.einsum('ecf,efd->ecd', he, w2) + b2[:, None, :]
        y_flat = ye[flat_e, jnp.minimum(pos, C - 1)] * valid[:, None].astype(x.dtype)
        y = (y_flat.reshape(T, K, D) * w[..., None]).sum(axis=1)
        return y.reshape(orig_shape)

    def _L1_attn_ref(x, W_disp, W_val, rel_pos_emb, strain_fused_w, strain_fused_b, pos_proj_w, bond_out_w, damage_out_w, damage_out_b, c_proj_w):
        import jax, jax.numpy as jnp
        import numpy as np
        B, T, C = (2, 512, 256)
        NH = 16
        HS = C // NH
        BD = max(HS // 4, 16)
        HORIZON = 64
        Bx, Tx, Cx = x.shape
        delta = min(HORIZON, Tx)
        gelu = lambda t: jax.nn.gelu(t, approximate=False)
        disp = (x @ W_disp.T).reshape(Bx, Tx, NH, BD).transpose(0, 2, 1, 3)
        val = (x @ W_val.T).reshape(Bx, Tx, NH, HS).transpose(0, 2, 1, 3)
        pad = ((0, 0), (0, 0), (delta - 1, 0), (0, 0))
        idx = jnp.arange(Tx)[:, None] + jnp.arange(delta)[None, :]
        disp_win = jnp.pad(disp, pad)[:, :, idx, :]
        strain = disp_win - disp[:, :, :, None, :]
        fused = strain @ strain_fused_w.T + strain_fused_b
        bond_feats, damage_feats = (fused[..., :BD], fused[..., BD:])
        pos_feat = rel_pos_emb[:delta] @ pos_proj_w.T
        bond_logits = (gelu(bond_feats + pos_feat) @ bond_out_w.T)[..., 0]
        damage = jax.nn.sigmoid((gelu(damage_feats) @ damage_out_w.T)[..., 0] + damage_out_b)
        logits = bond_logits - damage * 10.0
        cmask = jnp.arange(Tx)[:, None] - delta + 1 + jnp.arange(delta)[None, :] >= 0
        logits = jnp.where(cmask, logits, -jnp.inf)
        weights = jax.nn.softmax(logits, axis=-1)
        val_win = jnp.pad(val, pad)[:, :, idx, :]
        out = jnp.einsum('bhtw,bhtwd->bhtd', weights, val_win)
        out = out.transpose(0, 2, 1, 3).reshape(Bx, Tx, Cx)
        return out @ c_proj_w.T

    def _L1_ffn_ref(x, W_exp, b_exp, up_weights, up_bias, down_weights, W_con, b_con, down_bias):
        import jax, jax.numpy as jnp
        import numpy as np
        D_MODEL = 256
        EXPANSION = 4
        D_HIDDEN = D_MODEL * EXPANSION
        NUM_STAGES = int(np.log2(D_HIDDEN))

        def butterfly(y, weights, dim):
            lead = y.shape[:-1]
            for stage in range(weights.shape[0]):
                s = 2 ** stage
                nb = dim // (2 * s)
                yr = y.reshape(*lead, nb, 2, s)
                a = yr[..., 0, :]
                b = yr[..., 1, :]
                w = weights[stage].reshape(nb, s, 2, 2)
                na = w[..., 0, 0] * a + w[..., 0, 1] * b
                nb2 = w[..., 1, 0] * a + w[..., 1, 1] * b
                y = jnp.stack([na, nb2], axis=-2).reshape(*lead, dim)
            return y
        h = jnp.einsum('bsd,dh->bsh', x, W_exp) + b_exp
        h = butterfly(h, up_weights, D_HIDDEN)
        h = jax.nn.gelu(h + up_bias, approximate=False)
        h = butterfly(h, down_weights, D_HIDDEN)
        y = jnp.einsum('bsh,hd->bsd', h, W_con) + b_con
        return y + down_bias
    x = L0_attn_x
    x = x + 0.5 * _L0_ffn_ref(_layernorm(x, axis=-1), L0_ffn_gate_w, L0_ffn_gate_b, L0_ffn_w1, L0_ffn_b1, L0_ffn_w2, L0_ffn_b2)
    x = x + _L0_attn_ref(_layernorm(x, axis=-1), L0_attn_qkv_w, L0_attn_qkv_b, L0_attn_out_w, L0_attn_out_b)
    x = x + 0.5 * _L0_ffn_ref(_layernorm(x, axis=-1), L0_ffn_gate_w, L0_ffn_gate_b, L0_ffn_w1, L0_ffn_b1, L0_ffn_w2, L0_ffn_b2)
    x = x + 0.5 * _L1_ffn_ref(_layernorm(x, axis=-1), L1_ffn_W_exp, L1_ffn_b_exp, L1_ffn_up_weights, L1_ffn_up_bias, L1_ffn_down_weights, L1_ffn_W_con, L1_ffn_b_con, L1_ffn_down_bias)
    x = x + _L1_attn_ref(_layernorm(x, axis=-1), L1_attn_W_disp, L1_attn_W_val, L1_attn_rel_pos_emb, L1_attn_strain_fused_w, L1_attn_strain_fused_b, L1_attn_pos_proj_w, L1_attn_bond_out_w, L1_attn_damage_out_w, L1_attn_damage_out_b, L1_attn_c_proj_w)
    x = x + 0.5 * _L1_ffn_ref(_layernorm(x, axis=-1), L1_ffn_W_exp, L1_ffn_b_exp, L1_ffn_up_weights, L1_ffn_up_bias, L1_ffn_down_weights, L1_ffn_W_con, L1_ffn_b_con, L1_ffn_down_bias)
    return x

_drawn_inputs = setup_inputs


def setup_inputs(seed=0):
    import zlib

    import numpy as np

    out = dict(_drawn_inputs(seed))
    spreads = {'L0_attn_qkv_b': (0.0, 0.1),
     'L0_attn_out_b': (0.0, 0.1),
     'L0_ffn_gate_b': (0.0, 0.1),
     'L0_ffn_b1': (0.0, 0.348),
     'L0_ffn_b2': (0.0, 0.1),
     'L1_attn_strain_fused_b': (0.0, 2.0),
     'L1_ffn_b_exp': (0.0, 0.1),
     'L1_ffn_up_bias': (0.0, 0.1),
     'L1_ffn_b_con': (0.0, 0.1),
     'L1_ffn_down_bias': (0.0, 0.1)}
    factors = {'L1_attn_W_disp': 43.445,
     'L1_attn_rel_pos_emb': 64.0,
     'L1_attn_strain_fused_w': 32.12,
     'L1_attn_pos_proj_w': 64.0,
     'L1_attn_bond_out_w': 31.346,
     'L1_attn_damage_out_w': 64.0}
    for name, (base, spread) in spreads.items():
        noise = np.random.default_rng([zlib.crc32(name.encode()), seed]).standard_normal(out[name].shape)
        drawn = base * np.exp(spread * noise) if base else spread * noise
        out[name] = jnp.asarray(drawn.astype(out[name].dtype))
    for name, factor in factors.items():
        out[name] = (out[name] * factor).astype(out[name].dtype)
    return out
```

```python
import math
from contextlib import ExitStack

import concourse.bass as bass
from concourse import mybir

F32 = mybir.dt.float32
I32 = mybir.dt.int32
ALU = mybir.AluOpType
ACT = mybir.ActivationFunctionType
AX = mybir.AxisListType

P = 128
D = 256
DK = D // P
GT = 4
GW = GT * P
LN_EPS = 1e-5

LEAD = 128


def after(n):
    return n + 1 + LEAD


def landed(n, dmas=1):
    return 16 * dmas * (n + 2)


def sw_landed(n, dmas=1):
    return 16 * dmas * (n + 1)


def turns(eng, n, body):
    body(0)
    with eng.Fori(1, n) as i:
        body(i)


def at(t, n=1):
    return bass.ds(t, n)


def spread(ap, axis, n):
    shape = list(ap.shape)
    shape.insert(axis, n)
    return ap.unsqueeze(axis).broadcast_to(shape)


class Phase:

    def __init__(self, nc, memory, tag):
        self.nc, self.memory, self.tag, self.taken = nc, memory, tag, []
        memory.callback(self.give_back)

    def sb(self, name, shape, dt=F32):
        return self.memory.enter_context(self.nc.sbuf_tensor(f"{self.tag}_{name}", shape, dt))

    def ps(self, name, shape):
        return self.memory.enter_context(self.nc.psum_tensor(f"{self.tag}_{name}", shape, F32))

    def sem(self, name):
        self.taken.append(self.nc.alloc_semaphore(name=f"{self.tag}_{name}"))
        return self.taken[-1]

    def sems(self, name):
        return [self.sem(f"{name}{p}") for p in range(2)]

    def pool_dma_sems(self, name):
        return [self.nc.alloc_semaphore(name=f"{self.tag}_{name}{p}") for p in range(2)]

    def give_back(self):
        with self.nc.Block() as block:
            @block.gpsimd
            def _(pool):
                for sem in self.taken:
                    pool.sem_clear(sem)
        for sem in self.taken:
            self.nc.release_semaphore(sem)


def chain(eng, sem):
    count = [0]

    def link(ins):
        count[0] += 1
        ins.then_inc(sem, 1)
        eng.wait_ge(sem, count[0])

    return link


def make_constants(nc, ph, NT, E, C, H, BD):
    c = {
        "ident": ph.sb("ident", [P, P]),
        "lower": ph.sb("lower", [P, P]),
        "causal": ph.sb("causal", [P, P]),
        "ones": ph.sb("ones", [P, P]),
        "rev": ph.sb("rev", [P, E]),
        "dump": ph.sb("dump", [P, 2, NT]),
        "keep": ph.sb("keep", [P, E, NT]),
        "head_block": ph.sb("head_block", [P, P // BD, BD + 1]),
        "parity": ph.sb("parity", [P, 2]),
        "neg_half": ph.sb("neg_half", [P, NT]),
    }
    with ExitStack() as memory:
        tmp = Phase(nc, memory, "cst")
        rev_i = tmp.sb("rev_i", [P, E], I32)
        dump_i = tmp.sb("dump_i", [P, 2, NT], I32)
        filled, shaped, ints = tmp.sem("filled"), tmp.sem("shaped"), tmp.sem("ints")
        block = memory.enter_context(nc.Block())

        @block.gpsimd
        def _(pool):
            nc.gpsimd.memset(c["ident"][:], 0.0).then_inc(filled, 1)
            for name in ("lower", "causal", "ones", "head_block"):
                nc.gpsimd.memset(c[name][:], 1.0).then_inc(filled, 1)
            nc.gpsimd.iota(rev_i[:], pattern=[[-1, E]], base=E, channel_multiplier=0).then_inc(ints, 1)
            nc.gpsimd.iota(dump_i[:], pattern=[[1, 2], [2 * P, NT]], base=E * C, channel_multiplier=2).then_inc(ints, 1)
            pool.wait_ge(filled, 5)
            nc.gpsimd.affine_select(out=c["ident"][:], in_=c["ident"][:], compare_op=ALU.not_equal, fill=1.0,
                                    base=0, pattern=[[-1, P]], channel_multiplier=1).then_inc(shaped, 1)
            nc.gpsimd.affine_select(out=c["lower"][:], in_=c["lower"][:], compare_op=ALU.is_gt, fill=0.0,
                                    base=0, pattern=[[1, P]], channel_multiplier=-1).then_inc(shaped, 1)
            nc.gpsimd.affine_select(out=c["causal"][:], in_=c["causal"][:], compare_op=ALU.is_ge, fill=0.0,
                                    base=0, pattern=[[1, P]], channel_multiplier=-1).then_inc(shaped, 1)
            hb = c["head_block"]
            nh = P // BD
            nc.gpsimd.affine_select(out=hb[:], in_=hb[:], compare_op=ALU.is_ge, fill=0.0, base=0,
                                    pattern=[[-BD, nh], [0, BD + 1]], channel_multiplier=1).then_inc(shaped, 1)
            pool.wait_ge(shaped, 4)
            nc.gpsimd.affine_select(out=hb[:], in_=hb[:], compare_op=ALU.is_ge, fill=0.0, base=BD - 1,
                                    pattern=[[BD, nh], [0, BD + 1]], channel_multiplier=-1).then_inc(shaped, 1)

        @block.vector
        def _(dve):
            dve.wait_ge(ints, 2)
            nc.vector.tensor_copy(c["rev"][:], rev_i[:])
            nc.vector.tensor_copy(c["dump"][:], dump_i[:])
            nc.vector.memset(c["keep"][:], 1.0).then_inc(ints, 1)
            nc.vector.memset(c["neg_half"][:], -0.5)
            dve.wait_ge(ints, 3)
            nc.vector.memset(c["keep"][:, :, 0:1], 0.0)
            dve.wait_ge(shaped, 5)
            pairs = c["head_block"][:, :, 0].rearrange("p (h two) -> p two h", two=2)
            nc.vector.reduce_sum(c["parity"][:], pairs, AX.X)
    return c


def layer_norm_stats(nc, tag, x_res, mean, rstd, neg_half, NT):
    with ExitStack() as memory:
        ph = Phase(nc, memory, tag)
        stats = ph.sb("stats", [P, NT, 6])
        msum, mdif, m2, var = (ph.sb(n, [P, NT]) for n in ("msum", "mdif", "m2", "var"))
        stats_done, moments, rstd_ready = ph.sem("stats_done"), ph.sem("moments"), ph.sem("rstd_ready")
        block = memory.enter_context(nc.Block())

        @block.vector
        def _(dve):
            with dve.Fori(0, NT // 4) as i:
                for j in range(4):
                    nc.vector.bn_stats(stats[:, at(4 * i + j), :].rearrange("p a s -> p (a s)"),
                                       x_res[:, at(4 * i + j), :].rearrange("p a d -> p (a d)")).then_inc(stats_done, 1)
            dve.wait_ge(stats_done, NT)
            even, odd = stats[:, :, 1], stats[:, :, 4]
            nc.vector.tensor_tensor(msum[:], even, odd, ALU.add).then_inc(moments, 1)
            nc.vector.tensor_tensor(mdif[:], even, odd, ALU.subtract).then_inc(moments, 1)
            nc.vector.tensor_tensor(m2[:], stats[:, :, 2], stats[:, :, 5], ALU.add).then_inc(moments, 1)
            dve.wait_ge(moments, 3)
            nc.vector.tensor_scalar(mean[:], msum[:], 0.5, None, ALU.mult).then_inc(moments, 1)
            nc.vector.tensor_tensor(mdif[:], mdif[:], mdif[:], ALU.mult).then_inc(moments, 1)
            nc.vector.tensor_scalar(m2[:], m2[:], 1.0 / D, LN_EPS, ALU.mult, ALU.add).then_inc(moments, 1)
            dve.wait_ge(moments, 6)
            nc.vector.scalar_tensor_tensor(out=var[:], in0=mdif[:], scalar=0.25, in1=m2[:],
                                           op0=ALU.mult, op1=ALU.add).then_inc(moments, 1)

        @block.gpsimd
        def _(pool):
            pool.wait_ge(moments, 7)
            nc.gpsimd.tensor_tensor(rstd[:], var[:], neg_half[:], ALU.pow).then_inc(rstd_ready, 1)
            pool.wait_ge(rstd_ready, 1)


def moe_route(nc, tag, T, E, C, x_res, mean, rstd, cst, gate_w, gate_b, xe, gather_row, weight,
              first):
    NT, G = T // P, T // GW
    ident = cst["ident"]
    with ExitStack() as memory:
        ph = Phase(nc, memory, tag)
        gw, gb = ph.sb("gw", [P, DK, E]), ph.sb("gb", [P, E])
        xn = [ph.sb(f"xn{p}", [P, GT, D]) for p in range(2)]
        xnT = [ph.sb(f"xnT{p}", [P, DK, GW]) for p in range(2)]
        logits, work, work2 = (ph.sb(n, [P, NT, E]) for n in ("logits", "work", "work2"))
        hot = [ph.sb(f"hot{k}", [P, NT, E]) for k in range(2)]
        best, rank, place, first_row, valid, row, share = (
            [ph.sb(f"{n}{k}", [P, NT]) for k in range(2)]
            for n in ("best", "rank", "place", "first_row", "valid", "row", "share"))
        totals, scan = ph.sb("totals", [P, E, NT]), ph.sb("scan", [P, E, NT])
        scatter_row = ph.sb("scatter_row", [P, NT, 2], I32)
        stage_row = [ph.sb(f"stage_row{p}", [P, 2], I32) for p in range(2)]
        stage_x = [ph.sb(f"stage_x{p}", [P, D]) for p in range(2)]
        ZW = 2048
        zeros = ph.sb("zeros", [P, ZW]) if first else None
        pT = [ph.ps(f"pT{p}", [P, DK, GW]) for p in range(2)]
        pL = [ph.ps(f"pL{p}", [P, GT, E]) for p in range(2)]

        gate_loaded, zeros_ready, zeroed = ph.sem("gate_loaded"), ph.sem("zeros_ready"), ph.sem("zeroed")
        xn_ready, xT_in_psum, xnT_ready, logits_in_psum, logits_ready = (
            ph.sem(n) for n in ("xn_ready", "xT_in_psum", "xnT_ready", "logits_in_psum", "logits_ready"))
        step, gap_ready, ratio_ready, hot_ready, counts_in_psum = (
            ph.sem(n) for n in ("step", "gap_ready", "ratio_ready", "hot_ready", "counts_in_psum"))
        staged, scattered, turn = ph.sem("staged"), ph.pool_dma_sems("scattered"), ph.sem("turn")
        block = memory.enter_context(nc.Block())

        @block.sync
        def _(sp):
            sp.dma_start(gw[:], gate_w.rearrange("(k p) e -> p k e", p=P)).then_inc(gate_loaded, 16)
            sp.dma_start(gb[:], gate_b.partition_broadcast(P)).then_inc(gate_loaded, 16)
            if first:
                sp.wait_ge(zeros_ready, 1)
                flat = xe[0:E * C, :].rearrange("r d -> (r d)")
                whole, rest = divmod(E * C * D, P * ZW)
                for z in range(whole):
                    sp.dma_start(flat[z * P * ZW:(z + 1) * P * ZW].rearrange("(p f) -> p f", p=P),
                                 zeros[:]).then_inc(zeroed, 16)
                sp.dma_start(flat[whole * P * ZW:].rearrange("(p f) -> p f", p=P),
                             zeros[:, 0:rest // P]).then_inc(zeroed, 16)
                sp.wait_ge(zeroed, 16 * (whole + 1))

        @block.vector
        def _(dve):
            dve.sem_inc(xn_ready, LEAD)
            dve.sem_inc(logits_ready, LEAD)
            dve.sem_inc(staged, LEAD)
            if first:
                nc.vector.memset(zeros[:], 0.0).then_inc(zeros_ready, 1)
            dve.wait_ge(gate_loaded, 32)
            with dve.Fori(0, G // 2) as i:
                for p in range(2):
                    g = 2 * i + p
                    dve.wait_ge(xT_in_psum, after(g - 2))
                    for j in range(GT):
                        t = GT * g + j
                        nc.vector.tensor_scalar(xn[p][:, j:j + 1, :], x_res[:, at(t), :], mean[:, at(t)],
                                                rstd[:, at(t)], ALU.subtract, ALU.mult).then_inc(xn_ready, 1)
                    dve.wait_ge(logits_in_psum, after(g))
                    nc.vector.tensor_tensor(logits[:, at(GT * g, GT), :], pL[p][:], spread(gb[:], 1, GT),
                                            ALU.add).then_inc(logits_ready, 1)
            dve.wait_ge(logits_ready, after(G - 1))

            link = chain(dve, step)
            rev = spread(cst["rev"][:], 1, NT)
            for k, src in ((0, logits), (1, work2)):
                link(nc.vector.reduce_max(best[k][:], src[:], AX.X))
                link(nc.vector.tensor_tensor(work[:], src[:], spread(best[k][:], 2, E), ALU.is_equal))
                link(nc.vector.tensor_tensor(work[:], work[:], rev, ALU.mult))
                link(nc.vector.reduce_max(rank[k][:], work[:], AX.X))
                link(nc.vector.tensor_tensor(hot[k][:], rev, spread(rank[k][:], 2, E), ALU.is_equal))
                if k == 0:
                    link(nc.vector.scalar_tensor_tensor(out=work2[:], in0=hot[0][:], scalar=-1e38, in1=src[:],
                                                        op0=ALU.mult, op1=ALU.add))
            nc.vector.tensor_tensor(work[:], hot[0][:], hot[1][:], ALU.add).then_inc(hot_ready, 1)
            link(nc.vector.tensor_tensor(share[1][:], best[1][:], best[0][:], ALU.subtract))
            dve.sem_inc(gap_ready, 1)
            dve.wait_ge(ratio_ready, 1)
            link(nc.vector.tensor_scalar(share[0][:], valid[0][:], 1.0, None, ALU.add))
            link(nc.vector.reciprocal(share[0][:], share[0][:]))
            link(nc.vector.tensor_tensor(share[1][:], valid[0][:], share[0][:], ALU.mult))

            dve.wait_ge(counts_in_psum, 1)
            link(nc.vector.tensor_copy(totals[:], pT_view(pT[1], NT, E).rearrange("p t e -> p e t")))
            link(nc.vector.tensor_tensor_scan(scan[:].rearrange("p e t -> p (e t)"),
                                              cst["keep"][:].rearrange("p e t -> p (e t)"),
                                              totals[:].rearrange("p e t -> p (e t)"), 0.0, ALU.mult, ALU.add))
            link(nc.vector.tensor_tensor(totals[:], scan[:], totals[:], ALU.subtract))
            link(nc.vector.tensor_tensor(work2[:], pT_view(pT[0], NT, E), totals[:].rearrange("p e t -> p t e"),
                                         ALU.add))
            for k in range(2):
                link(nc.vector.tensor_tensor(work[:], work2[:], hot[k][:], ALU.mult))
                link(nc.vector.reduce_sum(place[k][:], work[:], AX.X))
                link(nc.vector.tensor_scalar(first_row[k][:], rank[k][:], -float(C), float(E * C), ALU.mult, ALU.add))
                link(nc.vector.tensor_scalar(valid[k][:], place[k][:], float(C), None, ALU.is_lt))
                link(nc.vector.scalar_tensor_tensor(out=gather_row[:, :, k], in0=place[k][:], scalar=float(C - 1),
                                                    in1=first_row[k][:], op0=ALU.min, op1=ALU.add))
                link(nc.vector.tensor_tensor(row[k][:], place[k][:], first_row[k][:], ALU.add))
                link(nc.vector.tensor_tensor(row[k][:], row[k][:], cst["dump"][:, k, :], ALU.subtract))
                link(nc.vector.tensor_tensor(row[k][:], row[k][:], valid[k][:], ALU.mult))
                link(nc.vector.tensor_tensor(scatter_row[:, :, k], row[k][:], cst["dump"][:, k, :], ALU.add))
                link(nc.vector.scalar_tensor_tensor(out=weight[:, :, k], in0=share[k][:], scalar=0.5,
                                                    in1=valid[k][:], op0=ALU.mult, op1=ALU.mult))
            def stage(i):
                for p in range(2):
                    t = 2 * i + p
                    if not (isinstance(i, int) and i == 0):
                        dve.wait_ge(scattered[p], sw_landed(i - 1, 2))
                    nc.vector.tensor_copy(stage_row[p][:], scatter_row[:, at(t), :].rearrange("p a k -> p (a k)")
                                          ).then_inc(staged, 1)
                    nc.vector.tensor_scalar(stage_x[p][:], x_res[:, at(t), :].rearrange("p a d -> p (a d)"),
                                            mean[:, at(t)], rstd[:, at(t)], ALU.subtract,
                                            ALU.mult).then_inc(staged, 1)

            turns(dve, NT // 2, stage)

        @block.scalar
        def _(act):
            act.sem_inc(xnT_ready, LEAD)
            with act.Fori(0, G // 2) as i:
                for p in range(2):
                    g = 2 * i + p
                    act.wait_ge(xT_in_psum, after(g))
                    act.wait_ge(logits_in_psum, after(g - 2))
                    nc.scalar.activation(xnT[p][:], pT[p][:], ACT.Copy).then_inc(xnT_ready, 1)
            act.wait_ge(gap_ready, 1)
            nc.scalar.activation(valid[0][:], share[1][:], ACT.Exp).then_inc(ratio_ready, 1)

        @block.tensor
        def _(pe):
            pe.sem_inc(xT_in_psum, LEAD)
            pe.sem_inc(logits_in_psum, LEAD)
            pe.wait_ge(gate_loaded, 32)
            with pe.Fori(0, G // 2) as i:
                for p in range(2):
                    g = 2 * i + p
                    pe.wait_ge(xn_ready, after(GT * g + GT - 1))
                    pe.wait_ge(xnT_ready, after(g - 2))
                    for j in range(GT):
                        for k in range(DK):
                            last = nc.tensor.transpose(pT[p][:, k, j * P:(j + 1) * P],
                                                       xn[p][:, j, k * P:(k + 1) * P], ident[:])
                    last.then_inc(xT_in_psum, 1)
                    pe.wait_ge(xnT_ready, after(g))
                    pe.wait_ge(logits_ready, after(g - 2))
                    for j in range(GT):
                        for k in range(DK):
                            last = nc.tensor.matmul(pL[p][:, j, :], xnT[p][:, k, j * P:(j + 1) * P], gw[:, k, :],
                                                    start=(k == 0), stop=(k == DK - 1))
                    last.then_inc(logits_in_psum, 1)
            pe.wait_ge(hot_ready, 1)
            for m, src in ((0, cst["lower"]), (1, cst["ones"])):
                for h in range(NT * E // 512):
                    last = nc.tensor.matmul(pT_view(pT[m], NT, E)[:, h * 512 // E:(h + 1) * 512 // E, :], src[:],
                                            work[:, h * 512 // E:(h + 1) * 512 // E, :], start=True, stop=True)
            last.then_inc(counts_in_psum, 1)

        @block.gpsimd
        def _(pool):
            if first:
                pool.wait_ge(zeroed, 16 * (math.ceil(E * C * D / (P * ZW))))
            with pool.Fori(0, NT // 2) as i:
                for p in range(2):
                    t = 2 * i + p
                    pool.wait_ge(staged, after(2 * t + 1))
                    pool.sem_inc(turn, 1)
                    for k in range(2):
                        pool.indirect_dma_start(
                            out=xe, out_offset=bass.IndirectOffsetOnAxis(ap=stage_row[p][:, k:k + 1], axis=0),
                            in_=stage_x[p][:], in_offset=None).then_inc(scattered[p], 16)
            for p in range(2):
                pool.wait_ge(scattered[p], sw_landed(NT // 2 - 1, 2))


def pT_view(bank_pair, NT, E):
    return bank_pair[:].rearrange("p a b -> p (a b)").rearrange("p (t e) -> p t e", e=E)


def moe_experts(nc, tag, E, C, F, xe, ye, cst, w1, b1, w2, b2):
    ident = cst["ident"]
    FK = F // P
    tiles = [(j * P, min(P, C - j * P)) for j in range(math.ceil(C / P))]
    NJ = len(tiles)
    whole = C // P
    with ExitStack() as memory:
        ph = Phase(nc, memory, tag)
        w1s = [ph.sb(f"w1s{p}", [P, DK, F]) for p in range(2)]
        w2s = [ph.sb(f"w2s{p}", [P, FK, D]) for p in range(2)]
        b2s = [ph.sb(f"b2s{p}", [P, D]) for p in range(2)]
        b1r, b1T = ph.sb("b1r", [E, F]), ph.sb("b1T", [P, FK, E])
        xr = [ph.sb(f"xr{p}", [P, NJ, D]) for p in range(2)]
        xT = [ph.sb(f"xT{p}", [P, DK, C]) for p in range(2)]
        hT = [ph.sb(f"hT{p}", [P, FK, C]) for p in range(2)]
        yo = [ph.sb(f"yo{p}", [P, NJ, D]) for p in range(2)]
        pX = ph.ps("pX", [P, DK, 512])
        NH = 4
        pH = ph.ps("pH", [P, NH, 512])
        pY = ph.ps("pY", [P, 2, 512])

        b1_loaded, b1_in_psum, b1_ready = ph.sem("b1_loaded"), ph.sem("b1_in_psum"), ph.sem("b1_ready")
        w1_loaded, w2_loaded, b2_loaded, x_loaded = (
            ph.sems(n) for n in ("w1_loaded", "w2_loaded", "b2_loaded", "x_loaded"))
        stored = ph.pool_dma_sems("stored")
        xT_in_psum, xT_ready, h_in_psum, h_ready, y_in_psum, y_ready = (
            ph.sem(n) for n in ("xT_in_psum", "xT_ready", "h_in_psum", "h_ready", "y_in_psum", "y_ready"))
        block = memory.enter_context(nc.Block())

        @block.sync
        def _(sp):
            for p in range(2):
                for s in (w1_loaded, w2_loaded, b2_loaded):
                    sp.sem_inc(s[p], 16)
                sp.sem_inc(x_loaded[p], 32)
            sp.dma_start(b1r[:], b1).then_inc(b1_loaded, 16)
            with sp.Fori(0, E // 2) as i:
                for p in range(2):
                    e = 2 * i + p
                    sp.wait_ge(xT_in_psum, after(e - 2))
                    sp.dma_start(xr[p][:, 0:whole, :],
                                 xe[at(e * C, whole * P), :].rearrange("(j q) d -> q j d", q=P)
                                 ).then_inc(x_loaded[p], 16)
                    sp.dma_start(xr[p][0:C - whole * P, whole, :], xe[at(e * C + whole * P, C - whole * P), :]
                                 ).then_inc(x_loaded[p], 16)
                    sp.wait_ge(h_in_psum, after(FK * (e - 1) - 1))
                    sp.dma_start(w1s[p][:], w1[at(e), :, :].rearrange("a (k q) f -> q (a k) f", q=P)
                                 ).then_inc(w1_loaded[p], 16)
                    sp.wait_ge(y_in_psum, after(NJ * (e - 1) - 1))
                    sp.dma_start(w2s[p][:], w2[at(e), :, :].rearrange("a (k q) d -> q (a k) d", q=P)
                                 ).then_inc(w2_loaded[p], 16)
                    sp.wait_ge(y_ready, after(NJ * (e - 1) - 1))
                    sp.dma_start(b2s[p][:], b2[at(e), :].rearrange("a d -> (a d)").partition_broadcast(P)
                                 ).then_inc(b2_loaded[p], 16)

        def pY_bank(j, p):
            return (NJ * p + j) % 2

        def transpose_queue(pe, e, i, p):
            pe.wait_ge(x_loaded[p], landed(i, 2))
            pe.wait_ge(xT_ready, after(e - 1))
            for j, (at_row, n) in enumerate(tiles):
                for k in range(DK):
                    last = nc.tensor.transpose(pX[:, k, at_row:at_row + n], xr[p][0:n, j, k * P:(k + 1) * P],
                                               ident[0:n, 0:n])
            last.then_inc(xT_in_psum, 1)

        @block.tensor
        def _(pe):
            for s in (xT_in_psum, h_in_psum, y_in_psum):
                pe.sem_inc(s, LEAD)
            pe.wait_ge(b1_loaded, 16)
            for f in range(FK):
                last = nc.tensor.transpose(pH[:, 0, f * E:(f + 1) * E], b1r[:, f * P:(f + 1) * P], ident[0:E, 0:E])
            last.then_inc(b1_in_psum, 1)
            transpose_queue(pe, 0, 0, 0)
            pe.wait_ge(b1_ready, 1)

            def expert(i, p, last_of_all=False):
                e = 2 * i + p
                pe.wait_ge(w1_loaded[p], landed(i))
                pe.wait_ge(xT_ready, after(e))
                for f in range(FK):
                    pe.wait_ge(h_ready, after(FK * e + f - NH))
                    for k in range(DK):
                        last = nc.tensor.matmul(pH[:, f % NH, 0:C], w1s[p][:, k, f * P:(f + 1) * P], xT[p][:, k, :],
                                                start=(k == 0), stop=(k == DK - 1))
                    last.then_inc(h_in_psum, 1)
                if not last_of_all:
                    transpose_queue(pe, e + 1, i + p, 1 - p)
                pe.wait_ge(w2_loaded[p], landed(i))
                pe.wait_ge(h_ready, after(FK * e + FK - 1))
                for j, (at_row, n) in enumerate(tiles):
                    pe.wait_ge(y_ready, after(NJ * e + j - 2))
                    bank = pY_bank(j, p)
                    for f in range(FK):
                        last = nc.tensor.matmul(pY[0:n, bank, 0:D], hT[p][:, f, at_row:at_row + n], w2s[p][:, f, :],
                                                start=(f == 0), stop=(f == FK - 1))
                    last.then_inc(y_in_psum, 1)

            with pe.Fori(0, E // 2 - 1) as i:
                for p in range(2):
                    expert(i, p)
            expert(E // 2 - 1, 0)
            expert(E // 2 - 1, 1, last_of_all=True)

        @block.scalar
        def _(act):
            act.sem_inc(xT_ready, LEAD)
            act.sem_inc(h_ready, LEAD)
            act.wait_ge(b1_in_psum, 1)
            nc.scalar.activation(b1T[:], pH[:, 0, 0:FK * E].rearrange("p (f e) -> p f e", e=E), ACT.Copy
                                 ).then_inc(b1_ready, 1)

            def copy_xT(e, p):
                act.wait_ge(xT_in_psum, after(e))
                act.wait_ge(h_in_psum, after(FK * (e - 1) - 1))
                nc.scalar.activation(xT[p][:], pX[:, :, 0:C], ACT.Copy).then_inc(xT_ready, 1)

            copy_xT(0, 0)
            act.wait_ge(b1_ready, 1)

            def expert(i, p, last_of_all=False):
                e = 2 * i + p
                act.wait_ge(y_in_psum, after(NJ * (e - 1) - 1))
                for f in range(FK):
                    act.wait_ge(h_in_psum, after(FK * e + f))
                    nc.scalar.activation(hT[p][:, f, :], pH[:, f % NH, 0:C], ACT.Gelu,
                                         bias=b1T[:, f, at(e)]).then_inc(h_ready, 1)
                if not last_of_all:
                    copy_xT(e + 1, 1 - p)

            with act.Fori(0, E // 2 - 1) as i:
                for p in range(2):
                    expert(i, p)
            expert(E // 2 - 1, 0)
            expert(E // 2 - 1, 1, last_of_all=True)

        @block.vector
        def _(dve):
            dve.sem_inc(y_ready, LEAD)

            def add_bias(i):
                for p in range(2):
                    e = 2 * i + p
                    dve.wait_ge(b2_loaded[p], landed(i))
                    if not (isinstance(i, int) and i == 0):
                        dve.wait_ge(stored[p], sw_landed(i - 1, 2))
                    for j, (_, n) in enumerate(tiles):
                        dve.wait_ge(y_in_psum, after(NJ * e + j))
                        nc.vector.tensor_tensor(yo[p][0:n, j, :], pY[0:n, pY_bank(j, p), 0:D], b2s[p][0:n, :],
                                                ALU.add).then_inc(y_ready, 1)

            turns(dve, E // 2, add_bias)

        @block.gpsimd
        def _(pool):
            with pool.Fori(0, E // 2) as i:
                for p in range(2):
                    e = 2 * i + p
                    pool.wait_ge(y_ready, after(NJ * e + NJ - 1))
                    pool.dma_start(ye[at(e * C, whole * P), :].rearrange("(j q) d -> q j d", q=P),
                                   yo[p][:, 0:whole, :]).then_inc(stored[p], 16)
                    pool.dma_start(ye[at(e * C + whole * P, C - whole * P), :],
                                   yo[p][0:C - whole * P, whole, :]).then_inc(stored[p], 16)
            for p in range(2):
                pool.wait_ge(stored[p], sw_landed(E // 2 - 1, 2))


def moe_combine(nc, tag, T, x_res, ye, gather_row, weight):
    NT = T // P
    with ExitStack() as memory:
        ph = Phase(nc, memory, tag)
        row = [ph.sb(f"row{p}", [P, 2], I32) for p in range(2)]
        got = [ph.sb(f"got{p}", [P, 2, D]) for p in range(2)]
        staged, gathered, added, turn = ph.sem("staged"), ph.pool_dma_sems("gathered"), ph.sem("added"), ph.sem("turn")
        block = memory.enter_context(nc.Block())

        @block.scalar
        def _(act):
            act.sem_inc(staged, LEAD)

            def stage(i):
                for p in range(2):
                    t = 2 * i + p
                    if not (isinstance(i, int) and i == 0):
                        act.wait_ge(gathered[p], sw_landed(i - 1, 2))
                    nc.scalar.activation(row[p][:], gather_row[:, at(t), :].rearrange("p a k -> p (a k)"), ACT.Copy
                                         ).then_inc(staged, 1)

            turns(act, NT // 2, stage)

        @block.gpsimd
        def _(pool):
            with pool.Fori(0, NT // 2) as i:
                for p in range(2):
                    t = 2 * i + p
                    pool.wait_ge(staged, after(t))
                    pool.wait_ge(added, after(2 * (t - 2) + 1))
                    pool.sem_inc(turn, 1)
                    for k in range(2):
                        pool.indirect_dma_start(
                            out=got[p][:, k, :], out_offset=None, in_=ye,
                            in_offset=bass.IndirectOffsetOnAxis(ap=row[p][:, k:k + 1], axis=0)
                        ).then_inc(gathered[p], 16)

        @block.vector
        def _(dve):
            dve.sem_inc(added, LEAD)
            with dve.Fori(0, NT // 2) as i:
                for p in range(2):
                    t = 2 * i + p
                    dve.wait_ge(gathered[p], sw_landed(i, 2))
                    for k in range(2):
                        if k:
                            dve.wait_ge(added, after(2 * t))
                        nc.vector.scalar_tensor_tensor(
                            out=x_res[:, at(t), :], in0=got[p][:, k:k + 1, :],
                            scalar=weight[:, at(t), k:k + 1].rearrange("p a k -> p (a k)"),
                            in1=x_res[:, at(t), :], op0=ALU.mult, op1=ALU.add).then_inc(added, 1)


def fold_butterflies(nc, tag, cst, w_exp, b_exp, up_w, up_b, down_w, w_con, b_con, down_b, folded):
    STAGES, PAIRS = up_w.shape[0], up_w.shape[1]
    HID = 2 * PAIRS
    HK = HID // P
    ident = cst["ident"]
    with ExitStack() as memory:
        ph = Phase(nc, memory, tag)
        up = ph.sb("up", [P, DK + 1, HID])
        down = ph.sb("down", [P, DK, HID])
        con = ph.sb("con", [P, HK, D])
        ub = ph.sb("ub", [1, HID])
        bc = [ph.sb(f"bc{k}", [P, D]) for k in range(2)]
        wu = [ph.sb(f"wu{p}", [P, 4 * PAIRS]) for p in range(2)]
        wd = [ph.sb(f"wd{p}", [P, 4 * PAIRS]) for p in range(2)]
        lo_u, hi_u = ph.sb("lo_u", [P, DK + 1, HID]), ph.sb("hi_u", [P, DK + 1, HID])
        lo_d, hi_d = ph.sb("lo_d", [P, DK, HID]), ph.sb("hi_d", [P, DK, HID])
        pD = ph.ps("pD", [P, DK, HID])
        pB = ph.ps("pB", [P, HK])
        loaded, up_loaded, down_loaded = ph.sem("loaded"), ph.sems("up_loaded"), ph.sems("down_loaded")
        up_step, down_step = ph.sem("up_step"), ph.sem("down_step")
        con_in_psum, con_ready, back_in_psum, folded_ready = (
            ph.sem(n) for n in ("con_in_psum", "con_ready", "back_in_psum", "folded_ready"))
        block = memory.enter_context(nc.Block())
        PER = 3

        @block.sync
        def _(sp):
            sp.dma_start(con[:], w_con.rearrange("(k p) d -> p k d", p=P)).then_inc(loaded, 16)
            sp.dma_start(up[:, 0:DK, :], w_exp.rearrange("(k p) h -> p k h", p=P)).then_inc(loaded, 16)
            sp.dma_start(up[:, DK, :], b_exp.partition_broadcast(P)).then_inc(loaded, 16)
            sp.dma_start(ub[:], up_b.rearrange("(a h) -> a h", a=1)).then_inc(loaded, 16)
            sp.dma_start(bc[0][:], b_con.partition_broadcast(P)).then_inc(loaded, 16)
            sp.dma_start(bc[1][:], down_b.partition_broadcast(P)).then_inc(loaded, 16)
            for s in range(STAGES):
                if s >= 2:
                    sp.wait_ge(up_step, PER * (s - 1))
                    sp.wait_ge(down_step, PER * (s - 1))
                sp.dma_start(wu[s % 2][:], up_w[s].rearrange("n i c -> (n i c)").partition_broadcast(P)
                             ).then_inc(up_loaded[s % 2], 16)
                sp.dma_start(wd[s % 2][:], down_w[STAGES - 1 - s].rearrange("n i c -> (n i c)").partition_broadcast(P)
                             ).then_inc(down_loaded[s % 2], 16)

        def stage(eng, y, w, lo, hi, s, rows, step, transposed, base):
            stride = 2 ** s
            order = "p (n j c i) -> p c n i j" if transposed else "p (n j i c) -> p c n i j"
            wv = w[:].rearrange(order, j=stride, i=2, c=2)
            for half, product in ((0, lo), (1, hi)):
                for r in range(rows):
                    mine = y[:, r, :].rearrange("p (n two j) -> p two n j", two=2, j=stride)[:, half]
                    ins = eng.tensor_tensor(product[:, r, :].rearrange("p (n i j) -> p n i j", i=2, j=stride),
                                            wv[:, half], spread(mine, 2, 2), ALU.mult)
                ins.then_inc(step, 1)
            eng.wait_ge(step, base + 2)
            eng.tensor_tensor(y[:, 0:rows, :], lo[:], hi[:], ALU.add).then_inc(step, 1)
            eng.wait_ge(step, base + 3)

        @block.vector
        def _(dve):
            dve.wait_ge(loaded, 16 * 6)
            for s in range(STAGES):
                dve.wait_ge(up_loaded[s % 2], 16 * (s // 2 + 1))
                stage(nc.vector, up, wu[s % 2], lo_u, hi_u, s, DK + 1, up_step, False, PER * s)
            nc.vector.tensor_tensor(bc[0][:], bc[0][:], bc[1][:], ALU.add).then_inc(up_step, 1)
            nc.vector.tensor_copy(folded["w_up"][:], up[:, 0:DK, :])
            dve.wait_ge(up_step, PER * STAGES + 1)
            nc.vector.tensor_scalar(folded["b_down"][:], bc[0][:], 0.5, None, ALU.mult)

        @block.gpsimd
        def _(pool):
            pool.wait_ge(con_ready, 1)
            for s in range(STAGES):
                pool.wait_ge(down_loaded[s % 2], 16 * (s // 2 + 1))
                stage(nc.gpsimd, down, wd[s % 2], lo_d, hi_d, STAGES - 1 - s, DK, down_step, True, PER * s)

        @block.tensor
        def _(pe):
            pe.wait_ge(loaded, 16 * 6)
            for k in range(HK):
                for m in range(DK):
                    last = nc.tensor.transpose(pD[:, m, k * P:(k + 1) * P], con[:, k, m * P:(m + 1) * P], ident[:])
            last.then_inc(con_in_psum, 1)
            pe.wait_ge(up_step, PER * STAGES)
            for k in range(HK):
                cols = slice(k * P, (k + 1) * P)
                nc.tensor.matmul(pB[:, k:k + 1], up[0:1, DK, cols], cst["ones"][0:1, 0:1], start=True, stop=False)
                last = nc.tensor.matmul(pB[:, k:k + 1], ub[0:1, cols], cst["ones"][0:1, 0:1], start=False, stop=True)
            last.then_inc(back_in_psum, 1)
            pe.wait_ge(down_step, PER * STAGES)
            pe.wait_ge(con_ready, 1)
            for k in range(HK):
                for m in range(DK):
                    last = nc.tensor.transpose(pD[:, :, :].rearrange("p m h -> p (m h)")[:, k * D + m * P:k * D + (m + 1) * P],
                                               down[:, m, k * P:(k + 1) * P], ident[:])
            last.then_inc(back_in_psum, 1)

        @block.scalar
        def _(act):
            act.wait_ge(con_in_psum, 1)
            nc.scalar.activation(down[:], pD[:], ACT.Copy).then_inc(con_ready, 1)
            act.wait_ge(back_in_psum, 1)
            nc.scalar.activation(folded["b_up"][:], pB[:], ACT.Copy)
            act.wait_ge(back_in_psum, 2)
            nc.scalar.activation(folded["w_down"][:].rearrange("p k d -> p (k d)"),
                                 pD[:].rearrange("p m h -> p (m h)"), ACT.Copy, scale=0.5).then_inc(folded_ready, 1)
            act.wait_ge(folded_ready, 1)


def butterfly_ffn(nc, tag, T, x_res, mean, rstd, cst, folded):
    NT, G = T // P, T // GW
    w_up, b_up, w_down, b_down = (folded[n] for n in ("w_up", "b_up", "w_down", "b_down"))
    HK = w_down.shape[1]
    ident = cst["ident"]
    NH = 4
    with ExitStack() as memory:
        ph = Phase(nc, memory, tag)
        xn = [ph.sb(f"xn{p}", [P, GT, D]) for p in range(2)]
        xnT = [ph.sb(f"xnT{p}", [P, DK, GW]) for p in range(2)]
        hT = [ph.sb(f"hT{p}", [P, HK, GW]) for p in range(2)]
        pX, pH, pY = ph.ps("pX", [P, DK, GW]), ph.ps("pH", [P, NH, GW]), ph.ps("pY", [P, 2, 512])
        xn_ready, xT_in_psum, xnT_ready, h_in_psum, h_ready, y_in_psum, y_added, biased = (
            ph.sem(n) for n in ("xn_ready", "xT_in_psum", "xnT_ready", "h_in_psum", "h_ready", "y_in_psum",
                                "y_added", "biased"))
        block = memory.enter_context(nc.Block())

        @block.vector
        def _(dve):
            dve.sem_inc(xn_ready, LEAD)
            dve.sem_inc(y_added, LEAD)
            dve.sem_inc(biased, LEAD)

            def normalise(g, p):
                dve.wait_ge(xT_in_psum, after(g - 2))
                for j in range(GT):
                    t = GT * g + j
                    nc.vector.tensor_scalar(xn[p][:, j:j + 1, :], x_res[:, at(t), :], mean[:, at(t)],
                                            rstd[:, at(t)], ALU.subtract, ALU.mult).then_inc(xn_ready, 1)

            def group(i, p, last_of_all=False):
                g = 2 * i + p
                if not last_of_all:
                    normalise(g + 1, 1 - p)
                for j in range(GT):
                    t = GT * g + j
                    dve.wait_ge(y_in_psum, after(t))
                    nc.vector.tensor_tensor(x_res[:, at(t), :], x_res[:, at(t), :], pY[:, j % 2:j % 2 + 1, 0:D],
                                            ALU.add).then_inc(y_added, 1)
                    dve.wait_ge(y_added, after(t))
                    nc.vector.tensor_tensor(x_res[:, at(t), :], x_res[:, at(t), :], spread(b_down[:], 1, 1),
                                            ALU.add).then_inc(biased, 1)

            normalise(0, 0)
            with dve.Fori(0, G // 2 - 1) as i:
                for p in range(2):
                    group(i, p)
            group(G // 2 - 1, 0)
            group(G // 2 - 1, 1, last_of_all=True)

        def transpose_group(pe, g, p):
            pe.wait_ge(xn_ready, after(GT * g + GT - 1))
            pe.wait_ge(xnT_ready, after(g - 1))
            for j in range(GT):
                for k in range(DK):
                    last = nc.tensor.transpose(pX[:, k, j * P:(j + 1) * P], xn[p][:, j, k * P:(k + 1) * P], ident[:])
            last.then_inc(xT_in_psum, 1)

        @block.tensor
        def _(pe):
            for s in (xT_in_psum, h_in_psum, y_in_psum):
                pe.sem_inc(s, LEAD)
            transpose_group(pe, 0, 0)

            def group(i, p, last_of_all=False):
                g = 2 * i + p
                pe.wait_ge(xnT_ready, after(g))
                for f in range(HK):
                    pe.wait_ge(h_ready, after(HK * g + f - NH))
                    for k in range(DK):
                        last = nc.tensor.matmul(pH[:, f % NH, :], w_up[:, k, f * P:(f + 1) * P], xnT[p][:, k, :],
                                                start=(k == 0), stop=(k == DK - 1))
                    last.then_inc(h_in_psum, 1)
                if not last_of_all:
                    transpose_group(pe, g + 1, 1 - p)
                pe.wait_ge(h_ready, after(HK * g + HK - 1))
                for j in range(GT):
                    pe.wait_ge(y_added, after(GT * g + j - 2))
                    for f in range(HK):
                        last = nc.tensor.matmul(pY[:, j % 2, 0:D], hT[p][:, f, j * P:(j + 1) * P], w_down[:, f, :],
                                                start=(f == 0), stop=(f == HK - 1))
                    last.then_inc(y_in_psum, 1)

            with pe.Fori(0, G // 2 - 1) as i:
                for p in range(2):
                    group(i, p)
            group(G // 2 - 1, 0)
            group(G // 2 - 1, 1, last_of_all=True)

        @block.scalar
        def _(act):
            act.sem_inc(xnT_ready, LEAD)
            act.sem_inc(h_ready, LEAD)

            def copy_xnT(g, p):
                act.wait_ge(xT_in_psum, after(g))
                act.wait_ge(h_in_psum, after(HK * (g - 1) - 1))
                nc.scalar.activation(xnT[p][:], pX[:], ACT.Copy).then_inc(xnT_ready, 1)

            def group(i, p, last_of_all=False):
                g = 2 * i + p
                act.wait_ge(y_in_psum, after(GT * (g - 1) - 1))
                for f in range(HK):
                    act.wait_ge(h_in_psum, after(HK * g + f))
                    nc.scalar.activation(hT[p][:, f, :], pH[:, f % NH, :], ACT.Gelu,
                                         bias=b_up[:, f:f + 1]).then_inc(h_ready, 1)
                if not last_of_all:
                    copy_xnT(g + 1, 1 - p)

            copy_xnT(0, 0)
            with act.Fori(0, G // 2 - 1) as i:
                for p in range(2):
                    group(i, p)
            group(G // 2 - 1, 0)
            group(G // 2 - 1, 1, last_of_all=True)


def linear_attention(nc, tag, T, H, BD, x_res, mean, rstd, cst, qkv_w, qkv_b, out_w, out_b):
    G = T // GW
    HT = P // BD
    VW = BD + 1
    EPS = 1e-6
    ident = cst["ident"]
    NM = 2 * DK
    with ExitStack() as memory:
        ph = Phase(nc, memory, tag)
        wqkv, wout = ph.sb("wqkv", [P, DK, 3 * D]), ph.sb("wout", [P, DK, D])
        b_rows, b_cols, b_cols1 = ph.sb("b_rows", [NM, P]), ph.sb("b_cols", [P, NM]), ph.sb("b_cols1", [P, NM])
        b_value, b_out = ph.sb("b_value", [P, D]), ph.sb("b_out", [P, D])
        xn = [ph.sb(f"xn{p}", [P, GT, D]) for p in range(2)]
        xnT = [ph.sb(f"xnT{p}", [P, DK, GW]) for p in range(2)]
        low = [ph.sb(f"low{m}", [P, GW]) for m in range(2)]
        qk = [ph.sb(f"qk{p}", [P, NM, GW]) for p in range(2)]
        q_of = [ph.sb(f"q_of{p}", [P, DK, 2, GW]) for p in range(2)]
        v1 = [ph.sb(f"v1{p}", [P, H, VW]) for p in range(2)]
        kt = [ph.sb(f"kt{p}", [P, D]) for p in range(2)]
        scores = [ph.sb(f"scores{p}", [P, H, P]) for p in range(2)]
        state, added = ph.sb("state", [P, DK, HT * VW]), ph.sb("added", [P, DK, HT * VW])
        denom = ph.sb("denom", [P, H])
        o = ph.sb("o", [P, H, BD])
        oT = ph.sb("oT", [P, DK, P])
        y = ph.sb("y", [P, D])

        pF = ph.ps("pF", [P, 2, GW])
        pS = ph.ps("pS", [P, 2, GW])
        pV, pC, pU, pO = (ph.ps(n, [P, 512]) for n in ("pV", "pC", "pU", "pO"))

        w_loaded, b_in_psum, bias_ready, setup = (ph.sem(n) for n in ("w_loaded", "b_in_psum", "bias_ready", "setup"))
        xn_ready, xT_in_psum, xnT_ready = (ph.sem(n) for n in ("xn_ready", "xT_in_psum", "xnT_ready"))
        f_in_psum, low_ready, exp_ready, f_ready, q_split = (
            ph.sem(n) for n in ("f_in_psum", "low_ready", "exp_ready", "f_ready", "q_split"))
        vk_in_psum, vk_ready, s_in_psum, s_ready, c_in_psum, u_in_psum = (
            ph.sem(n) for n in ("vk_in_psum", "vk_ready", "s_in_psum", "s_ready", "c_in_psum", "u_in_psum"))
        state_step, denom_step, o_step, oT_in_psum, oT_ready, y_in_psum, y_read, y_added = (
            ph.sem(n) for n in ("state_step", "denom_step", "o_step", "oT_in_psum", "oT_ready", "y_in_psum", "y_read", "y_added"))
        block = memory.enter_context(nc.Block())

        @block.sync
        def _(sp):
            sp.dma_start(wqkv[:], qkv_w.rearrange("(k p) n -> p k n", p=P)).then_inc(w_loaded, 16)
            sp.dma_start(wout[:], out_w.rearrange("(k p) n -> p k n", p=P)).then_inc(w_loaded, 16)
            sp.dma_start(b_rows[:], qkv_b[0:2 * D].rearrange("(m p) -> m p", p=P)).then_inc(w_loaded, 16)
            sp.dma_start(b_value[:], qkv_b[2 * D:3 * D].partition_broadcast(P)).then_inc(w_loaded, 16)
            sp.dma_start(b_out[:], out_b.partition_broadcast(P)).then_inc(w_loaded, 16)

        @block.tensor
        def _(pe):
            for s in (xT_in_psum, f_in_psum, vk_in_psum, s_in_psum, c_in_psum, u_in_psum, oT_in_psum, y_in_psum):
                pe.sem_inc(s, LEAD)
            pe.wait_ge(w_loaded, 16 * 5)
            nc.tensor.transpose(pV[:, 0:NM], b_rows[:], ident[0:NM, 0:NM]).then_inc(b_in_psum, 1)
            pe.wait_ge(bias_ready, 2)
            with pe.Fori(0, G // 2) as i:
                for p in range(2):
                    g = 2 * i + p
                    pe.wait_ge(xn_ready, after(GT * g + GT - 1))
                    pe.wait_ge(f_ready, after(NM * g - 1))
                    for k in range(DK):
                        for j in range(GT):
                            last = nc.tensor.transpose(pF[:, k, j * P:(j + 1) * P], xn[p][:, j, k * P:(k + 1) * P],
                                                       ident[:])
                    last.then_inc(xT_in_psum, 1)
                    pe.wait_ge(xnT_ready, after(g))
                    for m in range(NM):
                        pe.wait_ge(f_ready, after(NM * g + m - 2))
                        for k in range(DK):
                            last = nc.tensor.matmul(pF[:, m % 2, :], wqkv[:, k, m * P:(m + 1) * P], xnT[p][:, k, :],
                                                    start=(k == 0), stop=(k == DK - 1))
                        last.then_inc(f_in_psum, 1)
                    pe.wait_ge(q_split, after(2 * DK * g + 2 * DK - 1))
                    pe.wait_ge(f_ready, after(NM * g + NM - 1))

                    def output(c, j):
                        pe.wait_ge(o_step, after(c))
                        pe.wait_ge(y_read, after(c - 1))
                        for k in range(DK):
                            last = nc.tensor.transpose(pO[:, k * P:(k + 1) * P],
                                                       o[:].rearrange("p h e -> p (h e)")[:, k * P:(k + 1) * P], ident[:])
                        last.then_inc(oT_in_psum, 1)
                        pe.wait_ge(oT_ready, after(c))
                        for k in range(DK):
                            last = nc.tensor.matmul(pO[:, D:2 * D], oT[:, k, :], wout[:, k, :],
                                                    start=(k == 0), stop=(k == DK - 1))
                        last.then_inc(y_in_psum, 1)

                    for j in range(GT):
                        c = GT * g + j
                        b = j % 2
                        chunk = slice(j * P, (j + 1) * P)
                        pe.wait_ge(vk_ready, after(2 * c - 1))
                        for k in range(DK):
                            nc.tensor.matmul(pV[:, 0:D], xnT[p][:, k, chunk], wqkv[:, k, 2 * D:3 * D],
                                             start=(k == 0), stop=(k == DK - 1))
                        for k in range(DK):
                            last = nc.tensor.transpose(pV[:, D + k * P:D + (k + 1) * P], qk[p][:, DK + k, chunk], ident[:])
                        last.then_inc(vk_in_psum, 1)
                        for s in range(H // 4):
                            pe.wait_ge(s_ready, after(H // 4 * c + s - 2))
                            rows = slice(2 * BD * s, 2 * BD * (s + 1))
                            for k in range(DK):
                                last = nc.tensor.matmul(pS[:, s % 2, k * 2 * P:(k + 1) * 2 * P],
                                                        qk[p][rows, DK + k, chunk], q_of[p][rows, k, :, chunk],
                                                        start=True, stop=True)
                            last.then_inc(s_in_psum, 1)
                        if j:
                            output(c - 1, j - 1)
                        pe.wait_ge(state_step, after(2 * c - 1))
                        pe.wait_ge(o_step, after(c - 1))
                        pe.wait_ge(s_ready, after(H // 4 * c + H // 4 - 1))
                        pe.wait_ge(vk_ready, after(2 * c + 1))
                        for k in range(DK):
                            width = HT * VW
                            for h in range(k * HT, (k + 1) * HT):
                                cols = slice(h * VW, (h + 1) * VW)
                                if h == k * HT:
                                    nc.tensor.matmul(pC[:, k * width:(k + 1) * width], qk[p][:, k, chunk],
                                                     state[:, k, :], start=True, stop=False)
                                last = nc.tensor.matmul(pC[:, cols], scores[b][:, h, :], v1[b][:, h, :],
                                                        start=False, stop=(h == (k + 1) * HT - 1))
                        last.then_inc(c_in_psum, 1)
                        pe.wait_ge(state_step, after(2 * c - 2))
                        for k in range(DK):
                            last = nc.tensor.matmul(pU[:, k * HT * VW:(k + 1) * HT * VW], kt[b][:, k * P:(k + 1) * P],
                                                    v1[b][:, k * HT:(k + 1) * HT, :].rearrange("p h e -> p (h e)"),
                                                    start=True, stop=True)
                        last.then_inc(u_in_psum, 1)
                    output(GT * g + GT - 1, GT - 1)

        @block.scalar
        def _(act):
            for s in (xnT_ready, exp_ready, oT_ready):
                act.sem_inc(s, LEAD)
            act.wait_ge(b_in_psum, 1)
            nc.scalar.activation(b_cols[:], pV[:, 0:NM], ACT.Copy).then_inc(bias_ready, 1)
            with act.Fori(0, G // 2) as i:
                for p in range(2):
                    g = 2 * i + p
                    act.wait_ge(xT_in_psum, after(g))
                    act.wait_ge(vk_in_psum, after(GT * (g - 1) - 1))
                    nc.scalar.activation(xnT[p][:], pF[:], ACT.Copy).then_inc(xnT_ready, 1)
                    for m in range(NM):
                        act.wait_ge(low_ready, after(NM * g + m))
                        nc.scalar.activation(low[m % 2][:], low[m % 2][:], ACT.Exp).then_inc(exp_ready, 1)
                    for j in range(GT):
                        c = GT * g + j
                        act.wait_ge(oT_in_psum, after(c))
                        nc.scalar.activation(oT[:], pO[:, 0:D].rearrange("p (k t) -> p k t", k=DK), ACT.Copy
                                             ).then_inc(oT_ready, 1)

        @block.gpsimd
        def _(pool):
            pool.sem_inc(y_added, LEAD)
            with pool.Fori(0, G // 2) as i:
                for p in range(2):
                    for j in range(GT):
                        c = GT * (2 * i + p) + j
                        pool.wait_ge(y_read, after(c))
                        nc.gpsimd.tensor_tensor(x_res[:, at(c), :], x_res[:, at(c), :], spread(y[:], 1, 1), ALU.add
                                                ).then_inc(y_added, 1)

        @block.vector
        def _(dve):
            for s in (xn_ready, low_ready, f_ready, q_split, vk_ready, s_ready, state_step, denom_step, o_step, y_read):
                dve.sem_inc(s, LEAD)
            for b in range(2):
                nc.vector.memset(v1[b][:, :, BD:VW], 1.0).then_inc(setup, 1)
            nc.vector.memset(state[:], 0.0).then_inc(setup, 1)
            dve.wait_ge(bias_ready, 1)
            nc.vector.tensor_scalar(b_cols1[:], b_cols[:], 1.0, None, ALU.add).then_inc(bias_ready, 1)
            dve.wait_ge(bias_ready, 2)
            dve.wait_ge(setup, 3)
            dve.wait_ge(w_loaded, 16 * 5)

            def take_output(dve, c):
                dve.wait_ge(y_in_psum, after(c))
                dve.wait_ge(y_added, after(c - 1))
                nc.vector.tensor_tensor(y[:], pO[:, D:2 * D], b_out[:], ALU.add).then_inc(y_read, 1)

            with dve.Fori(0, G // 2) as i:
                for p in range(2):
                    g = 2 * i + p
                    dve.wait_ge(xT_in_psum, after(g - 2))
                    for j in range(GT):
                        t = GT * g + j
                        nc.vector.tensor_scalar(xn[p][:, j:j + 1, :], x_res[:, at(t), :], mean[:, at(t)],
                                                rstd[:, at(t)], ALU.subtract, ALU.mult).then_inc(xn_ready, 1)
                    dve.wait_ge(c_in_psum, after(GT * (g - 1) - 1))
                    for m in range(NM):
                        dve.wait_ge(f_in_psum, after(NM * g + m))
                        dve.wait_ge(f_ready, after(NM * g + m - 2))
                        nc.vector.tensor_scalar(low[m % 2][:], pF[:, m % 2, :], b_cols[:, m:m + 1], 0.0,
                                                ALU.add, ALU.min).then_inc(low_ready, 1)
                        dve.wait_ge(exp_ready, after(NM * g + m))
                        nc.vector.scalar_tensor_tensor(out=qk[p][:, m, :], in0=pF[:, m % 2, :],
                                                       scalar=b_cols1[:, m:m + 1], in1=low[m % 2][:],
                                                       op0=ALU.add, op1=ALU.max).then_inc(f_ready, 1)
                    dve.wait_ge(f_ready, after(NM * g + DK - 1))
                    for k in range(DK):
                        for odd in range(2):
                            nc.vector.tensor_scalar(q_of[p][:, k, odd, :], qk[p][:, k, :], cst["parity"][:, odd:odd + 1],
                                                    None, ALU.mult).then_inc(q_split, 1)
                    for j in range(GT):
                        c = GT * g + j
                        b = j % 2
                        dve.wait_ge(vk_in_psum, after(c))
                        dve.wait_ge(u_in_psum, after(c - 2))
                        nc.vector.tensor_tensor(v1[b][:, :, 0:BD], pV[:, 0:D].rearrange("p (h e) -> p h e", e=BD),
                                                b_value[:].rearrange("p (h e) -> p h e", e=BD), ALU.add
                                                ).then_inc(vk_ready, 1)
                        nc.vector.tensor_copy(kt[b][:], pV[:, D:2 * D]).then_inc(vk_ready, 1)
                        for s in range(H // 4):
                            dve.wait_ge(s_in_psum, after(H // 4 * c + s))
                            if s == 0:
                                dve.wait_ge(c_in_psum, after(c - 2))
                            nc.vector.tensor_tensor(
                                scores[b][:].rearrange("p (k h) t -> p k h t", k=DK)[:, :, 2 * s:2 * s + 2, :],
                                pS[:, s % 2, :].rearrange("p (k h t) -> p k h t", k=DK, t=P),
                                spread(spread(cst["causal"][:], 1, 2), 1, DK), ALU.mult).then_inc(s_ready, 1)
                        dve.wait_ge(c_in_psum, after(c))
                        dve.wait_ge(oT_in_psum, after(c - 1))
                        ctxv = pC[:, 0:H * VW].rearrange("p (h e) -> p h e", e=VW)
                        nc.vector.tensor_scalar(denom[:], ctxv[:, :, BD], EPS, None, ALU.add).then_inc(denom_step, 1)
                        dve.wait_ge(denom_step, after(2 * c))
                        nc.vector.reciprocal(denom[:], denom[:]).then_inc(denom_step, 1)
                        dve.wait_ge(denom_step, after(2 * c + 1))
                        nc.vector.tensor_tensor(o[:], ctxv[:, :, 0:BD], spread(denom[:], 2, BD), ALU.mult
                                                ).then_inc(o_step, 1)
                        dve.wait_ge(u_in_psum, after(c))
                        nc.vector.tensor_tensor(added[:].rearrange("p k (h e) -> p k h e", e=VW),
                                                pU[:, 0:H * VW].rearrange("p (k h e) -> p k h e", k=DK, e=VW),
                                                spread(cst["head_block"][:], 1, DK), ALU.mult).then_inc(state_step, 1)
                        dve.wait_ge(state_step, after(2 * c))
                        nc.vector.tensor_tensor(state[:], state[:], added[:], ALU.add).then_inc(state_step, 1)
                        if j:
                            take_output(dve, c - 1)
                    take_output(dve, GT * g + GT - 1)


def window_weights(nc, ph, tag, H, BD, cst, a):
    W = a["L1_attn_rel_pos_emb"].shape[0]
    FT = 2 * BD
    HG = P // FT
    NG = H // HG
    HT = P // BD
    res = {"features": ph.sb("features", [P, DK, H * FT]), "offset": ph.sb("offset", [P, W]),
           "reduce": ph.sb("reduce", [P, HG, 2, HG, HG]), "value": ph.sb("value", [P, DK, D]),
           "proj": ph.sb("proj", [P, NG, D]), "half_damage_b": ph.sb("half_damage_b", [P, 1])}
    with ExitStack() as memory:
        t = Phase(nc, memory, tag)
        disp, val_rows = t.sb("disp", [P, DK, D]), t.sb("val_rows", [P, DK, D])
        proj_rows = t.sb("proj_rows", [P, DK, H, FT])
        strain = t.sb("strain", [P, HT, FT])
        place_w, place = t.sb("place_w", [BD, HG, 2, BD]), t.sb("place", [BD, W])
        fused_b, last_w = t.sb("fused_b", [P, 1]), t.sb("last_w", [P, 1])
        reduced = t.sb("reduced", [P, 2, HG])
        pW = t.ps("pW", [P, DK, 512])
        pR = t.ps("pR", [P, 2, 512])
        pP = t.ps("pP", [P, 2, 512])
        pO = t.ps("pO", [P, 512])
        cleared, loaded, made, in_psum = t.sem("cleared"), t.sem("loaded"), t.sem("made"), t.sem("in_psum")
        block = memory.enter_context(nc.Block())

        @block.sync
        def _(sp):
            sp.dma_start(disp[:], a["L1_attn_W_disp"].rearrange("(k p) d -> p k d", p=P)).then_inc(loaded, 16)
            sp.dma_start(val_rows[:], a["L1_attn_W_val"].rearrange("(k p) d -> p k d", p=P)).then_inc(loaded, 16)
            sp.dma_start(res["half_damage_b"][:], a["L1_attn_damage_out_b"].partition_broadcast(P)).then_inc(loaded, 16)
            sp.dma_start(place[:], a["L1_attn_rel_pos_emb"].rearrange("w b -> b w"),
                             allow_slow_non_contiguous=True).then_inc(loaded, 16)
            for h in range(HG):
                sp.dma_start(fused_b[h * FT:(h + 1) * FT, :], a["L1_attn_strain_fused_b"].rearrange("(f a) -> f a", a=1),
                             allow_slow_non_contiguous=True).then_inc(loaded, 16)
                for half, name in ((0, "L1_attn_bond_out_w"), (1, "L1_attn_damage_out_w")):
                    rows = slice(h * FT + half * BD, h * FT + (half + 1) * BD)
                    sp.dma_start(last_w[rows, :], a[name].rearrange("a b -> b a"),
                             allow_slow_non_contiguous=True).then_inc(loaded, 16)
            sp.wait_ge(cleared, 3)
            for h in range(HT):
                sp.dma_start(strain[h * BD:(h + 1) * BD, h, :], a["L1_attn_strain_fused_w"].rearrange("f b -> b f"),
                             allow_slow_non_contiguous=True).then_inc(loaded, 16)
            for h in range(HG):
                sp.dma_start(place_w[:, h, 0, :], a["L1_attn_pos_proj_w"].rearrange("f b -> b f"),
                             allow_slow_non_contiguous=True).then_inc(loaded, 16)
            for k in range(DK):
                sp.dma_start(proj_rows[:, k, :, 0:BD], a["L1_attn_c_proj_w"][k * P:(k + 1) * P, :].rearrange(
                    "p (h e) -> p h e", e=BD)).then_inc(loaded, 16)

        n_loads = 4 + 3 * HG + HT + HG + DK

        @block.vector
        def _(dve):
            nc.vector.memset(strain[:], 0.0).then_inc(cleared, 1)
            nc.vector.memset(place_w[:], 0.0).then_inc(cleared, 1)
            nc.vector.memset(proj_rows[:], 0.0).then_inc(cleared, 1)
            nc.vector.memset(res["reduce"][:], 0.0).then_inc(made, 1)
            dve.wait_ge(loaded, 16 * n_loads)
            own = cst["head_block"][:, :, 0].rearrange("p (h two) -> p two h", two=2)
            nc.vector.tensor_scalar(reduced[:], own, last_w[:], None, ALU.mult).then_inc(made, 1)
            nc.vector.tensor_scalar(res["half_damage_b"][:], res["half_damage_b"][:], 0.5, None, ALU.mult)
            dve.wait_ge(made, 2)
            for k in range(HG):
                nc.vector.tensor_copy(res["reduce"][:, k, :, :, k], reduced[:])
            dve.wait_ge(in_psum, 1)
            nc.vector.tensor_scalar(res["offset"][:], pO[:, 0:W], fused_b[:], None, ALU.add)

        @block.tensor
        def _(pe):
            pe.wait_ge(loaded, 16 * n_loads)
            nc.tensor.matmul(pO[:, 0:W], place_w[:].rearrange("b h two f -> b (h two f)"), place[:],
                             start=True, stop=True).then_inc(in_psum, 1)
            for k in range(DK):
                for m in range(DK):
                    nc.tensor.matmul(pW[:, m, k * HT * FT:(k + 1) * HT * FT], disp[:, k, m * P:(m + 1) * P],
                                     strain[:].rearrange("p h f -> p (h f)"), start=True, stop=True)
                    nc.tensor.transpose(pR[:, 0, m * D + k * P:m * D + (k + 1) * P], val_rows[:, k, m * P:(m + 1) * P],
                                        cst["ident"][:])
                for q in range(NG):
                    last = nc.tensor.transpose(
                        pP[:, q // 2, (q % 2) * D + k * P:(q % 2) * D + (k + 1) * P],
                        proj_rows[:, k, q * HG:(q + 1) * HG, :].rearrange("p h f -> p (h f)"), cst["ident"][:])
            last.then_inc(in_psum, 1)

        @block.scalar
        def _(act):
            act.wait_ge(in_psum, 2)
            nc.scalar.activation(res["features"][:], pW[:], ACT.Copy)
            nc.scalar.activation(res["value"][:].rearrange("p k d -> p (k d)"), pR[:, 0, :], ACT.Copy)
            nc.scalar.activation(res["proj"][:].rearrange("p q d -> p (q d)"),
                                 pP[:].rearrange("p a b -> p (a b)"), ACT.Copy)
    return res


def window_attention(nc, tag, T, H, BD, x_res, mean, rstd, cst, a):
    G = T // GW
    W = a["L1_attn_rel_pos_emb"].shape[0]
    FT = 2 * BD
    HG = P // FT
    NG = H // HG
    KW = HG
    NW = W // KW
    RING = 4
    BAND = 2 * P
    PITCH = 3 * P
    LEFT = PITCH // 2
    ident = cst["ident"]
    band_dram = nc.dram_tensor(f"{tag}_band", [2, P, H, PITCH], F32)
    band = band_dram.ap()
    with ExitStack() as memory:
        ph = Phase(nc, memory, tag)
        wt = window_weights(nc, ph, tag + "_w", H, BD, cst, a)
        xn = ph.sb("xn", [P, GT, D])
        xnT = ph.sb("xnT", [P, DK, GW])
        feat = [ph.sb(f"feat{p}", [P, NG, W + GW]) for p in range(2)]
        val = [ph.sb(f"val{p}", [P, GT, H, FT]) for p in range(2)]
        pair = [ph.sb(f"pair{r}", [P, NG, GW]) for r in range(RING)]
        flat = [ph.sb(f"flat{b}", [P, GW]) for b in range(2)]
        logit = ph.sb("logit", [P, GT, 2, NW, H, KW])
        top, total = ph.sb("top", [P, H]), ph.sb("total", [P, H])
        prob = ph.sb("prob", [P, H, W])
        wide = ph.sb("wide", [P, H, BAND])
        wideT = [ph.sb(f"wideT{b}", [P, 2, 2, P]) for b in range(2)]
        oT = ph.sb("oT", [P, NG, P])
        pF, pW, pA = (ph.ps(n, [P, 2, 512]) for n in ("pF", "pW", "pA"))
        pL, pO = ph.ps("pL", [P, GT, P]), ph.ps("pO", [P, NG, P])

        names = ("zeros_ready", "band_zeroed", "setup", "xn_ready", "xT_in_psum", "xnT_ready", "f_in_psum", "f_ready",
                 "halo_ready", "v_in_psum", "v_ready", "diff_dve", "diff_pool", "gelu_ready", "reduced",
                 "flat_ready", "l_in_psum", "l_ready", "tanh_ready", "damage_ready", "soft_step", "exp_ready",
                 "masked", "prob_ready", "prob_stored", "wide_loaded", "a_in_psum", "a_ready", "o_in_psum",
                 "oT_ready", "y_in_psum", "y_added", "pool_turn", "dve_turn")
        s = {n: ph.sem(n) for n in names}
        block = memory.enter_context(nc.Block())

        @block.sync
        def _(sp):
            sp.wait_ge(s["zeros_ready"], 1)
            for b in range(2):
                sp.dma_start(band[b].rearrange("p h w -> p (h w)").rearrange("p (c f) -> p c f", f=H * PITCH // 3),
                             pair[0][:].rearrange("p g t -> p (g t)")[:, 0:H * PITCH // 3].unsqueeze(1).broadcast_to(
                                 [P, 3, H * PITCH // 3])).then_inc(s["band_zeroed"], 16)
            sp.wait_ge(s["band_zeroed"], 32)
            sp.sem_inc(s["prob_stored"], 16)
            sp.sem_inc(s["wide_loaded"], 16)
            with sp.Fori(0, G // 2) as i:
                for p in range(2):
                    for j in range(GT):
                        t = GT * (2 * i + p) + j
                        b = j % 2
                        sp.wait_ge(s["prob_ready"], after(3 * t + 2))
                        sp.dma_start(band[b, :, :, LEFT:LEFT + W], prob[:]).then_inc(s["prob_stored"], 16)
                        sp.wait_ge(s["prob_stored"], landed(t))
                        sp.wait_ge(s["a_in_psum"], after(H // 2 * t - 1))
                        skewed = bass.AP(tensor=band_dram, offset=b * P * H * PITCH + LEFT - (P - W + 1) + (P - W),
                                         ap=[[H * PITCH - 1, P], [PITCH, H], [1, BAND - (P - W)]])
                        sp.dma_start(wide[:, :, P - W:BAND], skewed).then_inc(s["wide_loaded"], 16)

        @block.tensor
        def _(pe):
            for n in ("xT_in_psum", "f_in_psum", "v_in_psum", "reduced", "l_in_psum", "a_in_psum", "o_in_psum",
                      "y_in_psum"):
                pe.sem_inc(s[n], LEAD)
            with pe.Fori(0, G // 2) as i:
                for p in range(2):
                    g = 2 * i + p
                    pe.wait_ge(s["xn_ready"], after(GT * g + GT - 1))
                    pe.wait_ge(s["v_ready"], after(GT * g - 1))
                    pe.wait_ge(s["y_added"], after(GT * g - 1))
                    for k in range(DK):
                        for j in range(GT):
                            last = nc.tensor.transpose(pF[:, k, j * P:(j + 1) * P], xn[:, j, k * P:(k + 1) * P], ident[:])
                    last.then_inc(s["xT_in_psum"], 1)
                    pe.wait_ge(s["xnT_ready"], after(g))
                    for m in range(NG):
                        pe.wait_ge(s["f_ready"], after(NG * g + m - 2))
                        for k in range(DK):
                            last = nc.tensor.matmul(pF[:, m % 2, :], wt["features"][:, k, m * P:(m + 1) * P],
                                                    xnT[:, k, :], start=(k == 0), stop=(k == DK - 1))
                        last.then_inc(s["f_in_psum"], 1)
                    for j in range(GT):
                        pe.wait_ge(s["v_ready"], after(GT * g + j - 2))
                        for k in range(DK):
                            last = nc.tensor.matmul(pA[:, j % 2, 0:D], xnT[:, k, j * P:(j + 1) * P],
                                                    wt["value"][:, k, :], start=(k == 0), stop=(k == DK - 1))
                        last.then_inc(s["v_in_psum"], 1)

                    with pe.Fori(0, NW // 2) as iw:
                        for b in range(2):
                            wg = 2 * iw + b
                            pe.wait_ge(s["flat_ready"], after(NW * g + wg - 2))
                            for k in range(KW):
                                n = W * g + KW * wg + k
                                pe.wait_ge(s["gelu_ready"], after(n))
                                for q in range(NG):
                                    last = nc.tensor.matmul(
                                        pW[q * FT:(q + 1) * FT, b, :],
                                        wt["reduce"][:, k].rearrange("p two h k -> p (two h k)"), pair[k][:, q, :],
                                        start=(k == 0), stop=(k == KW - 1))
                                last.then_inc(s["reduced"], 1)
                            pe.wait_ge(s["flat_ready"], after(NW * g + wg))
                            pe.wait_ge(s["l_ready"], after(2 * (NW * g + wg) - 1))
                            for j in range(GT):
                                last = nc.tensor.transpose(pL[:, j, :], flat[b][:, j * P:(j + 1) * P], ident[:])
                            last.then_inc(s["l_in_psum"], 1)

                    for j in range(GT):
                        t = GT * g + j
                        pe.wait_ge(s["wide_loaded"], landed(t))
                        before = val[p][:, j - 1] if j else val[1 - p][:, GT - 1]
                        for hp in range(H // 2):
                            n = H // 2 * t + hp
                            pe.wait_ge(s["a_ready"], after(n - 2))
                            for hh in range(2):
                                for blk in range(2):
                                    last = nc.tensor.transpose(
                                        pA[:, hp % 2, (2 * hh + blk) * P:(2 * hh + blk + 1) * P],
                                        wide[:, 2 * hp + hh, blk * P:(blk + 1) * P], ident[:])
                            last.then_inc(s["a_in_psum"], 1)
                            pe.wait_ge(s["a_ready"], after(n))
                            if hp == 0:
                                pe.wait_ge(s["oT_ready"], after(t - 1))
                            for blk, v in ((0, before), (1, val[p][:, j])):
                                for hh in range(2):
                                    h = 2 * hp + hh
                                    rows = slice((h % HG) * FT, (h % HG + 1) * FT)
                                    last = nc.tensor.matmul(pO[rows, h // HG, :], v[:, h, :],
                                                            wideT[hp % 2][:, hh, blk, :],
                                                            start=(blk == 0), stop=(blk == 1))
                        last.then_inc(s["o_in_psum"], 1)
                        pe.wait_ge(s["oT_ready"], after(t))
                        pe.wait_ge(s["y_added"], after(t - 2))
                        for q in range(NG):
                            last = nc.tensor.matmul(pF[:, j % 2, 0:D], oT[:, q, :], wt["proj"][:, q, :],
                                                    start=(q == 0), stop=(q == NG - 1))
                        last.then_inc(s["y_in_psum"], 1)

        @block.scalar
        def _(act):
            for n in ("xnT_ready", "f_ready", "gelu_ready", "tanh_ready", "exp_ready", "a_ready", "oT_ready"):
                act.sem_inc(s[n], LEAD)
            with act.Fori(0, G // 2) as i:
                for p in range(2):
                    g = 2 * i + p
                    act.wait_ge(s["xT_in_psum"], after(g))
                    nc.scalar.activation(xnT[:], pF[:], ACT.Copy).then_inc(s["xnT_ready"], 1)
                    act.wait_ge(s["halo_ready"], after(g - 1))
                    for m in range(NG):
                        act.wait_ge(s["f_in_psum"], after(NG * g + m))
                        nc.scalar.activation(feat[p][:, m, W:W + GW], pF[:, m % 2, :], ACT.Copy
                                             ).then_inc(s["f_ready"], 1)
                    with act.Fori(0, NW) as iw:
                        for k in range(KW):
                            w = KW * iw + k
                            n = W * g + w
                            act.wait_ge(s["diff_dve"], after(n))
                            act.wait_ge(s["diff_pool"], after(n))
                            nc.scalar.activation(pair[k][:], pair[k][:], ACT.Gelu, bias=wt["offset"][:, at(w)]
                                                 ).then_inc(s["gelu_ready"], 1)
                    for j in range(GT):
                        t = GT * g + j
                        act.wait_ge(s["l_ready"], after(2 * NW * (g + 1) - 1))
                        damage = logit[:, j, 1].rearrange("p w h k -> p (w h k)")
                        nc.scalar.activation(damage, damage, ACT.Tanh, scale=0.5, bias=wt["half_damage_b"][:]
                                             ).then_inc(s["tanh_ready"], 1)
                    for j in range(GT):
                        t = GT * g + j
                        act.wait_ge(s["soft_step"], after(3 * t + 2))
                        bond = logit[:, j, 0].rearrange("p w h k -> p (w h k)")
                        nc.scalar.activation(bond, bond, ACT.Exp).then_inc(s["exp_ready"], 1)
                    for j in range(GT):
                        t = GT * g + j
                        for hp in range(H // 2):
                            n = H // 2 * t + hp
                            act.wait_ge(s["a_in_psum"], after(n))
                            nc.scalar.activation(wideT[hp % 2][:].rearrange("p h b t -> p (h b t)"), pA[:, hp % 2, :],
                                                 ACT.Copy).then_inc(s["a_ready"], 1)
                        act.wait_ge(s["o_in_psum"], after(t))
                        nc.scalar.activation(oT[:], pO[:], ACT.Copy).then_inc(s["oT_ready"], 1)

        @block.gpsimd
        def _(pool):
            for n in ("diff_pool", "damage_ready", "masked", "halo_ready"):
                pool.sem_inc(s[n], LEAD)
            pool.wait_ge(s["setup"], 5)

            def two_groups(i):
                for p in range(2):
                    g = 2 * i + p
                    pool.wait_ge(s["f_ready"], after(NG * g + NG - 1))
                    pool.wait_ge(s["diff_dve"], after(W * (g - 1) - 1))
                    pool.sem_inc(s["pool_turn"], 1)
                    nc.gpsimd.tensor_copy(feat[p][:, :, 0:W], feat[1 - p][:, :, GW:GW + W]).then_inc(s["halo_ready"], 1)
                    pool.wait_ge(s["halo_ready"], after(g))
                    pool.sem_inc(s["pool_turn"], 1)
                    with pool.Fori(0, NW) as iw:
                        for k in range(KW):
                            w = KW * iw + k
                            n = W * g + w
                            pool.wait_ge(s["reduced"], after(n - RING))
                            nc.gpsimd.tensor_tensor(pair[k][:, NG - 1:NG, :], feat[p][:, NG - 1:NG, at(w + 1, GW)],
                                                    feat[p][:, NG - 1:NG, W:W + GW], ALU.subtract
                                                    ).then_inc(s["diff_pool"], 1)
                    for j in range(GT):
                        t = GT * g + j
                        pool.wait_ge(s["tanh_ready"], after(t))
                        pool.sem_inc(s["pool_turn"], 1)
                        damage = logit[:, j, 1].rearrange("p w h k -> p (w h k)")
                        nc.gpsimd.tensor_scalar(damage, damage, 1.0, -5.0, ALU.add, ALU.mult
                                                ).then_inc(s["damage_ready"], 1)
                        if isinstance(g, int) and t == 0:
                            pool.wait_ge(s["damage_ready"], after(t))
                            nc.gpsimd.affine_select(out=logit[:, j, 1], in_=logit[:, j, 1], compare_op=ALU.is_ge,
                                                    fill=-1e30, base=-(W - 1), pattern=[[KW, NW], [0, H], [1, KW]],
                                                    channel_multiplier=1).then_inc(s["masked"], 1)

            turns(pool, G // 2, two_groups)

        @block.vector
        def _(dve):
            nc.vector.memset(pair[0][:], 0.0).then_inc(s["zeros_ready"], 1)
            for p in range(2):
                nc.vector.memset(val[p][:], 0.0).then_inc(s["setup"], 1)
                nc.vector.memset(feat[p][:], 0.0).then_inc(s["setup"], 1)
            nc.vector.memset(wide[:, :, 0:P - W], 0.0).then_inc(s["setup"], 1)
            for n in ("xn_ready", "v_ready", "diff_dve", "flat_ready", "l_ready", "soft_step", "prob_ready", "y_added"):
                dve.sem_inc(s[n], LEAD)
            dve.wait_ge(s["setup"], 5)
            dve.wait_ge(s["band_zeroed"], 32)

            def two_groups(i):
                for p in range(2):
                    g = 2 * i + p
                    dve.wait_ge(s["xT_in_psum"], after(g - 1))
                    for j in range(GT):
                        t = GT * g + j
                        nc.vector.tensor_scalar(xn[:, j:j + 1, :], x_res[:, at(t), :], mean[:, at(t)],
                                                rstd[:, at(t)], ALU.subtract, ALU.mult).then_inc(s["xn_ready"], 1)
                    dve.wait_ge(s["o_in_psum"], after(GT * (g - 1) - 1))
                    for j in range(GT):
                        dve.wait_ge(s["v_in_psum"], after(GT * g + j))
                        nc.vector.tensor_copy(val[p][:, j, :, 0:BD], pA[:, j % 2, 0:D].rearrange("p (h e) -> p h e", e=BD)
                                              ).then_inc(s["v_ready"], 1)
                    dve.wait_ge(s["halo_ready"], after(g))
                    dve.sem_inc(s["dve_turn"], 1)

                    with dve.Fori(0, NW // 2) as iw:
                        for b in range(2):
                            wg = 2 * iw + b
                            for k in range(KW):
                                w = KW * wg + k
                                n = W * g + w
                                dve.wait_ge(s["reduced"], after(n - RING))
                                nc.vector.tensor_tensor(pair[k][:, 0:NG - 1, :], feat[p][:, 0:NG - 1, at(w + 1, GW)],
                                                        feat[p][:, 0:NG - 1, W:W + GW], ALU.subtract
                                                        ).then_inc(s["diff_dve"], 1)
                            dve.wait_ge(s["reduced"], after(W * g + KW * wg + KW - 1))
                            dve.wait_ge(s["l_in_psum"], after(NW * g + wg - 2))
                            nc.vector.tensor_copy(flat[b][:], pW[:, b, :]).then_inc(s["flat_ready"], 1)
                            dve.wait_ge(s["l_in_psum"], after(NW * g + wg))
                            for kind in range(2):
                                nc.vector.tensor_copy(
                                    logit[:, :, kind, at(wg)].rearrange("p j a (q h) k -> p j (a q) (h k)", q=NG),
                                    pL[:].rearrange("p j (q two x) -> p j q two x", q=NG, two=2)[:, :, :, kind, :]
                                ).then_inc(s["l_ready"], 1)

                    for j in range(GT):
                        t = GT * g + j
                        bond, damage = logit[:, j, 0], logit[:, j, 1]
                        dve.wait_ge(s["damage_ready"], after(t))
                        if isinstance(g, int) and t == 0:
                            dve.wait_ge(s["masked"], after(0))
                        dve.wait_ge(s["l_ready"], after(2 * NW * (g + 1) - 1))
                        nc.vector.tensor_tensor(bond, bond, damage, ALU.add).then_inc(s["soft_step"], 1)
                        dve.wait_ge(s["soft_step"], after(3 * t))
                        nc.vector.tensor_reduce(top[:], bond.rearrange("p w h k -> p h w k"), AX.XY, ALU.max
                                                ).then_inc(s["soft_step"], 1)
                        dve.wait_ge(s["soft_step"], after(3 * t + 1))
                        nc.vector.tensor_tensor(bond, bond, spread(spread(top[:], 1, NW), 3, KW), ALU.subtract
                                                ).then_inc(s["soft_step"], 1)
                    for j in range(GT):
                        t = GT * g + j
                        bond = logit[:, j, 0]
                        dve.wait_ge(s["exp_ready"], after(t))
                        dve.wait_ge(s["prob_ready"], after(3 * t - 1))
                        nc.vector.tensor_reduce(total[:], bond.rearrange("p w h k -> p h w k"), AX.XY, ALU.add
                                                ).then_inc(s["prob_ready"], 1)
                        dve.wait_ge(s["prob_ready"], after(3 * t))
                        nc.vector.reciprocal(total[:], total[:]).then_inc(s["prob_ready"], 1)
                        dve.wait_ge(s["prob_ready"], after(3 * t + 1))
                        dve.wait_ge(s["prob_stored"], landed(t - 1))
                        nc.vector.tensor_tensor(prob[:].rearrange("p h (w k) -> p w h k", k=KW), bond,
                                                spread(spread(total[:], 1, NW), 3, KW), ALU.mult
                                                ).then_inc(s["prob_ready"], 1)
                    for j in range(GT):
                        t = GT * g + j
                        dve.wait_ge(s["y_in_psum"], after(t))
                        nc.vector.tensor_tensor(x_res[:, at(t), :], x_res[:, at(t), :], pF[:, j % 2:j % 2 + 1, 0:D],
                                                ALU.add).then_inc(s["y_added"], 1)

            turns(dve, G // 2, two_groups)


def macaron_kernel(nc, a, out, upto=6, start=0):
    x_in = a["L0_attn_x"]
    T = x_in.shape[1]
    NT = T // P
    E, _, F = a["L0_ffn_w1"].shape
    C = math.ceil(T * 2 / E * 1.2)
    H, BD = 16, 16
    xe = nc.dram_tensor("xe", [E * C + 2 * T, D], F32).ap()
    ye = nc.dram_tensor("ye", [E * C, D], F32).ap()
    with ExitStack() as program:
        ph = Phase(nc, program, "all")
        x_res = ph.sb("x_res", [P, NT, D])
        mean, rstd = ph.sb("mean", [P, NT]), ph.sb("rstd", [P, NT])
        gather_row, weight = ph.sb("gather_row", [P, NT, 2], I32), ph.sb("weight", [P, NT, 2])
        cst = make_constants(nc, ph, NT, E, C, H, BD)
        x_loaded, x_stored = ph.sem("x_loaded"), ph.sem("x_stored")
        tokens = "a (t p) d -> p (a t) d"
        with nc.Block() as block:
            @block.sync
            def _(sp):
                sp.dma_start(x_res[:], x_in.rearrange(tokens, p=P)).then_inc(x_loaded, 16)
                sp.wait_ge(x_loaded, 16)

        def stats(tag):
            layer_norm_stats(nc, tag, x_res, mean, rstd, cst["neg_half"], NT)

        def experts(tag, first):
            stats(tag + "_ln")
            moe_route(nc, tag + "_route", T, E, C, x_res, mean, rstd, cst, a["L0_ffn_gate_w"],
                      a["L0_ffn_gate_b"], xe, gather_row, weight, first)
            moe_experts(nc, tag + "_experts", E, C, F, xe, ye, cst, a["L0_ffn_w1"], a["L0_ffn_b1"],
                        a["L0_ffn_w2"], a["L0_ffn_b2"])
            moe_combine(nc, tag + "_combine", T, x_res, ye, gather_row, weight)

        if start < 1 <= upto:
            experts("moe0", True)
        if start < 2 <= upto:
            stats("linear_ln")
            linear_attention(nc, "linear", T, H, BD, x_res, mean, rstd, cst, a["L0_attn_qkv_w"],
                             a["L0_attn_qkv_b"], a["L0_attn_out_w"], a["L0_attn_out_b"])
        if start < 3 <= upto:
            experts("moe1", start == 2)

        HID = a["L1_ffn_W_exp"].shape[1]
        folded = {"w_up": ph.sb("w_up", [P, DK, HID]), "b_up": ph.sb("b_up", [P, HID // P]),
                  "w_down": ph.sb("w_down", [P, HID // P, D]), "b_down": ph.sb("b_down", [P, D])}
        if start < 6 and upto > 3:
            fold_butterflies(nc, "fold", cst, a["L1_ffn_W_exp"], a["L1_ffn_b_exp"],
                             a["L1_ffn_up_weights"], a["L1_ffn_up_bias"], a["L1_ffn_down_weights"],
                             a["L1_ffn_W_con"], a["L1_ffn_b_con"], a["L1_ffn_down_bias"], folded)
        if start < 4 <= upto:
            stats("ffn0_ln")
            butterfly_ffn(nc, "ffn0", T, x_res, mean, rstd, cst, folded)
        if start < 5 <= upto:
            stats("window_ln")
            window_attention(nc, "window", T, H, BD, x_res, mean, rstd, cst, a)
        if start < 6 <= upto:
            stats("ffn1_ln")
            butterfly_ffn(nc, "ffn1", T, x_res, mean, rstd, cst, folded)

        with nc.Block() as block:
            @block.sync
            def _(sp):
                sp.dma_start(out.rearrange(tokens, p=P), x_res[:]).then_inc(x_stored, 16)
                sp.wait_ge(x_stored, 16)


def kernel(**inputs):
    import numpy as _np
    import concourse.bacc as _bacc
    from concourse import mybir as _mybir
    from concourse.bass_utils import run_bass_kernel_spmd as _run

    nc = _bacc.Bacc("TRN2", target_bir_lowering=False, num_devices=1)
    arrays, aps = {}, {}
    for name, value in inputs.items():
        a = _np.ascontiguousarray(value)
        arrays[f"in_{name}_dram"] = a
        aps[name] = nc.dram_tensor(f"in_{name}_dram", a.shape, _mybir.dt.from_np(a.dtype), kind="ExternalInput").ap()
    shape = inputs["L0_attn_x"].shape
    out = nc.dram_tensor("out_0_dram", shape, F32, kind="ExternalOutput").ap()
    macaron_kernel(nc, aps, out)
    r = _run(nc, [arrays], core_ids=[0])
    return r.results[0]["out_0_dram"]
```

```python
import math
from contextlib import ExitStack

import concourse.bass as bass
from concourse import mybir

F32 = mybir.dt.float32
I32 = mybir.dt.int32
ALU = mybir.AluOpType
ACT = mybir.ActivationFunctionType
AX = mybir.AxisListType

P = 128
D = 256
DK = D // P
GT = 4
GW = GT * P
LN_EPS = 1e-5

LEAD = 128


def after(n):
    return n + 1 + LEAD


def landed(n, dmas=1):
    return 16 * dmas * (n + 2)


def sw_landed(n, dmas=1):
    return 16 * dmas * (n + 1)


def turns(eng, n, body):
    body(0)
    with eng.Fori(1, n) as i:
        body(i)


def at(t, n=1):
    return bass.ds(t, n)


def spread(ap, axis, n):
    shape = list(ap.shape)
    shape.insert(axis, n)
    return ap.unsqueeze(axis).broadcast_to(shape)


class Phase:

    def __init__(self, nc, memory, tag):
        self.nc, self.memory, self.tag, self.taken = nc, memory, tag, []
        memory.callback(self.give_back)

    def sb(self, name, shape, dt=F32):
        return self.memory.enter_context(self.nc.sbuf_tensor(f"{self.tag}_{name}", shape, dt))

    def ps(self, name, shape):
        return self.memory.enter_context(self.nc.psum_tensor(f"{self.tag}_{name}", shape, F32))

    def sem(self, name):
        self.taken.append(self.nc.alloc_semaphore(name=f"{self.tag}_{name}"))
        return self.taken[-1]

    def sems(self, name):
        return [self.sem(f"{name}{p}") for p in range(2)]

    def pool_dma_sems(self, name):
        return [self.nc.alloc_semaphore(name=f"{self.tag}_{name}{p}") for p in range(2)]

    def give_back(self):
        with self.nc.Block() as block:
            @block.gpsimd
            def _(pool):
                for sem in self.taken:
                    pool.sem_clear(sem)
        for sem in self.taken:
            self.nc.release_semaphore(sem)


def chain(eng, sem):
    count = [0]

    def link(ins):
        count[0] += 1
        ins.then_inc(sem, 1)
        eng.wait_ge(sem, count[0])

    return link


def make_constants(nc, ph, NT, E, C, H, BD):
    c = {
        "ident": ph.sb("ident", [P, P]),
        "lower": ph.sb("lower", [P, P]),
        "causal": ph.sb("causal", [P, P]),
        "ones": ph.sb("ones", [P, P]),
        "rev": ph.sb("rev", [P, E]),
        "dump": ph.sb("dump", [P, 2, NT]),
        "keep": ph.sb("keep", [P, E, NT]),
        "head_block": ph.sb("head_block", [P, P // BD, BD + 1]),
        "parity": ph.sb("parity", [P, 2]),
        "neg_half": ph.sb("neg_half", [P, NT]),
    }
    with ExitStack() as memory:
        tmp = Phase(nc, memory, "cst")
        rev_i = tmp.sb("rev_i", [P, E], I32)
        dump_i = tmp.sb("dump_i", [P, 2, NT], I32)
        filled, shaped, ints = tmp.sem("filled"), tmp.sem("shaped"), tmp.sem("ints")
        block = memory.enter_context(nc.Block())

        @block.gpsimd
        def _(pool):
            nc.gpsimd.memset(c["ident"][:], 0.0).then_inc(filled, 1)
            for name in ("lower", "causal", "ones", "head_block"):
                nc.gpsimd.memset(c[name][:], 1.0).then_inc(filled, 1)
            nc.gpsimd.iota(rev_i[:], pattern=[[-1, E]], base=E, channel_multiplier=0).then_inc(ints, 1)
            nc.gpsimd.iota(dump_i[:], pattern=[[1, 2], [2 * P, NT]], base=E * C, channel_multiplier=2).then_inc(ints, 1)
            pool.wait_ge(filled, 5)
            nc.gpsimd.affine_select(out=c["ident"][:], in_=c["ident"][:], compare_op=ALU.not_equal, fill=1.0,
                                    base=0, pattern=[[-1, P]], channel_multiplier=1).then_inc(shaped, 1)
            nc.gpsimd.affine_select(out=c["lower"][:], in_=c["lower"][:], compare_op=ALU.is_gt, fill=0.0,
                                    base=0, pattern=[[1, P]], channel_multiplier=-1).then_inc(shaped, 1)
            nc.gpsimd.affine_select(out=c["causal"][:], in_=c["causal"][:], compare_op=ALU.is_ge, fill=0.0,
                                    base=0, pattern=[[1, P]], channel_multiplier=-1).then_inc(shaped, 1)
            hb = c["head_block"]
            nh = P // BD
            nc.gpsimd.affine_select(out=hb[:], in_=hb[:], compare_op=ALU.is_ge, fill=0.0, base=0,
                                    pattern=[[-BD, nh], [0, BD + 1]], channel_multiplier=1).then_inc(shaped, 1)
            pool.wait_ge(shaped, 4)
            nc.gpsimd.affine_select(out=hb[:], in_=hb[:], compare_op=ALU.is_ge, fill=0.0, base=BD - 1,
                                    pattern=[[BD, nh], [0, BD + 1]], channel_multiplier=-1).then_inc(shaped, 1)

        @block.vector
        def _(dve):
            dve.wait_ge(ints, 2)
            nc.vector.tensor_copy(c["rev"][:], rev_i[:])
            nc.vector.tensor_copy(c["dump"][:], dump_i[:])
            nc.vector.memset(c["keep"][:], 1.0).then_inc(ints, 1)
            nc.vector.memset(c["neg_half"][:], -0.5)
            dve.wait_ge(ints, 3)
            nc.vector.memset(c["keep"][:, :, 0:1], 0.0)
            dve.wait_ge(shaped, 5)
            pairs = c["head_block"][:, :, 0].rearrange("p (h two) -> p two h", two=2)
            nc.vector.reduce_sum(c["parity"][:], pairs, AX.X)
    return c


def layer_norm_stats(nc, tag, x_res, mean, rstd, neg_half, NT):
    with ExitStack() as memory:
        ph = Phase(nc, memory, tag)
        stats = ph.sb("stats", [P, NT, 6])
        msum, mdif, m2, var = (ph.sb(n, [P, NT]) for n in ("msum", "mdif", "m2", "var"))
        stats_done, moments, rstd_ready = ph.sem("stats_done"), ph.sem("moments"), ph.sem("rstd_ready")
        block = memory.enter_context(nc.Block())

        @block.vector
        def _(dve):
            with dve.Fori(0, NT // 4) as i:
                for j in range(4):
                    nc.vector.bn_stats(stats[:, at(4 * i + j), :].rearrange("p a s -> p (a s)"),
                                       x_res[:, at(4 * i + j), :].rearrange("p a d -> p (a d)")).then_inc(stats_done, 1)
            dve.wait_ge(stats_done, NT)
            even, odd = stats[:, :, 1], stats[:, :, 4]
            nc.vector.tensor_tensor(msum[:], even, odd, ALU.add).then_inc(moments, 1)
            nc.vector.tensor_tensor(mdif[:], even, odd, ALU.subtract).then_inc(moments, 1)
            nc.vector.tensor_tensor(m2[:], stats[:, :, 2], stats[:, :, 5], ALU.add).then_inc(moments, 1)
            dve.wait_ge(moments, 3)
            nc.vector.tensor_scalar(mean[:], msum[:], 0.5, None, ALU.mult).then_inc(moments, 1)
            nc.vector.tensor_tensor(mdif[:], mdif[:], mdif[:], ALU.mult).then_inc(moments, 1)
            nc.vector.tensor_scalar(m2[:], m2[:], 1.0 / D, LN_EPS, ALU.mult, ALU.add).then_inc(moments, 1)
            dve.wait_ge(moments, 6)
            nc.vector.scalar_tensor_tensor(out=var[:], in0=mdif[:], scalar=0.25, in1=m2[:],
                                           op0=ALU.mult, op1=ALU.add).then_inc(moments, 1)

        @block.gpsimd
        def _(pool):
            pool.wait_ge(moments, 7)
            nc.gpsimd.tensor_tensor(rstd[:], var[:], neg_half[:], ALU.pow).then_inc(rstd_ready, 1)
            pool.wait_ge(rstd_ready, 1)


def moe_route(nc, tag, T, E, C, x_res, mean, rstd, cst, gate_w, gate_b, xe, gather_row, weight,
              first):
    NT, G = T // P, T // GW
    ident = cst["ident"]
    with ExitStack() as memory:
        ph = Phase(nc, memory, tag)
        gw, gb = ph.sb("gw", [P, DK, E]), ph.sb("gb", [P, E])
        xn = [ph.sb(f"xn{p}", [P, GT, D]) for p in range(2)]
        xnT = [ph.sb(f"xnT{p}", [P, DK, GW]) for p in range(2)]
        logits, work, work2 = (ph.sb(n, [P, NT, E]) for n in ("logits", "work", "work2"))
        hot = [ph.sb(f"hot{k}", [P, NT, E]) for k in range(2)]
        best, rank, place, first_row, valid, row, share = (
            [ph.sb(f"{n}{k}", [P, NT]) for k in range(2)]
            for n in ("best", "rank", "place", "first_row", "valid", "row", "share"))
        totals, scan = ph.sb("totals", [P, E, NT]), ph.sb("scan", [P, E, NT])
        scatter_row = ph.sb("scatter_row", [P, NT, 2], I32)
        stage_row = [ph.sb(f"stage_row{p}", [P, 2], I32) for p in range(2)]
        stage_x = [ph.sb(f"stage_x{p}", [P, D]) for p in range(2)]
        ZW = 2048
        zeros = ph.sb("zeros", [P, ZW]) if first else None
        pT = [ph.ps(f"pT{p}", [P, DK, GW]) for p in range(2)]
        pL = [ph.ps(f"pL{p}", [P, GT, E]) for p in range(2)]

        gate_loaded, zeros_ready, zeroed = ph.sem("gate_loaded"), ph.sem("zeros_ready"), ph.sem("zeroed")
        xn_ready, xT_in_psum, xnT_ready, logits_in_psum, logits_ready = (
            ph.sem(n) for n in ("xn_ready", "xT_in_psum", "xnT_ready", "logits_in_psum", "logits_ready"))
        step, gap_ready, ratio_ready, hot_ready, counts_in_psum = (
            ph.sem(n) for n in ("step", "gap_ready", "ratio_ready", "hot_ready", "counts_in_psum"))
        staged, scattered, turn = ph.sem("staged"), ph.pool_dma_sems("scattered"), ph.sem("turn")
        block = memory.enter_context(nc.Block())

        @block.sync
        def _(sp):
            sp.dma_start(gw[:], gate_w.rearrange("(k p) e -> p k e", p=P)).then_inc(gate_loaded, 16)
            sp.dma_start(gb[:], gate_b.partition_broadcast(P)).then_inc(gate_loaded, 16)
            if first:
                sp.wait_ge(zeros_ready, 1)
                flat = xe[0:E * C, :].rearrange("r d -> (r d)")
                whole, rest = divmod(E * C * D, P * ZW)
                for z in range(whole):
                    sp.dma_start(flat[z * P * ZW:(z + 1) * P * ZW].rearrange("(p f) -> p f", p=P),
                                 zeros[:]).then_inc(zeroed, 16)
                sp.dma_start(flat[whole * P * ZW:].rearrange("(p f) -> p f", p=P),
                             zeros[:, 0:rest // P]).then_inc(zeroed, 16)
                sp.wait_ge(zeroed, 16 * (whole + 1))

        @block.vector
        def _(dve):
            dve.sem_inc(xn_ready, LEAD)
            dve.sem_inc(logits_ready, LEAD)
            dve.sem_inc(staged, LEAD)
            if first:
                nc.vector.memset(zeros[:], 0.0).then_inc(zeros_ready, 1)
            dve.wait_ge(gate_loaded, 32)
            with dve.Fori(0, G // 2) as i:
                for p in range(2):
                    g = 2 * i + p
                    dve.wait_ge(xT_in_psum, after(g - 2))
                    for j in range(GT):
                        t = GT * g + j
                        nc.vector.tensor_scalar(xn[p][:, j:j + 1, :], x_res[:, at(t), :], mean[:, at(t)],
                                                rstd[:, at(t)], ALU.subtract, ALU.mult).then_inc(xn_ready, 1)
                    dve.wait_ge(logits_in_psum, after(g))
                    nc.vector.tensor_tensor(logits[:, at(GT * g, GT), :], pL[p][:], spread(gb[:], 1, GT),
                                            ALU.add).then_inc(logits_ready, 1)
            dve.wait_ge(logits_ready, after(G - 1))

            link = chain(dve, step)
            rev = spread(cst["rev"][:], 1, NT)
            for k, src in ((0, logits), (1, work2)):
                link(nc.vector.reduce_max(best[k][:], src[:], AX.X))
                link(nc.vector.tensor_tensor(work[:], src[:], spread(best[k][:], 2, E), ALU.is_equal))
                link(nc.vector.tensor_tensor(work[:], work[:], rev, ALU.mult))
                link(nc.vector.reduce_max(rank[k][:], work[:], AX.X))
                link(nc.vector.tensor_tensor(hot[k][:], rev, spread(rank[k][:], 2, E), ALU.is_equal))
                if k == 0:
                    link(nc.vector.scalar_tensor_tensor(out=work2[:], in0=hot[0][:], scalar=-1e38, in1=src[:],
                                                        op0=ALU.mult, op1=ALU.add))
            nc.vector.tensor_tensor(work[:], hot[0][:], hot[1][:], ALU.add).then_inc(hot_ready, 1)
            link(nc.vector.tensor_tensor(share[1][:], best[1][:], best[0][:], ALU.subtract))
            dve.sem_inc(gap_ready, 1)
            dve.wait_ge(ratio_ready, 1)
            link(nc.vector.tensor_scalar(share[0][:], valid[0][:], 1.0, None, ALU.add))
            link(nc.vector.reciprocal(share[0][:], share[0][:]))
            link(nc.vector.tensor_tensor(share[1][:], valid[0][:], share[0][:], ALU.mult))

            dve.wait_ge(counts_in_psum, 1)
            link(nc.vector.tensor_copy(totals[:], pT_view(pT[1], NT, E).rearrange("p t e -> p e t")))
            link(nc.vector.tensor_tensor_scan(scan[:].rearrange("p e t -> p (e t)"),
                                              cst["keep"][:].rearrange("p e t -> p (e t)"),
                                              totals[:].rearrange("p e t -> p (e t)"), 0.0, ALU.mult, ALU.add))
            link(nc.vector.tensor_tensor(totals[:], scan[:], totals[:], ALU.subtract))
            link(nc.vector.tensor_tensor(work2[:], pT_view(pT[0], NT, E), totals[:].rearrange("p e t -> p t e"),
                                         ALU.add))
            for k in range(2):
                link(nc.vector.tensor_tensor(work[:], work2[:], hot[k][:], ALU.mult))
                link(nc.vector.reduce_sum(place[k][:], work[:], AX.X))
                link(nc.vector.tensor_scalar(first_row[k][:], rank[k][:], -float(C), float(E * C), ALU.mult, ALU.add))
                link(nc.vector.tensor_scalar(valid[k][:], place[k][:], float(C), None, ALU.is_lt))
                link(nc.vector.scalar_tensor_tensor(out=gather_row[:, :, k], in0=place[k][:], scalar=float(C - 1),
                                                    in1=first_row[k][:], op0=ALU.min, op1=ALU.add))
                link(nc.vector.tensor_tensor(row[k][:], place[k][:], first_row[k][:], ALU.add))
                link(nc.vector.tensor_tensor(row[k][:], row[k][:], cst["dump"][:, k, :], ALU.subtract))
                link(nc.vector.tensor_tensor(row[k][:], row[k][:], valid[k][:], ALU.mult))
                link(nc.vector.tensor_tensor(scatter_row[:, :, k], row[k][:], cst["dump"][:, k, :], ALU.add))
                link(nc.vector.scalar_tensor_tensor(out=weight[:, :, k], in0=share[k][:], scalar=0.5,
                                                    in1=valid[k][:], op0=ALU.mult, op1=ALU.mult))
            def stage(i):
                for p in range(2):
                    t = 2 * i + p
                    if not (isinstance(i, int) and i == 0):
                        dve.wait_ge(scattered[p], sw_landed(i - 1, 2))
                    nc.vector.tensor_copy(stage_row[p][:], scatter_row[:, at(t), :].rearrange("p a k -> p (a k)")
                                          ).then_inc(staged, 1)
                    nc.vector.tensor_scalar(stage_x[p][:], x_res[:, at(t), :].rearrange("p a d -> p (a d)"),
                                            mean[:, at(t)], rstd[:, at(t)], ALU.subtract,
                                            ALU.mult).then_inc(staged, 1)

            turns(dve, NT // 2, stage)

        @block.scalar
        def _(act):
            act.sem_inc(xnT_ready, LEAD)
            with act.Fori(0, G // 2) as i:
                for p in range(2):
                    g = 2 * i + p
                    act.wait_ge(xT_in_psum, after(g))
                    act.wait_ge(logits_in_psum, after(g - 2))
                    nc.scalar.activation(xnT[p][:], pT[p][:], ACT.Copy).then_inc(xnT_ready, 1)
            act.wait_ge(gap_ready, 1)
            nc.scalar.activation(valid[0][:], share[1][:], ACT.Exp).then_inc(ratio_ready, 1)

        @block.tensor
        def _(pe):
            pe.sem_inc(xT_in_psum, LEAD)
            pe.sem_inc(logits_in_psum, LEAD)
            pe.wait_ge(gate_loaded, 32)
            with pe.Fori(0, G // 2) as i:
                for p in range(2):
                    g = 2 * i + p
                    pe.wait_ge(xn_ready, after(GT * g + GT - 1))
                    pe.wait_ge(xnT_ready, after(g - 2))
                    for j in range(GT):
                        for k in range(DK):
                            last = nc.tensor.transpose(pT[p][:, k, j * P:(j + 1) * P],
                                                       xn[p][:, j, k * P:(k + 1) * P], ident[:])
                    last.then_inc(xT_in_psum, 1)
                    pe.wait_ge(xnT_ready, after(g))
                    pe.wait_ge(logits_ready, after(g - 2))
                    for j in range(GT):
                        for k in range(DK):
                            last = nc.tensor.matmul(pL[p][:, j, :], xnT[p][:, k, j * P:(j + 1) * P], gw[:, k, :],
                                                    start=(k == 0), stop=(k == DK - 1))
                    last.then_inc(logits_in_psum, 1)
            pe.wait_ge(hot_ready, 1)
            for m, src in ((0, cst["lower"]), (1, cst["ones"])):
                for h in range(NT * E // 512):
                    last = nc.tensor.matmul(pT_view(pT[m], NT, E)[:, h * 512 // E:(h + 1) * 512 // E, :], src[:],
                                            work[:, h * 512 // E:(h + 1) * 512 // E, :], start=True, stop=True)
            last.then_inc(counts_in_psum, 1)

        @block.gpsimd
        def _(pool):
            if first:
                pool.wait_ge(zeroed, 16 * (math.ceil(E * C * D / (P * ZW))))
            with pool.Fori(0, NT // 2) as i:
                for p in range(2):
                    t = 2 * i + p
                    pool.wait_ge(staged, after(2 * t + 1))
                    pool.sem_inc(turn, 1)
                    for k in range(2):
                        pool.indirect_dma_start(
                            out=xe, out_offset=bass.IndirectOffsetOnAxis(ap=stage_row[p][:, k:k + 1], axis=0),
                            in_=stage_x[p][:], in_offset=None).then_inc(scattered[p], 16)
            for p in range(2):
                pool.wait_ge(scattered[p], sw_landed(NT // 2 - 1, 2))


def pT_view(bank_pair, NT, E):
    return bank_pair[:].rearrange("p a b -> p (a b)").rearrange("p (t e) -> p t e", e=E)


def moe_experts(nc, tag, E, C, F, xe, ye, cst, w1, b1, w2, b2):
    ident = cst["ident"]
    FK = F // P
    tiles = [(j * P, min(P, C - j * P)) for j in range(math.ceil(C / P))]
    NJ = len(tiles)
    whole = C // P
    with ExitStack() as memory:
        ph = Phase(nc, memory, tag)
        w1s = [ph.sb(f"w1s{p}", [P, DK, F]) for p in range(2)]
        w2s = [ph.sb(f"w2s{p}", [P, FK, D]) for p in range(2)]
        b2s = [ph.sb(f"b2s{p}", [P, D]) for p in range(2)]
        b1r, b1T = ph.sb("b1r", [E, F]), ph.sb("b1T", [P, FK, E])
        xr = [ph.sb(f"xr{p}", [P, NJ, D]) for p in range(2)]
        xT = [ph.sb(f"xT{p}", [P, DK, C]) for p in range(2)]
        hT = [ph.sb(f"hT{p}", [P, FK, C]) for p in range(2)]
        yo = [ph.sb(f"yo{p}", [P, NJ, D]) for p in range(2)]
        pX = ph.ps("pX", [P, DK, 512])
        NH = 4
        pH = ph.ps("pH", [P, NH, 512])
        pY = ph.ps("pY", [P, 2, 512])

        b1_loaded, b1_in_psum, b1_ready = ph.sem("b1_loaded"), ph.sem("b1_in_psum"), ph.sem("b1_ready")
        w1_loaded, w2_loaded, b2_loaded, x_loaded = (
            ph.sems(n) for n in ("w1_loaded", "w2_loaded", "b2_loaded", "x_loaded"))
        stored = ph.pool_dma_sems("stored")
        xT_in_psum, xT_ready, h_in_psum, h_ready, y_in_psum, y_ready = (
            ph.sem(n) for n in ("xT_in_psum", "xT_ready", "h_in_psum", "h_ready", "y_in_psum", "y_ready"))
        block = memory.enter_context(nc.Block())

        @block.sync
        def _(sp):
            for p in range(2):
                for s in (w1_loaded, w2_loaded, b2_loaded):
                    sp.sem_inc(s[p], 16)
                sp.sem_inc(x_loaded[p], 32)
            sp.dma_start(b1r[:], b1).then_inc(b1_loaded, 16)
            with sp.Fori(0, E // 2) as i:
                for p in range(2):
                    e = 2 * i + p
                    sp.wait_ge(xT_in_psum, after(e - 2))
                    sp.dma_start(xr[p][:, 0:whole, :],
                                 xe[at(e * C, whole * P), :].rearrange("(j q) d -> q j d", q=P)
                                 ).then_inc(x_loaded[p], 16)
                    sp.dma_start(xr[p][0:C - whole * P, whole, :], xe[at(e * C + whole * P, C - whole * P), :]
                                 ).then_inc(x_loaded[p], 16)
                    sp.wait_ge(h_in_psum, after(FK * (e - 1) - 1))
                    sp.dma_start(w1s[p][:], w1[at(e), :, :].rearrange("a (k q) f -> q (a k) f", q=P)
                                 ).then_inc(w1_loaded[p], 16)
                    sp.wait_ge(y_in_psum, after(NJ * (e - 1) - 1))
                    sp.dma_start(w2s[p][:], w2[at(e), :, :].rearrange("a (k q) d -> q (a k) d", q=P)
                                 ).then_inc(w2_loaded[p], 16)
                    sp.wait_ge(y_ready, after(NJ * (e - 1) - 1))
                    sp.dma_start(b2s[p][:], b2[at(e), :].rearrange("a d -> (a d)").partition_broadcast(P)
                                 ).then_inc(b2_loaded[p], 16)

        def pY_bank(j, p):
            return (NJ * p + j) % 2

        def transpose_queue(pe, e, i, p):
            pe.wait_ge(x_loaded[p], landed(i, 2))
            pe.wait_ge(xT_ready, after(e - 1))
            for j, (at_row, n) in enumerate(tiles):
                for k in range(DK):
                    last = nc.tensor.transpose(pX[:, k, at_row:at_row + n], xr[p][0:n, j, k * P:(k + 1) * P],
                                               ident[0:n, 0:n])
            last.then_inc(xT_in_psum, 1)

        @block.tensor
        def _(pe):
            for s in (xT_in_psum, h_in_psum, y_in_psum):
                pe.sem_inc(s, LEAD)
            pe.wait_ge(b1_loaded, 16)
            for f in range(FK):
                last = nc.tensor.transpose(pH[:, 0, f * E:(f + 1) * E], b1r[:, f * P:(f + 1) * P], ident[0:E, 0:E])
            last.then_inc(b1_in_psum, 1)
            transpose_queue(pe, 0, 0, 0)
            pe.wait_ge(b1_ready, 1)

            def expert(i, p, last_of_all=False):
                e = 2 * i + p
                pe.wait_ge(w1_loaded[p], landed(i))
                pe.wait_ge(xT_ready, after(e))
                for f in range(FK):
                    pe.wait_ge(h_ready, after(FK * e + f - NH))
                    for k in range(DK):
                        last = nc.tensor.matmul(pH[:, f % NH, 0:C], w1s[p][:, k, f * P:(f + 1) * P], xT[p][:, k, :],
                                                start=(k == 0), stop=(k == DK - 1))
                    last.then_inc(h_in_psum, 1)
                if not last_of_all:
                    transpose_queue(pe, e + 1, i + p, 1 - p)
                pe.wait_ge(w2_loaded[p], landed(i))
                pe.wait_ge(h_ready, after(FK * e + FK - 1))
                for j, (at_row, n) in enumerate(tiles):
                    pe.wait_ge(y_ready, after(NJ * e + j - 2))
                    bank = pY_bank(j, p)
                    for f in range(FK):
                        last = nc.tensor.matmul(pY[0:n, bank, 0:D], hT[p][:, f, at_row:at_row + n], w2s[p][:, f, :],
                                                start=(f == 0), stop=(f == FK - 1))
                    last.then_inc(y_in_psum, 1)

            with pe.Fori(0, E // 2 - 1) as i:
                for p in range(2):
                    expert(i, p)
            expert(E // 2 - 1, 0)
            expert(E // 2 - 1, 1, last_of_all=True)

        @block.scalar
        def _(act):
            act.sem_inc(xT_ready, LEAD)
            act.sem_inc(h_ready, LEAD)
            act.wait_ge(b1_in_psum, 1)
            nc.scalar.activation(b1T[:], pH[:, 0, 0:FK * E].rearrange("p (f e) -> p f e", e=E), ACT.Copy
                                 ).then_inc(b1_ready, 1)

            def copy_xT(e, p):
                act.wait_ge(xT_in_psum, after(e))
                act.wait_ge(h_in_psum, after(FK * (e - 1) - 1))
                nc.scalar.activation(xT[p][:], pX[:, :, 0:C], ACT.Copy).then_inc(xT_ready, 1)

            copy_xT(0, 0)
            act.wait_ge(b1_ready, 1)

            def expert(i, p, last_of_all=False):
                e = 2 * i + p
                act.wait_ge(y_in_psum, after(NJ * (e - 1) - 1))
                for f in range(FK):
                    act.wait_ge(h_in_psum, after(FK * e + f))
                    nc.scalar.activation(hT[p][:, f, :], pH[:, f % NH, 0:C], ACT.Gelu,
                                         bias=b1T[:, f, at(e)]).then_inc(h_ready, 1)
                if not last_of_all:
                    copy_xT(e + 1, 1 - p)

            with act.Fori(0, E // 2 - 1) as i:
                for p in range(2):
                    expert(i, p)
            expert(E // 2 - 1, 0)
            expert(E // 2 - 1, 1, last_of_all=True)

        @block.vector
        def _(dve):
            dve.sem_inc(y_ready, LEAD)

            def add_bias(i):
                for p in range(2):
                    e = 2 * i + p
                    dve.wait_ge(b2_loaded[p], landed(i))
                    if not (isinstance(i, int) and i == 0):
                        dve.wait_ge(stored[p], sw_landed(i - 1, 2))
                    for j, (_, n) in enumerate(tiles):
                        dve.wait_ge(y_in_psum, after(NJ * e + j))
                        nc.vector.tensor_tensor(yo[p][0:n, j, :], pY[0:n, pY_bank(j, p), 0:D], b2s[p][0:n, :],
                                                ALU.add).then_inc(y_ready, 1)

            turns(dve, E // 2, add_bias)

        @block.gpsimd
        def _(pool):
            with pool.Fori(0, E // 2) as i:
                for p in range(2):
                    e = 2 * i + p
                    pool.wait_ge(y_ready, after(NJ * e + NJ - 1))
                    pool.dma_start(ye[at(e * C, whole * P), :].rearrange("(j q) d -> q j d", q=P),
                                   yo[p][:, 0:whole, :]).then_inc(stored[p], 16)
                    pool.dma_start(ye[at(e * C + whole * P, C - whole * P), :],
                                   yo[p][0:C - whole * P, whole, :]).then_inc(stored[p], 16)
            for p in range(2):
                pool.wait_ge(stored[p], sw_landed(E // 2 - 1, 2))


def moe_combine(nc, tag, T, x_res, ye, gather_row, weight):
    NT = T // P
    with ExitStack() as memory:
        ph = Phase(nc, memory, tag)
        row = [ph.sb(f"row{p}", [P, 2], I32) for p in range(2)]
        got = [ph.sb(f"got{p}", [P, 2, D]) for p in range(2)]
        staged, gathered, added, turn = ph.sem("staged"), ph.pool_dma_sems("gathered"), ph.sem("added"), ph.sem("turn")
        block = memory.enter_context(nc.Block())

        @block.scalar
        def _(act):
            act.sem_inc(staged, LEAD)

            def stage(i):
                for p in range(2):
                    t = 2 * i + p
                    if not (isinstance(i, int) and i == 0):
                        act.wait_ge(gathered[p], sw_landed(i - 1, 2))
                    nc.scalar.activation(row[p][:], gather_row[:, at(t), :].rearrange("p a k -> p (a k)"), ACT.Copy
                                         ).then_inc(staged, 1)

            turns(act, NT // 2, stage)

        @block.gpsimd
        def _(pool):
            with pool.Fori(0, NT // 2) as i:
                for p in range(2):
                    t = 2 * i + p
                    pool.wait_ge(staged, after(t))
                    pool.wait_ge(added, after(2 * (t - 2) + 1))
                    pool.sem_inc(turn, 1)
                    for k in range(2):
                        pool.indirect_dma_start(
                            out=got[p][:, k, :], out_offset=None, in_=ye,
                            in_offset=bass.IndirectOffsetOnAxis(ap=row[p][:, k:k + 1], axis=0)
                        ).then_inc(gathered[p], 16)

        @block.vector
        def _(dve):
            dve.sem_inc(added, LEAD)
            with dve.Fori(0, NT // 2) as i:
                for p in range(2):
                    t = 2 * i + p
                    dve.wait_ge(gathered[p], sw_landed(i, 2))
                    for k in range(2):
                        if k:
                            dve.wait_ge(added, after(2 * t))
                        nc.vector.scalar_tensor_tensor(
                            out=x_res[:, at(t), :], in0=got[p][:, k:k + 1, :],
                            scalar=weight[:, at(t), k:k + 1].rearrange("p a k -> p (a k)"),
                            in1=x_res[:, at(t), :], op0=ALU.mult, op1=ALU.add).then_inc(added, 1)


def fold_butterflies(nc, tag, cst, w_exp, b_exp, up_w, up_b, down_w, w_con, b_con, down_b, folded):
    STAGES, PAIRS = up_w.shape[0], up_w.shape[1]
    HID = 2 * PAIRS
    HK = HID // P
    ident = cst["ident"]
    with ExitStack() as memory:
        ph = Phase(nc, memory, tag)
        up = ph.sb("up", [P, DK + 1, HID])
        down = ph.sb("down", [P, DK, HID])
        con = ph.sb("con", [P, HK, D])
        ub = ph.sb("ub", [1, HID])
        bc = [ph.sb(f"bc{k}", [P, D]) for k in range(2)]
        wu = [ph.sb(f"wu{p}", [P, 4 * PAIRS]) for p in range(2)]
        wd = [ph.sb(f"wd{p}", [P, 4 * PAIRS]) for p in range(2)]
        lo_u, hi_u = ph.sb("lo_u", [P, DK + 1, HID]), ph.sb("hi_u", [P, DK + 1, HID])
        lo_d, hi_d = ph.sb("lo_d", [P, DK, HID]), ph.sb("hi_d", [P, DK, HID])
        pD = ph.ps("pD", [P, DK, HID])
        pB = ph.ps("pB", [P, HK])
        loaded, up_loaded, down_loaded = ph.sem("loaded"), ph.sems("up_loaded"), ph.sems("down_loaded")
        up_step, down_step = ph.sem("up_step"), ph.sem("down_step")
        con_in_psum, con_ready, back_in_psum, folded_ready = (
            ph.sem(n) for n in ("con_in_psum", "con_ready", "back_in_psum", "folded_ready"))
        block = memory.enter_context(nc.Block())
        PER = 3

        @block.sync
        def _(sp):
            sp.dma_start(con[:], w_con.rearrange("(k p) d -> p k d", p=P)).then_inc(loaded, 16)
            sp.dma_start(up[:, 0:DK, :], w_exp.rearrange("(k p) h -> p k h", p=P)).then_inc(loaded, 16)
            sp.dma_start(up[:, DK, :], b_exp.partition_broadcast(P)).then_inc(loaded, 16)
            sp.dma_start(ub[:], up_b.rearrange("(a h) -> a h", a=1)).then_inc(loaded, 16)
            sp.dma_start(bc[0][:], b_con.partition_broadcast(P)).then_inc(loaded, 16)
            sp.dma_start(bc[1][:], down_b.partition_broadcast(P)).then_inc(loaded, 16)
            for s in range(STAGES):
                if s >= 2:
                    sp.wait_ge(up_step, PER * (s - 1))
                    sp.wait_ge(down_step, PER * (s - 1))
                sp.dma_start(wu[s % 2][:], up_w[s].rearrange("n i c -> (n i c)").partition_broadcast(P)
                             ).then_inc(up_loaded[s % 2], 16)
                sp.dma_start(wd[s % 2][:], down_w[STAGES - 1 - s].rearrange("n i c -> (n i c)").partition_broadcast(P)
                             ).then_inc(down_loaded[s % 2], 16)

        def stage(eng, y, w, lo, hi, s, rows, step, transposed, base):
            stride = 2 ** s
            order = "p (n j c i) -> p c n i j" if transposed else "p (n j i c) -> p c n i j"
            wv = w[:].rearrange(order, j=stride, i=2, c=2)
            for half, product in ((0, lo), (1, hi)):
                for r in range(rows):
                    mine = y[:, r, :].rearrange("p (n two j) -> p two n j", two=2, j=stride)[:, half]
                    ins = eng.tensor_tensor(product[:, r, :].rearrange("p (n i j) -> p n i j", i=2, j=stride),
                                            wv[:, half], spread(mine, 2, 2), ALU.mult)
                ins.then_inc(step, 1)
            eng.wait_ge(step, base + 2)
            eng.tensor_tensor(y[:, 0:rows, :], lo[:], hi[:], ALU.add).then_inc(step, 1)
            eng.wait_ge(step, base + 3)

        @block.vector
        def _(dve):
            dve.wait_ge(loaded, 16 * 6)
            for s in range(STAGES):
                dve.wait_ge(up_loaded[s % 2], 16 * (s // 2 + 1))
                stage(nc.vector, up, wu[s % 2], lo_u, hi_u, s, DK + 1, up_step, False, PER * s)
            nc.vector.tensor_tensor(bc[0][:], bc[0][:], bc[1][:], ALU.add).then_inc(up_step, 1)
            nc.vector.tensor_copy(folded["w_up"][:], up[:, 0:DK, :])
            dve.wait_ge(up_step, PER * STAGES + 1)
            nc.vector.tensor_scalar(folded["b_down"][:], bc[0][:], 0.5, None, ALU.mult)

        @block.gpsimd
        def _(pool):
            pool.wait_ge(con_ready, 1)
            for s in range(STAGES):
                pool.wait_ge(down_loaded[s % 2], 16 * (s // 2 + 1))
                stage(nc.gpsimd, down, wd[s % 2], lo_d, hi_d, STAGES - 1 - s, DK, down_step, True, PER * s)

        @block.tensor
        def _(pe):
            pe.wait_ge(loaded, 16 * 6)
            for k in range(HK):
                for m in range(DK):
                    last = nc.tensor.transpose(pD[:, m, k * P:(k + 1) * P], con[:, k, m * P:(m + 1) * P], ident[:])
            last.then_inc(con_in_psum, 1)
            pe.wait_ge(up_step, PER * STAGES)
            for k in range(HK):
                cols = slice(k * P, (k + 1) * P)
                nc.tensor.matmul(pB[:, k:k + 1], up[0:1, DK, cols], cst["ones"][0:1, 0:1], start=True, stop=False)
                last = nc.tensor.matmul(pB[:, k:k + 1], ub[0:1, cols], cst["ones"][0:1, 0:1], start=False, stop=True)
            last.then_inc(back_in_psum, 1)
            pe.wait_ge(down_step, PER * STAGES)
            pe.wait_ge(con_ready, 1)
            for k in range(HK):
                for m in range(DK):
                    last = nc.tensor.transpose(pD[:, :, :].rearrange("p m h -> p (m h)")[:, k * D + m * P:k * D + (m + 1) * P],
                                               down[:, m, k * P:(k + 1) * P], ident[:])
            last.then_inc(back_in_psum, 1)

        @block.scalar
        def _(act):
            act.wait_ge(con_in_psum, 1)
            nc.scalar.activation(down[:], pD[:], ACT.Copy).then_inc(con_ready, 1)
            act.wait_ge(back_in_psum, 1)
            nc.scalar.activation(folded["b_up"][:], pB[:], ACT.Copy)
            act.wait_ge(back_in_psum, 2)
            nc.scalar.activation(folded["w_down"][:].rearrange("p k d -> p (k d)"),
                                 pD[:].rearrange("p m h -> p (m h)"), ACT.Copy, scale=0.5).then_inc(folded_ready, 1)
            act.wait_ge(folded_ready, 1)


def butterfly_ffn(nc, tag, T, x_res, mean, rstd, cst, folded):
    NT, G = T // P, T // GW
    w_up, b_up, w_down, b_down = (folded[n] for n in ("w_up", "b_up", "w_down", "b_down"))
    HK = w_down.shape[1]
    ident = cst["ident"]
    NH = 4
    with ExitStack() as memory:
        ph = Phase(nc, memory, tag)
        xn = [ph.sb(f"xn{p}", [P, GT, D]) for p in range(2)]
        xnT = [ph.sb(f"xnT{p}", [P, DK, GW]) for p in range(2)]
        hT = [ph.sb(f"hT{p}", [P, HK, GW]) for p in range(2)]
        pX, pH, pY = ph.ps("pX", [P, DK, GW]), ph.ps("pH", [P, NH, GW]), ph.ps("pY", [P, 2, 512])
        xn_ready, xT_in_psum, xnT_ready, h_in_psum, h_ready, y_in_psum, y_added, biased = (
            ph.sem(n) for n in ("xn_ready", "xT_in_psum", "xnT_ready", "h_in_psum", "h_ready", "y_in_psum",
                                "y_added", "biased"))
        block = memory.enter_context(nc.Block())

        @block.vector
        def _(dve):
            dve.sem_inc(xn_ready, LEAD)
            dve.sem_inc(y_added, LEAD)
            dve.sem_inc(biased, LEAD)

            def normalise(g, p):
                dve.wait_ge(xT_in_psum, after(g - 2))
                for j in range(GT):
                    t = GT * g + j
                    nc.vector.tensor_scalar(xn[p][:, j:j + 1, :], x_res[:, at(t), :], mean[:, at(t)],
                                            rstd[:, at(t)], ALU.subtract, ALU.mult).then_inc(xn_ready, 1)

            def group(i, p, last_of_all=False):
                g = 2 * i + p
                if not last_of_all:
                    normalise(g + 1, 1 - p)
                for j in range(GT):
                    t = GT * g + j
                    dve.wait_ge(y_in_psum, after(t))
                    nc.vector.tensor_tensor(x_res[:, at(t), :], x_res[:, at(t), :], pY[:, j % 2:j % 2 + 1, 0:D],
                                            ALU.add).then_inc(y_added, 1)
                    dve.wait_ge(y_added, after(t))
                    nc.vector.tensor_tensor(x_res[:, at(t), :], x_res[:, at(t), :], spread(b_down[:], 1, 1),
                                            ALU.add).then_inc(biased, 1)

            normalise(0, 0)
            with dve.Fori(0, G // 2 - 1) as i:
                for p in range(2):
                    group(i, p)
            group(G // 2 - 1, 0)
            group(G // 2 - 1, 1, last_of_all=True)

        def transpose_group(pe, g, p):
            pe.wait_ge(xn_ready, after(GT * g + GT - 1))
            pe.wait_ge(xnT_ready, after(g - 1))
            for j in range(GT):
                for k in range(DK):
                    last = nc.tensor.transpose(pX[:, k, j * P:(j + 1) * P], xn[p][:, j, k * P:(k + 1) * P], ident[:])
            last.then_inc(xT_in_psum, 1)

        @block.tensor
        def _(pe):
            for s in (xT_in_psum, h_in_psum, y_in_psum):
                pe.sem_inc(s, LEAD)
            transpose_group(pe, 0, 0)

            def group(i, p, last_of_all=False):
                g = 2 * i + p
                pe.wait_ge(xnT_ready, after(g))
                for f in range(HK):
                    pe.wait_ge(h_ready, after(HK * g + f - NH))
                    for k in range(DK):
                        last = nc.tensor.matmul(pH[:, f % NH, :], w_up[:, k, f * P:(f + 1) * P], xnT[p][:, k, :],
                                                start=(k == 0), stop=(k == DK - 1))
                    last.then_inc(h_in_psum, 1)
                if not last_of_all:
                    transpose_group(pe, g + 1, 1 - p)
                pe.wait_ge(h_ready, after(HK * g + HK - 1))
                for j in range(GT):
                    pe.wait_ge(y_added, after(GT * g + j - 2))
                    for f in range(HK):
                        last = nc.tensor.matmul(pY[:, j % 2, 0:D], hT[p][:, f, j * P:(j + 1) * P], w_down[:, f, :],
                                                start=(f == 0), stop=(f == HK - 1))
                    last.then_inc(y_in_psum, 1)

            with pe.Fori(0, G // 2 - 1) as i:
                for p in range(2):
                    group(i, p)
            group(G // 2 - 1, 0)
            group(G // 2 - 1, 1, last_of_all=True)

        @block.scalar
        def _(act):
            act.sem_inc(xnT_ready, LEAD)
            act.sem_inc(h_ready, LEAD)

            def copy_xnT(g, p):
                act.wait_ge(xT_in_psum, after(g))
                act.wait_ge(h_in_psum, after(HK * (g - 1) - 1))
                nc.scalar.activation(xnT[p][:], pX[:], ACT.Copy).then_inc(xnT_ready, 1)

            def group(i, p, last_of_all=False):
                g = 2 * i + p
                act.wait_ge(y_in_psum, after(GT * (g - 1) - 1))
                for f in range(HK):
                    act.wait_ge(h_in_psum, after(HK * g + f))
                    nc.scalar.activation(hT[p][:, f, :], pH[:, f % NH, :], ACT.Gelu,
                                         bias=b_up[:, f:f + 1]).then_inc(h_ready, 1)
                if not last_of_all:
                    copy_xnT(g + 1, 1 - p)

            copy_xnT(0, 0)
            with act.Fori(0, G // 2 - 1) as i:
                for p in range(2):
                    group(i, p)
            group(G // 2 - 1, 0)
            group(G // 2 - 1, 1, last_of_all=True)


def linear_attention(nc, tag, T, H, BD, x_res, mean, rstd, cst, qkv_w, qkv_b, out_w, out_b):
    G = T // GW
    HT = P // BD
    VW = BD + 1
    EPS = 1e-6
    ident = cst["ident"]
    NM = 2 * DK
    with ExitStack() as memory:
        ph = Phase(nc, memory, tag)
        wqkv, wout = ph.sb("wqkv", [P, DK, 3 * D]), ph.sb("wout", [P, DK, D])
        b_rows, b_cols, b_cols1 = ph.sb("b_rows", [NM, P]), ph.sb("b_cols", [P, NM]), ph.sb("b_cols1", [P, NM])
        b_value, b_out = ph.sb("b_value", [P, D]), ph.sb("b_out", [P, D])
        xn = [ph.sb(f"xn{p}", [P, GT, D]) for p in range(2)]
        xnT = [ph.sb(f"xnT{p}", [P, DK, GW]) for p in range(2)]
        low = [ph.sb(f"low{m}", [P, GW]) for m in range(2)]
        qk = [ph.sb(f"qk{p}", [P, NM, GW]) for p in range(2)]
        q_of = [ph.sb(f"q_of{p}", [P, DK, 2, GW]) for p in range(2)]
        v1 = [ph.sb(f"v1{p}", [P, H, VW]) for p in range(2)]
        kt = [ph.sb(f"kt{p}", [P, D]) for p in range(2)]
        scores = [ph.sb(f"scores{p}", [P, H, P]) for p in range(2)]
        state, added = ph.sb("state", [P, DK, HT * VW]), ph.sb("added", [P, DK, HT * VW])
        denom = ph.sb("denom", [P, H])
        o = ph.sb("o", [P, H, BD])
        oT = ph.sb("oT", [P, DK, P])
        y = ph.sb("y", [P, D])

        pF = ph.ps("pF", [P, 2, GW])
        pS = ph.ps("pS", [P, 2, GW])
        pV, pC, pU, pO = (ph.ps(n, [P, 512]) for n in ("pV", "pC", "pU", "pO"))

        w_loaded, b_in_psum, bias_ready, setup = (ph.sem(n) for n in ("w_loaded", "b_in_psum", "bias_ready", "setup"))
        xn_ready, xT_in_psum, xnT_ready = (ph.sem(n) for n in ("xn_ready", "xT_in_psum", "xnT_ready"))
        f_in_psum, low_ready, exp_ready, f_ready, q_split = (
            ph.sem(n) for n in ("f_in_psum", "low_ready", "exp_ready", "f_ready", "q_split"))
        vk_in_psum, vk_ready, s_in_psum, s_ready, c_in_psum, u_in_psum = (
            ph.sem(n) for n in ("vk_in_psum", "vk_ready", "s_in_psum", "s_ready", "c_in_psum", "u_in_psum"))
        state_step, denom_step, o_step, oT_in_psum, oT_ready, y_in_psum, y_read, y_added = (
            ph.sem(n) for n in ("state_step", "denom_step", "o_step", "oT_in_psum", "oT_ready", "y_in_psum", "y_read", "y_added"))
        block = memory.enter_context(nc.Block())

        @block.sync
        def _(sp):
            sp.dma_start(wqkv[:], qkv_w.rearrange("(k p) n -> p k n", p=P)).then_inc(w_loaded, 16)
            sp.dma_start(wout[:], out_w.rearrange("(k p) n -> p k n", p=P)).then_inc(w_loaded, 16)
            sp.dma_start(b_rows[:], qkv_b[0:2 * D].rearrange("(m p) -> m p", p=P)).then_inc(w_loaded, 16)
            sp.dma_start(b_value[:], qkv_b[2 * D:3 * D].partition_broadcast(P)).then_inc(w_loaded, 16)
            sp.dma_start(b_out[:], out_b.partition_broadcast(P)).then_inc(w_loaded, 16)

        @block.tensor
        def _(pe):
            for s in (xT_in_psum, f_in_psum, vk_in_psum, s_in_psum, c_in_psum, u_in_psum, oT_in_psum, y_in_psum):
                pe.sem_inc(s, LEAD)
            pe.wait_ge(w_loaded, 16 * 5)
            nc.tensor.transpose(pV[:, 0:NM], b_rows[:], ident[0:NM, 0:NM]).then_inc(b_in_psum, 1)
            pe.wait_ge(bias_ready, 2)
            with pe.Fori(0, G // 2) as i:
                for p in range(2):
                    g = 2 * i + p
                    pe.wait_ge(xn_ready, after(GT * g + GT - 1))
                    pe.wait_ge(f_ready, after(NM * g - 1))
                    for k in range(DK):
                        for j in range(GT):
                            last = nc.tensor.transpose(pF[:, k, j * P:(j + 1) * P], xn[p][:, j, k * P:(k + 1) * P],
                                                       ident[:])
                    last.then_inc(xT_in_psum, 1)
                    pe.wait_ge(xnT_ready, after(g))
                    for m in range(NM):
                        pe.wait_ge(f_ready, after(NM * g + m - 2))
                        for k in range(DK):
                            last = nc.tensor.matmul(pF[:, m % 2, :], wqkv[:, k, m * P:(m + 1) * P], xnT[p][:, k, :],
                                                    start=(k == 0), stop=(k == DK - 1))
                        last.then_inc(f_in_psum, 1)
                    pe.wait_ge(q_split, after(2 * DK * g + 2 * DK - 1))
                    pe.wait_ge(f_ready, after(NM * g + NM - 1))

                    def output(c, j):
                        pe.wait_ge(o_step, after(c))
                        pe.wait_ge(y_read, after(c - 1))
                        for k in range(DK):
                            last = nc.tensor.transpose(pO[:, k * P:(k + 1) * P],
                                                       o[:].rearrange("p h e -> p (h e)")[:, k * P:(k + 1) * P], ident[:])
                        last.then_inc(oT_in_psum, 1)
                        pe.wait_ge(oT_ready, after(c))
                        for k in range(DK):
                            last = nc.tensor.matmul(pO[:, D:2 * D], oT[:, k, :], wout[:, k, :],
                                                    start=(k == 0), stop=(k == DK - 1))
                        last.then_inc(y_in_psum, 1)

                    for j in range(GT):
                        c = GT * g + j
                        b = j % 2
                        chunk = slice(j * P, (j + 1) * P)
                        pe.wait_ge(vk_ready, after(2 * c - 1))
                        for k in range(DK):
                            nc.tensor.matmul(pV[:, 0:D], xnT[p][:, k, chunk], wqkv[:, k, 2 * D:3 * D],
                                             start=(k == 0), stop=(k == DK - 1))
                        for k in range(DK):
                            last = nc.tensor.transpose(pV[:, D + k * P:D + (k + 1) * P], qk[p][:, DK + k, chunk], ident[:])
                        last.then_inc(vk_in_psum, 1)
                        for s in range(H // 4):
                            pe.wait_ge(s_ready, after(H // 4 * c + s - 2))
                            rows = slice(2 * BD * s, 2 * BD * (s + 1))
                            for k in range(DK):
                                last = nc.tensor.matmul(pS[:, s % 2, k * 2 * P:(k + 1) * 2 * P],
                                                        qk[p][rows, DK + k, chunk], q_of[p][rows, k, :, chunk],
                                                        start=True, stop=True)
                            last.then_inc(s_in_psum, 1)
                        if j:
                            output(c - 1, j - 1)
                        pe.wait_ge(state_step, after(2 * c - 1))
                        pe.wait_ge(o_step, after(c - 1))
                        pe.wait_ge(s_ready, after(H // 4 * c + H // 4 - 1))
                        pe.wait_ge(vk_ready, after(2 * c + 1))
                        for k in range(DK):
                            width = HT * VW
                            for h in range(k * HT, (k + 1) * HT):
                                cols = slice(h * VW, (h + 1) * VW)
                                if h == k * HT:
                                    nc.tensor.matmul(pC[:, k * width:(k + 1) * width], qk[p][:, k, chunk],
                                                     state[:, k, :], start=True, stop=False)
                                last = nc.tensor.matmul(pC[:, cols], scores[b][:, h, :], v1[b][:, h, :],
                                                        start=False, stop=(h == (k + 1) * HT - 1))
                        last.then_inc(c_in_psum, 1)
                        pe.wait_ge(state_step, after(2 * c - 2))
                        for k in range(DK):
                            last = nc.tensor.matmul(pU[:, k * HT * VW:(k + 1) * HT * VW], kt[b][:, k * P:(k + 1) * P],
                                                    v1[b][:, k * HT:(k + 1) * HT, :].rearrange("p h e -> p (h e)"),
                                                    start=True, stop=True)
                        last.then_inc(u_in_psum, 1)
                    output(GT * g + GT - 1, GT - 1)

        @block.scalar
        def _(act):
            for s in (xnT_ready, exp_ready, oT_ready):
                act.sem_inc(s, LEAD)
            act.wait_ge(b_in_psum, 1)
            nc.scalar.activation(b_cols[:], pV[:, 0:NM], ACT.Copy).then_inc(bias_ready, 1)
            with act.Fori(0, G // 2) as i:
                for p in range(2):
                    g = 2 * i + p
                    act.wait_ge(xT_in_psum, after(g))
                    act.wait_ge(vk_in_psum, after(GT * (g - 1) - 1))
                    nc.scalar.activation(xnT[p][:], pF[:], ACT.Copy).then_inc(xnT_ready, 1)
                    for m in range(NM):
                        act.wait_ge(low_ready, after(NM * g + m))
                        nc.scalar.activation(low[m % 2][:], low[m % 2][:], ACT.Exp).then_inc(exp_ready, 1)
                    for j in range(GT):
                        c = GT * g + j
                        act.wait_ge(oT_in_psum, after(c))
                        nc.scalar.activation(oT[:], pO[:, 0:D].rearrange("p (k t) -> p k t", k=DK), ACT.Copy
                                             ).then_inc(oT_ready, 1)

        @block.gpsimd
        def _(pool):
            pool.sem_inc(y_added, LEAD)
            with pool.Fori(0, G // 2) as i:
                for p in range(2):
                    for j in range(GT):
                        c = GT * (2 * i + p) + j
                        pool.wait_ge(y_read, after(c))
                        nc.gpsimd.tensor_tensor(x_res[:, at(c), :], x_res[:, at(c), :], spread(y[:], 1, 1), ALU.add
                                                ).then_inc(y_added, 1)

        @block.vector
        def _(dve):
            for s in (xn_ready, low_ready, f_ready, q_split, vk_ready, s_ready, state_step, denom_step, o_step, y_read):
                dve.sem_inc(s, LEAD)
            for b in range(2):
                nc.vector.memset(v1[b][:, :, BD:VW], 1.0).then_inc(setup, 1)
            nc.vector.memset(state[:], 0.0).then_inc(setup, 1)
            dve.wait_ge(bias_ready, 1)
            nc.vector.tensor_scalar(b_cols1[:], b_cols[:], 1.0, None, ALU.add).then_inc(bias_ready, 1)
            dve.wait_ge(bias_ready, 2)
            dve.wait_ge(setup, 3)
            dve.wait_ge(w_loaded, 16 * 5)

            def take_output(dve, c):
                dve.wait_ge(y_in_psum, after(c))
                dve.wait_ge(y_added, after(c - 1))
                nc.vector.tensor_tensor(y[:], pO[:, D:2 * D], b_out[:], ALU.add).then_inc(y_read, 1)

            with dve.Fori(0, G // 2) as i:
                for p in range(2):
                    g = 2 * i + p
                    dve.wait_ge(xT_in_psum, after(g - 2))
                    for j in range(GT):
                        t = GT * g + j
                        nc.vector.tensor_scalar(xn[p][:, j:j + 1, :], x_res[:, at(t), :], mean[:, at(t)],
                                                rstd[:, at(t)], ALU.subtract, ALU.mult).then_inc(xn_ready, 1)
                    dve.wait_ge(c_in_psum, after(GT * (g - 1) - 1))
                    for m in range(NM):
                        dve.wait_ge(f_in_psum, after(NM * g + m))
                        dve.wait_ge(f_ready, after(NM * g + m - 2))
                        nc.vector.tensor_scalar(low[m % 2][:], pF[:, m % 2, :], b_cols[:, m:m + 1], 0.0,
                                                ALU.add, ALU.min).then_inc(low_ready, 1)
                        dve.wait_ge(exp_ready, after(NM * g + m))
                        nc.vector.scalar_tensor_tensor(out=qk[p][:, m, :], in0=pF[:, m % 2, :],
                                                       scalar=b_cols1[:, m:m + 1], in1=low[m % 2][:],
                                                       op0=ALU.add, op1=ALU.max).then_inc(f_ready, 1)
                    dve.wait_ge(f_ready, after(NM * g + DK - 1))
                    for k in range(DK):
                        for odd in range(2):
                            nc.vector.tensor_scalar(q_of[p][:, k, odd, :], qk[p][:, k, :], cst["parity"][:, odd:odd + 1],
                                                    None, ALU.mult).then_inc(q_split, 1)
                    for j in range(GT):
                        c = GT * g + j
                        b = j % 2
                        dve.wait_ge(vk_in_psum, after(c))
                        dve.wait_ge(u_in_psum, after(c - 2))
                        nc.vector.tensor_tensor(v1[b][:, :, 0:BD], pV[:, 0:D].rearrange("p (h e) -> p h e", e=BD),
                                                b_value[:].rearrange("p (h e) -> p h e", e=BD), ALU.add
                                                ).then_inc(vk_ready, 1)
                        nc.vector.tensor_copy(kt[b][:], pV[:, D:2 * D]).then_inc(vk_ready, 1)
                        for s in range(H // 4):
                            dve.wait_ge(s_in_psum, after(H // 4 * c + s))
                            if s == 0:
                                dve.wait_ge(c_in_psum, after(c - 2))
                            nc.vector.tensor_tensor(
                                scores[b][:].rearrange("p (k h) t -> p k h t", k=DK)[:, :, 2 * s:2 * s + 2, :],
                                pS[:, s % 2, :].rearrange("p (k h t) -> p k h t", k=DK, t=P),
                                spread(spread(cst["causal"][:], 1, 2), 1, DK), ALU.mult).then_inc(s_ready, 1)
                        dve.wait_ge(c_in_psum, after(c))
                        dve.wait_ge(oT_in_psum, after(c - 1))
                        ctxv = pC[:, 0:H * VW].rearrange("p (h e) -> p h e", e=VW)
                        nc.vector.tensor_scalar(denom[:], ctxv[:, :, BD], EPS, None, ALU.add).then_inc(denom_step, 1)
                        dve.wait_ge(denom_step, after(2 * c))
                        nc.vector.reciprocal(denom[:], denom[:]).then_inc(denom_step, 1)
                        dve.wait_ge(denom_step, after(2 * c + 1))
                        nc.vector.tensor_tensor(o[:], ctxv[:, :, 0:BD], spread(denom[:], 2, BD), ALU.mult
                                                ).then_inc(o_step, 1)
                        dve.wait_ge(u_in_psum, after(c))
                        nc.vector.tensor_tensor(added[:].rearrange("p k (h e) -> p k h e", e=VW),
                                                pU[:, 0:H * VW].rearrange("p (k h e) -> p k h e", k=DK, e=VW),
                                                spread(cst["head_block"][:], 1, DK), ALU.mult).then_inc(state_step, 1)
                        dve.wait_ge(state_step, after(2 * c))
                        nc.vector.tensor_tensor(state[:], state[:], added[:], ALU.add).then_inc(state_step, 1)
                        if j:
                            take_output(dve, c - 1)
                    take_output(dve, GT * g + GT - 1)


def window_weights(nc, ph, tag, H, BD, cst, a):
    W = a["L1_attn_rel_pos_emb"].shape[0]
    FT = 2 * BD
    HG = P // FT
    NG = H // HG
    HT = P // BD
    res = {"features": ph.sb("features", [P, DK, H * FT]), "offset": ph.sb("offset", [P, W]),
           "reduce": ph.sb("reduce", [P, HG, 2, HG, HG]), "value": ph.sb("value", [P, DK, D]),
           "proj": ph.sb("proj", [P, NG, D]), "half_damage_b": ph.sb("half_damage_b", [P, 1])}
    with ExitStack() as memory:
        t = Phase(nc, memory, tag)
        disp, val_rows = t.sb("disp", [P, DK, D]), t.sb("val_rows", [P, DK, D])
        proj_rows = t.sb("proj_rows", [P, DK, H, FT])
        strain = t.sb("strain", [P, HT, FT])
        place_w, place = t.sb("place_w", [BD, HG, 2, BD]), t.sb("place", [BD, W])
        fused_b, last_w = t.sb("fused_b", [P, 1]), t.sb("last_w", [P, 1])
        reduced = t.sb("reduced", [P, 2, HG])
        pW = t.ps("pW", [P, DK, 512])
        pR = t.ps("pR", [P, 2, 512])
        pP = t.ps("pP", [P, 2, 512])
        pO = t.ps("pO", [P, 512])
        cleared, loaded, made, in_psum = t.sem("cleared"), t.sem("loaded"), t.sem("made"), t.sem("in_psum")
        block = memory.enter_context(nc.Block())

        @block.sync
        def _(sp):
            sp.dma_start(disp[:], a["L1_attn_W_disp"].rearrange("(k p) d -> p k d", p=P)).then_inc(loaded, 16)
            sp.dma_start(val_rows[:], a["L1_attn_W_val"].rearrange("(k p) d -> p k d", p=P)).then_inc(loaded, 16)
            sp.dma_start(res["half_damage_b"][:], a["L1_attn_damage_out_b"].partition_broadcast(P)).then_inc(loaded, 16)
            sp.dma_start(place[:], a["L1_attn_rel_pos_emb"].rearrange("w b -> b w"),
                             allow_slow_non_contiguous=True).then_inc(loaded, 16)
            for h in range(HG):
                sp.dma_start(fused_b[h * FT:(h + 1) * FT, :], a["L1_attn_strain_fused_b"].rearrange("(f a) -> f a", a=1),
                             allow_slow_non_contiguous=True).then_inc(loaded, 16)
                for half, name in ((0, "L1_attn_bond_out_w"), (1, "L1_attn_damage_out_w")):
                    rows = slice(h * FT + half * BD, h * FT + (half + 1) * BD)
                    sp.dma_start(last_w[rows, :], a[name].rearrange("a b -> b a"),
                             allow_slow_non_contiguous=True).then_inc(loaded, 16)
            sp.wait_ge(cleared, 3)
            for h in range(HT):
                sp.dma_start(strain[h * BD:(h + 1) * BD, h, :], a["L1_attn_strain_fused_w"].rearrange("f b -> b f"),
                             allow_slow_non_contiguous=True).then_inc(loaded, 16)
            for h in range(HG):
                sp.dma_start(place_w[:, h, 0, :], a["L1_attn_pos_proj_w"].rearrange("f b -> b f"),
                             allow_slow_non_contiguous=True).then_inc(loaded, 16)
            for k in range(DK):
                sp.dma_start(proj_rows[:, k, :, 0:BD], a["L1_attn_c_proj_w"][k * P:(k + 1) * P, :].rearrange(
                    "p (h e) -> p h e", e=BD)).then_inc(loaded, 16)

        n_loads = 4 + 3 * HG + HT + HG + DK

        @block.vector
        def _(dve):
            nc.vector.memset(strain[:], 0.0).then_inc(cleared, 1)
            nc.vector.memset(place_w[:], 0.0).then_inc(cleared, 1)
            nc.vector.memset(proj_rows[:], 0.0).then_inc(cleared, 1)
            nc.vector.memset(res["reduce"][:], 0.0).then_inc(made, 1)
            dve.wait_ge(loaded, 16 * n_loads)
            own = cst["head_block"][:, :, 0].rearrange("p (h two) -> p two h", two=2)
            nc.vector.tensor_scalar(reduced[:], own, last_w[:], None, ALU.mult).then_inc(made, 1)
            nc.vector.tensor_scalar(res["half_damage_b"][:], res["half_damage_b"][:], 0.5, None, ALU.mult)
            dve.wait_ge(made, 2)
            for k in range(HG):
                nc.vector.tensor_copy(res["reduce"][:, k, :, :, k], reduced[:])
            dve.wait_ge(in_psum, 1)
            nc.vector.tensor_scalar(res["offset"][:], pO[:, 0:W], fused_b[:], None, ALU.add)

        @block.tensor
        def _(pe):
            pe.wait_ge(loaded, 16 * n_loads)
            nc.tensor.matmul(pO[:, 0:W], place_w[:].rearrange("b h two f -> b (h two f)"), place[:],
                             start=True, stop=True).then_inc(in_psum, 1)
            for k in range(DK):
                for m in range(DK):
                    nc.tensor.matmul(pW[:, m, k * HT * FT:(k + 1) * HT * FT], disp[:, k, m * P:(m + 1) * P],
                                     strain[:].rearrange("p h f -> p (h f)"), start=True, stop=True)
                    nc.tensor.transpose(pR[:, 0, m * D + k * P:m * D + (k + 1) * P], val_rows[:, k, m * P:(m + 1) * P],
                                        cst["ident"][:])
                for q in range(NG):
                    last = nc.tensor.transpose(
                        pP[:, q // 2, (q % 2) * D + k * P:(q % 2) * D + (k + 1) * P],
                        proj_rows[:, k, q * HG:(q + 1) * HG, :].rearrange("p h f -> p (h f)"), cst["ident"][:])
            last.then_inc(in_psum, 1)

        @block.scalar
        def _(act):
            act.wait_ge(in_psum, 2)
            nc.scalar.activation(res["features"][:], pW[:], ACT.Copy)
            nc.scalar.activation(res["value"][:].rearrange("p k d -> p (k d)"), pR[:, 0, :], ACT.Copy)
            nc.scalar.activation(res["proj"][:].rearrange("p q d -> p (q d)"),
                                 pP[:].rearrange("p a b -> p (a b)"), ACT.Copy)
    return res


def window_attention(nc, tag, T, H, BD, x_res, mean, rstd, cst, a):
    G = T // GW
    W = a["L1_attn_rel_pos_emb"].shape[0]
    FT = 2 * BD
    HG = P // FT
    NG = H // HG
    KW = HG
    NW = W // KW
    RING = 4
    HP = H // 2
    DVE_TOKENS = 296
    BAND = 2 * P
    PITCH = 3 * P
    LEFT = PITCH // 2
    SOFT, EXPS, PROB, WIDE = 2 * KW, 5 * KW + 3, 6 * KW + 1, W // 2
    COPY_LAG = 3
    ident = cst["ident"]
    band_dram = nc.dram_tensor(f"{tag}_band", [2, P, H, PITCH], F32)
    band = band_dram.ap()
    with ExitStack() as memory:
        ph = Phase(nc, memory, tag)
        wt = window_weights(nc, ph, tag + "_w", H, BD, cst, a)
        xn = ph.sb("xn", [P, GT, D])
        xnT = ph.sb("xnT", [P, DK, GW])
        feat = [ph.sb(f"feat{p}", [P, NG, W + GW]) for p in range(2)]
        val = [ph.sb(f"val{p}", [P, GT, H, FT]) for p in range(2)]
        val_before = ph.sb("val_before", [P, H, FT])
        pair = [ph.sb(f"pair{r}", [P, NG, GW]) for r in range(RING)]
        flat = [ph.sb(f"flat{b}", [P, GW]) for b in range(2)]
        damage = ph.sb("damage", [P, GT, NG, HG * KW])
        logit = [ph.sb(f"logit{p}", [P, GT, NW, H, KW]) for p in range(2)]
        top, total = ph.sb("top", [P, H]), ph.sb("total", [P, H])
        prob = ph.sb("prob", [P, H, W])
        wide = [ph.sb(f"wide{b}", [P, H, BAND]) for b in range(2)]
        wideT = [ph.sb(f"wideT{b}", [P, 2, 2, P]) for b in range(2)]
        oT = ph.sb("oT", [P, NG, P])
        pF, pW, pA = (ph.ps(n, [P, 2, 512]) for n in ("pF", "pW", "pA"))
        pL, pO = ph.ps("pL", [P, GT, P]), ph.ps("pO", [P, NG, P])

        names = ("zeros_ready", "band_zeroed", "setup", "xn_ready", "xT_in_psum", "xnT_ready", "f_in_psum", "f_ready",
                 "halo_ready", "before_ready", "v_in_psum", "v_ready", "diff_dve", "diff_pool", "gelu_ready",
                 "reduced", "flat_ready", "l_in_psum", "tanh_ready", "logit_ready", "soft_step", "exp_ready",
                 "masked", "prob_step", "prob_stored", "a_in_psum", "a_ready", "o_in_psum",
                 "oT_ready", "y_in_psum", "y_added", "pool_turn")
        s = {n: ph.sem(n) for n in names}
        wide_loaded = ph.sems("wide_loaded")
        block = memory.enter_context(nc.Block())

        def all_groups(eng, group):
            group(0, 0, True, False, False)
            group(1, 1, True, True, False)
            with eng.Fori(1, G // 2 - 1) as i:
                for p in range(2):
                    group(2 * i + p, p, True, True, True)
            group(G - 2, 0, True, True, True)
            group(G - 1, 1, True, True, True)
            group(G, 0, False, True, True)
            group(G + 1, 1, False, False, True)

        def head_pair(g, p, step, tail, rest):
            if tail and 0 <= step < GT * HP:
                return g - 1, 1 - p, step // HP, step % HP
            if rest and 0 <= step + W < GT * HP:
                step += W
                return g - 2, p, step // HP, step % HP
            return None

        def tile_done(g, p, step, tail, rest):
            found = head_pair(g, p, step - HP, tail, rest)
            return found[:3] if found and found[3] == 0 else None

        @block.sync
        def _(sp):
            sp.wait_ge(s["zeros_ready"], 1)
            third = H * PITCH // 3
            for b in range(2):
                sp.dma_start(band[b].rearrange("p h w -> p (h w)").rearrange("p (c f) -> p c f", f=third),
                             spread(pair[0][:].rearrange("p g t -> p (g t)")[:, 0:third], 1, 3)
                             ).then_inc(s["band_zeroed"], 16)
            sp.wait_ge(s["band_zeroed"], 32)
            sp.sem_inc(s["prob_stored"], 16)
            for b in range(2):
                sp.sem_inc(wide_loaded[b], 16)
            with sp.Fori(0, T // P // 2) as i:
                for b in range(2):
                    t = 2 * i + b
                    sp.wait_ge(s["prob_step"], after(3 * t + 2))
                    sp.wait_ge(wide_loaded[b], landed(i - 1))
                    sp.dma_start(band[b, :, :, LEFT:LEFT + W], prob[:]).then_inc(s["prob_stored"], 16)
                    sp.wait_ge(s["prob_stored"], landed(t))
                    sp.wait_ge(s["a_in_psum"], after(HP * (t - 1) - 1))
                    skewed = bass.AP(tensor=band_dram, offset=b * P * H * PITCH + LEFT - 1,
                                     ap=[[H * PITCH - 1, P], [PITCH, H], [1, BAND - (P - W)]])
                    sp.dma_start(wide[b][:, :, P - W:BAND], skewed).then_inc(wide_loaded[b], 16)

        @block.tensor
        def _(pe):
            for n in ("xT_in_psum", "f_in_psum", "v_in_psum", "reduced", "l_in_psum", "a_in_psum", "o_in_psum",
                      "y_in_psum"):
                pe.sem_inc(s[n], LEAD)

            def transposes(g):
                pe.wait_ge(s["xn_ready"], after(GT * g + GT - 1))
                pe.wait_ge(s["y_added"], after(GT * (g - 2) - 1))
                pe.wait_ge(s["f_ready"], after(NG * g - 1))
                for k in range(DK):
                    for j in range(GT):
                        last = nc.tensor.transpose(pF[:, k, j * P:(j + 1) * P], xn[:, j, k * P:(k + 1) * P], ident[:])
                last.then_inc(s["xT_in_psum"], 1)

            def features(g, m):
                pe.wait_ge(s["xnT_ready"], after(g))
                pe.wait_ge(s["f_ready"], after(NG * g + m - 2))
                for k in range(DK):
                    last = nc.tensor.matmul(pF[:, m % 2, :], wt["features"][:, k, m * P:(m + 1) * P],
                                            xnT[:, k, :], start=(k == 0), stop=(k == DK - 1))
                last.then_inc(s["f_in_psum"], 1)

            def values(g, j):
                pe.wait_ge(s["v_ready"], after(GT * g + j - 2))
                for k in range(DK):
                    last = nc.tensor.matmul(pA[:, j % 2, 0:D], xnT[:, k, j * P:(j + 1) * P],
                                            wt["value"][:, k, :], start=(k == 0), stop=(k == DK - 1))
                last.then_inc(s["v_in_psum"], 1)

            transposes(0)
            for m in range(NG):
                features(0, m)

            def group(g, p, main, tail, rest):
                for st in range(W):
                    slot, k = divmod(st, KW)
                    b = slot % 2
                    wg = NW * g + slot
                    if main:
                        if k == 0:
                            pe.wait_ge(s["flat_ready"], after(wg - 2))
                        pe.wait_ge(s["gelu_ready"], after(W * g + st))
                        for q in range(NG):
                            last = nc.tensor.matmul(
                                pW[q * FT:(q + 1) * FT, b, :],
                                wt["reduce"][:, k].rearrange("p two h k -> p (two h k)"), pair[st % RING][:, q, :],
                                start=(k == 0), stop=(k == KW - 1))
                        last.then_inc(s["reduced"], 1)
                    if k == 2 and (main or (tail and slot == 0)) and not (isinstance(g, int) and wg == 0):
                        pe.wait_ge(s["flat_ready"], after(wg - 1))
                        pe.wait_ge(s["logit_ready"], after(wg - 2))
                        for j in range(GT):
                            last = nc.tensor.transpose(pL[:, j, :], flat[1 - b][:, j * P:(j + 1) * P], ident[:])
                        last.then_inc(s["l_in_psum"], 1)
                    if main and slot == 1:
                        if k == 0:
                            pe.wait_ge(s["a_ready"], after(HP * GT * (g - 1) - 1))
                        values(g, k)
                    if main and not (isinstance(g, int) and g == G - 1):
                        if st == 2 * KW + 3:
                            transposes(g + 1)
                        if 3 <= slot < 3 + NG and k == 3:
                            features(g + 1, slot - 3)
                    item = head_pair(g, p, st - WIDE - 2, tail, rest)
                    if item:
                        gt, own, j, hp = item
                        t = GT * gt + j
                        pe.wait_ge(s["a_ready"], after(HP * t + hp))
                        if hp == 0:
                            pe.wait_ge(s["oT_ready"], after(t - 1))
                            if j == 0:
                                pe.wait_ge(s["before_ready"], after(gt))
                        before = val[own][:, j - 1] if j else val_before
                        for blk, v in ((0, before), (1, val[own][:, j])):
                            for hh in range(2):
                                h = 2 * hp + hh
                                rows = slice((h % HG) * FT, (h % HG + 1) * FT)
                                last = nc.tensor.matmul(pO[rows, h // HG, :], v[:, h, :], wideT[hp % 2][:, hh, blk, :],
                                                        start=(blk == 0), stop=(blk == 1))
                        if hp == HP - 1:
                            last.then_inc(s["o_in_psum"], 1)
                    item = head_pair(g, p, st - WIDE, tail, rest)
                    if item:
                        gt, _, j, hp = item
                        t = GT * gt + j
                        if hp == 0:
                            pe.wait_ge(wide_loaded[j % 2], landed(GT // 2 * gt + j // 2))
                        pe.wait_ge(s["a_ready"], after(HP * t + hp - 2))
                        if j == 0 and hp == 0:
                            pe.wait_ge(s["v_ready"], after(GT * g + GT - 1) if main else after(GT * G - 1))
                        for hh in range(2):
                            for blk in range(2):
                                last = nc.tensor.transpose(
                                    pA[:, hp % 2, (2 * hh + blk) * P:(2 * hh + blk + 1) * P],
                                    wide[j % 2][:, 2 * hp + hh, blk * P:(blk + 1) * P], ident[:])
                        last.then_inc(s["a_in_psum"], 1)
                    item = tile_done(g, p, st - WIDE - 5, tail, rest)
                    if item:
                        gt, _, j = item
                        t = GT * gt + j
                        pe.wait_ge(s["oT_ready"], after(t))
                        pe.wait_ge(s["y_added"], after(t - 2))
                        for q in range(NG):
                            last = nc.tensor.matmul(pF[:, j % 2, 0:D], oT[:, q, :], wt["proj"][:, q, :],
                                                    start=(q == 0), stop=(q == NG - 1))
                        last.then_inc(s["y_in_psum"], 1)

            all_groups(pe, group)

        @block.scalar
        def _(act):
            for n in ("xnT_ready", "f_ready", "gelu_ready", "tanh_ready", "exp_ready", "oT_ready"):
                act.sem_inc(s[n], LEAD)

            def copy_xnT(g):
                act.wait_ge(s["xT_in_psum"], after(g))
                act.wait_ge(s["v_in_psum"], after(GT * g - 1))
                nc.scalar.activation(xnT[:], pF[:], ACT.Copy).then_inc(s["xnT_ready"], 1)

            def copy_features(g, p, m):
                act.wait_ge(s["f_in_psum"], after(NG * g + m))
                nc.scalar.activation(feat[p][:, m, W:W + GW], pF[:, m % 2, :], ACT.Copy).then_inc(s["f_ready"], 1)

            act.wait_ge(s["setup"], 7)
            copy_xnT(0)
            for m in range(NG):
                copy_features(0, 0, m)

            def group(g, p, main, tail, rest):
                for st in range(W):
                    slot, k = divmod(st, KW)
                    wg = NW * g + slot
                    if main:
                        act.wait_ge(s["diff_dve"], after(W * g + st))
                        act.wait_ge(s["diff_pool"], after(W * g + st))
                        nc.scalar.activation(pair[st % RING][:], pair[st % RING][:], ACT.Gelu,
                                             bias=wt["offset"][:, st:st + 1]).then_inc(s["gelu_ready"], 1)
                    if k == 3 and (main or (tail and slot == 0)) and not (isinstance(g, int) and wg == 0):
                        act.wait_ge(s["l_in_psum"], after(wg - 1))
                        act.wait_ge(s["logit_ready"], after(wg - 2))
                        nc.scalar.activation(damage[:], pL[:].rearrange("p j (q two x) -> p j q two x", q=NG, two=2)[:, :, :, 1, :],
                                             ACT.Tanh, scale=0.5, bias=wt["half_damage_b"][:]).then_inc(s["tanh_ready"], 1)
                    if main and not (isinstance(g, int) and g == G - 1):
                        if st == 3 * KW:
                            copy_xnT(g + 1)
                        if 4 <= slot < 4 + NG and k == 1:
                            copy_features(g + 1, 1 - p, slot - 4)
                    if tail and st == EXPS:
                        for j in range(GT):
                            t = GT * (g - 1) + j
                            act.wait_ge(s["soft_step"], after(2 * t + 1))
                            bond = logit[1 - p][:, j].rearrange("p w h k -> p (w h k)")
                            nc.scalar.activation(bond, bond, ACT.Exp).then_inc(s["exp_ready"], 1)
                    item = tile_done(g, p, st - WIDE - 4, tail, rest)
                    if item:
                        gt, _, j = item
                        t = GT * gt + j
                        act.wait_ge(s["o_in_psum"], after(t))
                        act.wait_ge(s["y_in_psum"], after(t - 1))
                        nc.scalar.activation(oT[:], pO[:], ACT.Copy).then_inc(s["oT_ready"], 1)

            all_groups(act, group)

        @block.gpsimd
        def _(pool):
            for n in ("diff_pool", "masked", "halo_ready", "before_ready"):
                pool.sem_inc(s[n], LEAD)
            pool.wait_ge(s["setup"], 7)

            def halo(g, p):
                pool.wait_ge(s["f_ready"], after(NG * g - 1))
                pool.wait_ge(s["diff_dve"], after(W * (g - 1) - 1))
                pool.sem_inc(s["pool_turn"], 1)
                nc.gpsimd.tensor_copy(feat[p][:, :, 0:W], feat[1 - p][:, :, GW:GW + W]).then_inc(s["halo_ready"], 1)

            halo(0, 0)

            def group(g, p, main, tail, rest):
                if tail:
                    pool.wait_ge(s["v_ready"], after(GT * g - 1))
                    pool.wait_ge(s["a_in_psum"], after(HP * GT * (g - 1) - 1))
                    pool.wait_ge(s["o_in_psum"], after(GT * (g - 2)))
                    pool.sem_inc(s["pool_turn"], 1)
                    nc.gpsimd.tensor_copy(val_before[:], val[p][:, GT - 1]).then_inc(s["before_ready"], 1)
                if main:
                    pool.wait_ge(s["f_ready"], after(NG * g + NG - 1))
                    pool.wait_ge(s["halo_ready"], after(g))
                for st in range(W):
                    if main:
                        pool.wait_ge(s["reduced"], after(W * g + st - RING))
                        nc.gpsimd.tensor_tensor(
                            pair[st % RING][:, :, DVE_TOKENS:GW], feat[p][:, :, st + 1 + DVE_TOKENS:st + 1 + GW],
                            feat[p][:, :, W + DVE_TOKENS:W + GW], ALU.subtract).then_inc(s["diff_pool"], 1)
                    if isinstance(g, int) and g == 1 and st == SOFT:
                        pool.wait_ge(s["logit_ready"], after(NW - 1))
                        first = logit[0][:, 0]
                        nc.gpsimd.affine_select(out=first, in_=first, compare_op=ALU.is_ge, fill=-1e30,
                                                base=-(W - 1), pattern=[[KW, NW], [0, H], [1, KW]],
                                                channel_multiplier=1).then_inc(s["masked"], 1)
                    if main and st == W - 2 * KW and not (isinstance(g, int) and g == G - 1):
                        halo(g + 1, 1 - p)

            all_groups(pool, group)

        @block.vector
        def _(dve):
            nc.vector.memset(pair[0][:], 0.0).then_inc(s["zeros_ready"], 1)
            for p in range(2):
                nc.vector.memset(val[p][:], 0.0).then_inc(s["setup"], 1)
                nc.vector.memset(feat[p][:], 0.0).then_inc(s["setup"], 1)
                nc.vector.memset(wide[p][:, :, 0:P - W], 0.0).then_inc(s["setup"], 1)
            nc.vector.memset(wideT[0][:], 0.0).then_inc(s["setup"], 1)
            for n in ("xn_ready", "v_ready", "diff_dve", "flat_ready", "logit_ready", "soft_step", "prob_step",
                      "a_ready", "y_added"):
                dve.sem_inc(s[n], LEAD)
            dve.wait_ge(s["setup"], 7)
            dve.wait_ge(s["band_zeroed"], 32)

            def normalise(g):
                dve.wait_ge(s["xT_in_psum"], after(g - 1))
                for j in range(GT):
                    t = GT * g + j
                    nc.vector.tensor_scalar(xn[:, j:j + 1, :], x_res[:, at(t), :], mean[:, at(t)],
                                            rstd[:, at(t)], ALU.subtract, ALU.mult).then_inc(s["xn_ready"], 1)

            normalise(0)

            def group(g, p, main, tail, rest):
                if main:
                    dve.wait_ge(s["f_ready"], after(NG * g + NG - 1))
                    dve.wait_ge(s["halo_ready"], after(g))
                for st in range(W):
                    slot, k = divmod(st, KW)
                    b = slot % 2
                    wg = NW * g + slot
                    if main:
                        dve.wait_ge(s["reduced"], after(W * g + st - RING))
                        nc.vector.tensor_tensor(
                            pair[st % RING][:, :, 0:DVE_TOKENS], feat[p][:, :, st + 1:st + 1 + DVE_TOKENS],
                            feat[p][:, :, W:W + DVE_TOKENS], ALU.subtract).then_inc(s["diff_dve"], 1)
                    if k == 2 and (main or (tail and slot < 2)) and not (isinstance(g, int) and wg < 2):
                        own, place = (p, slot - 2) if slot >= 2 else (1 - p, NW - 2 + slot)
                        dve.wait_ge(s["tanh_ready"], after(wg - 2))
                        nc.vector.scalar_tensor_tensor(
                            out=logit[own][:, :, place].rearrange("p j (q h) k -> p j q (h k)", q=NG),
                            in0=damage[:], scalar=-5.0,
                            in1=pL[:].rearrange("p j (q two x) -> p j q two x", q=NG, two=2)[:, :, :, 0, :],
                            op0=ALU.mult, op1=ALU.add).then_inc(s["logit_ready"], 1)
                    if k == 3 and (main or (tail and slot == 0)) and not (isinstance(g, int) and wg == 0):
                        dve.wait_ge(s["reduced"], after(KW * wg - 1))
                        dve.wait_ge(s["l_in_psum"], after(wg - 3))
                        nc.vector.tensor_copy(flat[1 - b][:], pW[:, 1 - b, :]).then_inc(s["flat_ready"], 1)
                    if main and slot == 1:
                        if k == 0:
                            dve.wait_ge(s["o_in_psum"], after(GT * (g - 1) - 1))
                            dve.wait_ge(s["before_ready"], after(g - 1))
                    if main and slot == 2:
                        dve.wait_ge(s["v_in_psum"], after(GT * g + k))
                        nc.vector.tensor_copy(val[p][:, k, :, 0:BD], pA[:, k % 2, 0:D].rearrange("p (h e) -> p h e", e=BD)
                                              ).then_inc(s["v_ready"], 1)
                    if main and st == KW + 3 and not (isinstance(g, int) and g == G - 1):
                        normalise(g + 1)
                    if tail and SOFT <= st < SOFT + GT * KW and k == 1:
                        j = (st - SOFT) // KW
                        t = GT * (g - 1) + j
                        bond = logit[1 - p][:, j]
                        if isinstance(g, int) and t == 0:
                            dve.wait_ge(s["masked"], after(0))
                        dve.wait_ge(s["logit_ready"], after(NW * g - 1))
                        dve.wait_ge(s["soft_step"], after(2 * t - 1))
                        nc.vector.tensor_reduce(top[:], bond.rearrange("p w h k -> p h w k"), AX.XY, ALU.max
                                                ).then_inc(s["soft_step"], 1)
                        dve.wait_ge(s["soft_step"], after(2 * t))
                        nc.vector.tensor_tensor(bond, bond, spread(spread(top[:], 1, NW), 3, KW), ALU.subtract
                                                ).then_inc(s["soft_step"], 1)
                    if tail and PROB <= st < PROB + GT * KW and k == 1:
                        j = (st - PROB) // KW
                        t = GT * (g - 1) + j
                        bond = logit[1 - p][:, j]
                        dve.wait_ge(s["exp_ready"], after(t))
                        dve.wait_ge(s["prob_step"], after(3 * t - 1))
                        nc.vector.tensor_reduce(total[:], bond.rearrange("p w h k -> p h w k"), AX.XY, ALU.add
                                                ).then_inc(s["prob_step"], 1)
                        dve.wait_ge(s["prob_step"], after(3 * t))
                        nc.vector.reciprocal(total[:], total[:]).then_inc(s["prob_step"], 1)
                        dve.wait_ge(s["prob_step"], after(3 * t + 1))
                        dve.wait_ge(s["prob_stored"], landed(t - 1))
                        nc.vector.tensor_tensor(prob[:].rearrange("p h (w k) -> p w h k", k=KW), bond,
                                                spread(spread(total[:], 1, NW), 3, KW), ALU.mult
                                                ).then_inc(s["prob_step"], 1)
                    item = head_pair(g, p, st - WIDE - COPY_LAG, tail, rest)
                    if item:
                        gt, _, j, hp = item
                        t = GT * gt + j
                        dve.wait_ge(s["a_in_psum"], after(HP * t + hp))
                        nc.vector.tensor_copy(wideT[hp % 2][:].rearrange("p h b t -> p (h b t)"), pA[:, hp % 2, :]
                                              ).then_inc(s["a_ready"], 1)
                    item = tile_done(g, p, st - WIDE - 8, tail, rest)
                    if item:
                        gt, _, j = item
                        t = GT * gt + j
                        dve.wait_ge(s["y_in_psum"], after(t))
                        nc.vector.tensor_tensor(x_res[:, at(t), :], x_res[:, at(t), :], pF[:, j % 2:j % 2 + 1, 0:D],
                                                ALU.add).then_inc(s["y_added"], 1)

            all_groups(dve, group)


def macaron_kernel(nc, a, out, upto=6, start=0):
    x_in = a["L0_attn_x"]
    T = x_in.shape[1]
    NT = T // P
    E, _, F = a["L0_ffn_w1"].shape
    C = math.ceil(T * 2 / E * 1.2)
    H, BD = 16, 16
    xe = nc.dram_tensor("xe", [E * C + 2 * T, D], F32).ap()
    ye = nc.dram_tensor("ye", [E * C, D], F32).ap()
    with ExitStack() as program:
        ph = Phase(nc, program, "all")
        x_res = ph.sb("x_res", [P, NT, D])
        mean, rstd = ph.sb("mean", [P, NT]), ph.sb("rstd", [P, NT])
        gather_row, weight = ph.sb("gather_row", [P, NT, 2], I32), ph.sb("weight", [P, NT, 2])
        cst = make_constants(nc, ph, NT, E, C, H, BD)
        x_loaded, x_stored = ph.sem("x_loaded"), ph.sem("x_stored")
        tokens = "a (t p) d -> p (a t) d"
        with nc.Block() as block:
            @block.sync
            def _(sp):
                sp.dma_start(x_res[:], x_in.rearrange(tokens, p=P)).then_inc(x_loaded, 16)
                sp.wait_ge(x_loaded, 16)

        def stats(tag):
            layer_norm_stats(nc, tag, x_res, mean, rstd, cst["neg_half"], NT)

        def experts(tag, first):
            stats(tag + "_ln")
            moe_route(nc, tag + "_route", T, E, C, x_res, mean, rstd, cst, a["L0_ffn_gate_w"],
                      a["L0_ffn_gate_b"], xe, gather_row, weight, first)
            moe_experts(nc, tag + "_experts", E, C, F, xe, ye, cst, a["L0_ffn_w1"], a["L0_ffn_b1"],
                        a["L0_ffn_w2"], a["L0_ffn_b2"])
            moe_combine(nc, tag + "_combine", T, x_res, ye, gather_row, weight)

        if start < 1 <= upto:
            experts("moe0", True)
        if start < 2 <= upto:
            stats("linear_ln")
            linear_attention(nc, "linear", T, H, BD, x_res, mean, rstd, cst, a["L0_attn_qkv_w"],
                             a["L0_attn_qkv_b"], a["L0_attn_out_w"], a["L0_attn_out_b"])
        if start < 3 <= upto:
            experts("moe1", start == 2)

        HID = a["L1_ffn_W_exp"].shape[1]
        shapes = {"w_up": [P, DK, HID], "b_up": [P, HID // P], "w_down": [P, HID // P, D], "b_down": [P, D]}
        stored = {n: nc.dram_tensor(n + "_dram", shape, F32).ap() for n, shape in shapes.items()}

        def move(tag, pairs):
            with ExitStack() as memory:
                moved = Phase(nc, memory, tag).sem("moved")
                with nc.Block() as block:
                    @block.sync
                    def _(sp):
                        for to, source in pairs:
                            sp.dma_start(to, source).then_inc(moved, 16)
                        sp.wait_ge(moved, 16 * len(pairs))

        with ExitStack() as memory:
            fold = Phase(nc, memory, "folded0")
            folded = {n: fold.sb(n, shape) for n, shape in shapes.items()}
            if start < 6 and upto > 3:
                fold_butterflies(nc, "fold", cst, a["L1_ffn_W_exp"], a["L1_ffn_b_exp"],
                                 a["L1_ffn_up_weights"], a["L1_ffn_up_bias"], a["L1_ffn_down_weights"],
                                 a["L1_ffn_W_con"], a["L1_ffn_b_con"], a["L1_ffn_down_bias"], folded)
                move("store_folded", [(stored[n], folded[n][:]) for n in shapes])
            if start < 4 <= upto:
                stats("ffn0_ln")
                butterfly_ffn(nc, "ffn0", T, x_res, mean, rstd, cst, folded)
        if start < 5 <= upto:
            stats("window_ln")
            window_attention(nc, "window", T, H, BD, x_res, mean, rstd, cst, a)
        if start < 6 <= upto:
            with ExitStack() as memory:
                fold = Phase(nc, memory, "folded1")
                folded = {n: fold.sb(n, shape) for n, shape in shapes.items()}
                move("load_folded", [(folded[n][:], stored[n]) for n in shapes])
                stats("ffn1_ln")
                butterfly_ffn(nc, "ffn1", T, x_res, mean, rstd, cst, folded)

        with nc.Block() as block:
            @block.sync
            def _(sp):
                sp.dma_start(out.rearrange(tokens, p=P), x_res[:]).then_inc(x_stored, 16)
                sp.wait_ge(x_stored, 16)


def kernel(**inputs):
    import numpy as _np
    import concourse.bacc as _bacc
    from concourse import mybir as _mybir
    from concourse.bass_utils import run_bass_kernel_spmd as _run

    nc = _bacc.Bacc("TRN2", target_bir_lowering=False, num_devices=1)
    arrays, aps = {}, {}
    for name, value in inputs.items():
        a = _np.ascontiguousarray(value)
        arrays[f"in_{name}_dram"] = a
        aps[name] = nc.dram_tensor(f"in_{name}_dram", a.shape, _mybir.dt.from_np(a.dtype), kind="ExternalInput").ap()
    shape = inputs["L0_attn_x"].shape
    out = nc.dram_tensor("out_0_dram", shape, F32, kind="ExternalOutput").ap()
    macaron_kernel(nc, aps, out)
    r = _run(nc, [arrays], core_ids=[0])
    return r.results[0]["out_0_dram"]
```

```python
import math
from contextlib import ExitStack

import concourse.bass as bass
from concourse import mybir

F32 = mybir.dt.float32
I32 = mybir.dt.int32
F32R = mybir.dt.float32r
ALU = mybir.AluOpType
ACT = mybir.ActivationFunctionType
AX = mybir.AxisListType

P = 128
D = 256
DK = D // P
GT = 4
GW = GT * P
LN_EPS = 1e-5
FLIGHT = 4

LEAD = 128


def after(n):
    return n + 1 + LEAD


def landed(n, dmas=1):
    return 16 * dmas * (n + 2)


def sw_landed(n, dmas=1):
    return 16 * dmas * (n + 1)


def turns(eng, n, body):
    body(0)
    with eng.Fori(1, n) as i:
        body(i)


def at(t, n=1):
    return bass.ds(t, n)


def spread(ap, axis, n):
    shape = list(ap.shape)
    shape.insert(axis, n)
    return ap.unsqueeze(axis).broadcast_to(shape)


def cut_high(dve, high, whole):
    return dve.tensor_copy(high, whole)


def cut_low(eng, low, whole, high):
    return eng.tensor_tensor(low, whole, high.bitcast(F32), ALU.subtract)


def split_matmul(nc, out, left, right, first, last):
    (lh, ll), (rh, rl) = left, right
    nc.tensor.matmul(out, lh, rh, start=first, stop=False)
    nc.tensor.matmul(out, lh, rl, start=False, stop=False)
    return nc.tensor.matmul(out, ll, rh, start=False, stop=last)


class Phase:

    def __init__(self, nc, memory, tag):
        self.nc, self.memory, self.tag, self.taken = nc, memory, tag, []
        memory.callback(self.give_back)

    def sb(self, name, shape, dt=F32):
        return self.memory.enter_context(self.nc.sbuf_tensor(f"{self.tag}_{name}", shape, dt))

    def ps(self, name, shape):
        return self.memory.enter_context(self.nc.psum_tensor(f"{self.tag}_{name}", shape, F32))

    def sem(self, name):
        self.taken.append(self.nc.alloc_semaphore(name=f"{self.tag}_{name}"))
        return self.taken[-1]

    def sems(self, name):
        return [self.sem(f"{name}{p}") for p in range(2)]

    def pool_dma_sems(self, name, n=2):
        return [self.nc.alloc_semaphore(name=f"{self.tag}_{name}{p}") for p in range(n)]

    def give_back(self):
        with self.nc.Block() as block:
            @block.gpsimd
            def _(pool):
                for sem in self.taken:
                    pool.sem_clear(sem)
        for sem in self.taken:
            self.nc.release_semaphore(sem)


def chain(eng, sem):
    count = [0]

    def link(ins):
        count[0] += 1
        ins.then_inc(sem, 1)
        eng.wait_ge(sem, count[0])

    return link


def make_constants(nc, ph, NT, E, C, H, BD):
    c = {
        "ident": ph.sb("ident", [P, P]),
        "lower": ph.sb("lower", [P, P]),
        "causal": ph.sb("causal", [P, P]),
        "ones": ph.sb("ones", [P, P]),
        "rev": ph.sb("rev", [P, E]),
        "dump": ph.sb("dump", [P, 2, NT]),
        "keep": ph.sb("keep", [P, E, NT]),
        "head_block": ph.sb("head_block", [P, P // BD, BD + 1]),
        "parity": ph.sb("parity", [P, 2]),
        "neg_half": ph.sb("neg_half", [P, NT]),
    }
    with ExitStack() as memory:
        tmp = Phase(nc, memory, "cst")
        rev_i = tmp.sb("rev_i", [P, E], I32)
        dump_i = tmp.sb("dump_i", [P, 2, NT], I32)
        filled, shaped, ints = tmp.sem("filled"), tmp.sem("shaped"), tmp.sem("ints")
        block = memory.enter_context(nc.Block())

        @block.gpsimd
        def _(pool):
            nc.gpsimd.memset(c["ident"][:], 0.0).then_inc(filled, 1)
            for name in ("lower", "causal", "ones", "head_block"):
                nc.gpsimd.memset(c[name][:], 1.0).then_inc(filled, 1)
            nc.gpsimd.iota(rev_i[:], pattern=[[-1, E]], base=E, channel_multiplier=0).then_inc(ints, 1)
            nc.gpsimd.iota(dump_i[:], pattern=[[1, 2], [2 * P, NT]], base=E * C, channel_multiplier=2).then_inc(ints, 1)
            pool.wait_ge(filled, 5)
            nc.gpsimd.affine_select(out=c["ident"][:], in_=c["ident"][:], compare_op=ALU.not_equal, fill=1.0,
                                    base=0, pattern=[[-1, P]], channel_multiplier=1).then_inc(shaped, 1)
            nc.gpsimd.affine_select(out=c["lower"][:], in_=c["lower"][:], compare_op=ALU.is_gt, fill=0.0,
                                    base=0, pattern=[[1, P]], channel_multiplier=-1).then_inc(shaped, 1)
            nc.gpsimd.affine_select(out=c["causal"][:], in_=c["causal"][:], compare_op=ALU.is_ge, fill=0.0,
                                    base=0, pattern=[[1, P]], channel_multiplier=-1).then_inc(shaped, 1)
            hb = c["head_block"]
            nh = P // BD
            nc.gpsimd.affine_select(out=hb[:], in_=hb[:], compare_op=ALU.is_ge, fill=0.0, base=0,
                                    pattern=[[-BD, nh], [0, BD + 1]], channel_multiplier=1).then_inc(shaped, 1)
            pool.wait_ge(shaped, 4)
            nc.gpsimd.affine_select(out=hb[:], in_=hb[:], compare_op=ALU.is_ge, fill=0.0, base=BD - 1,
                                    pattern=[[BD, nh], [0, BD + 1]], channel_multiplier=-1).then_inc(shaped, 1)

        @block.vector
        def _(dve):
            dve.wait_ge(ints, 2)
            nc.vector.tensor_copy(c["rev"][:], rev_i[:])
            nc.vector.tensor_copy(c["dump"][:], dump_i[:])
            nc.vector.memset(c["keep"][:], 1.0).then_inc(ints, 1)
            nc.vector.memset(c["neg_half"][:], -0.5)
            dve.wait_ge(ints, 3)
            nc.vector.memset(c["keep"][:, :, 0:1], 0.0)
            dve.wait_ge(shaped, 5)
            pairs = c["head_block"][:, :, 0].rearrange("p (h two) -> p two h", two=2)
            nc.vector.reduce_sum(c["parity"][:], pairs, AX.X)
    return c


def token_stats(nc, stats, x_res, t):
    return nc.vector.bn_stats(stats[:, at(t), :].rearrange("p a s -> p (a s)"),
                              x_res[:, at(t), :].rearrange("p a d -> p (a d)"))


def layer_norm_stats(nc, tag, x_res, stats, mean, rstd, neg_half, NT, taken, moves=(), x_in=None):
    with ExitStack() as memory:
        ph = Phase(nc, memory, tag)
        msum, mdif, m2, var = (ph.sb(n, [P, NT]) for n in ("msum", "mdif", "m2", "var"))
        stats_done, moments, rstd_ready = ph.sem("stats_done"), ph.sem("moments"), ph.sem("rstd_ready")
        moved = ph.sem("moved")
        group_loaded = [ph.sem(f"group_loaded{g}") for g in range(NT // GT)] if x_in is not None else []
        block = memory.enter_context(nc.Block())

        @block.sync
        def _(sp):
            for g, sem in enumerate(group_loaded):
                sp.dma_start(x_res[:, g * GT:(g + 1) * GT, :], x_in[:, g * GW:(g + 1) * GW, :].rearrange(
                    "a (t p) d -> p (a t) d", p=P)).then_inc(sem, 16)
            for to, source in moves:
                sp.dma_start(to, source).then_inc(moved, 16)
            if moves:
                sp.wait_ge(moved, 16 * len(moves))

        @block.vector
        def _(dve):
            for g, sem in enumerate(group_loaded):
                dve.wait_ge(sem, 16)
                for j in range(GT):
                    token_stats(nc, stats, x_res, g * GT + j).then_inc(stats_done, 1)
            if not taken and not group_loaded:
                with dve.Fori(0, NT // 4) as i:
                    for j in range(4):
                        token_stats(nc, stats, x_res, 4 * i + j).then_inc(stats_done, 1)
            if not taken:
                dve.wait_ge(stats_done, NT)
            even, odd = stats[:, :, 1], stats[:, :, 4]
            nc.vector.tensor_tensor(msum[:], even, odd, ALU.add).then_inc(moments, 1)
            nc.vector.tensor_tensor(mdif[:], even, odd, ALU.subtract).then_inc(moments, 1)
            nc.vector.tensor_tensor(m2[:], stats[:, :, 2], stats[:, :, 5], ALU.add).then_inc(moments, 1)
            dve.wait_ge(moments, 3)
            nc.vector.tensor_scalar(mean[:], msum[:], 0.5, None, ALU.mult).then_inc(moments, 1)
            nc.vector.tensor_tensor(mdif[:], mdif[:], mdif[:], ALU.mult).then_inc(moments, 1)
            nc.vector.tensor_scalar(m2[:], m2[:], 1.0 / D, LN_EPS, ALU.mult, ALU.add).then_inc(moments, 1)
            dve.wait_ge(moments, 6)
            nc.vector.scalar_tensor_tensor(out=var[:], in0=mdif[:], scalar=0.25, in1=m2[:],
                                           op0=ALU.mult, op1=ALU.add).then_inc(moments, 1)

        @block.gpsimd
        def _(pool):
            pool.wait_ge(moments, 7)
            nc.gpsimd.tensor_tensor(rstd[:], var[:], neg_half[:], ALU.pow).then_inc(rstd_ready, 1)
            pool.wait_ge(rstd_ready, 1)


def moe_route(nc, tag, T, E, C, x_res, mean, rstd, cst, gate_w, gate_b, xe, gather_row, weight,
              first):
    NT, G = T // P, T // GW
    ident = cst["ident"]
    with ExitStack() as memory:
        ph = Phase(nc, memory, tag)
        gw, gb = ph.sb("gw", [P, DK, E]), ph.sb("gb", [P, E])
        xn = [ph.sb(f"xn{p}", [P, GT, D]) for p in range(2)]
        xnT = [ph.sb(f"xnT{p}", [P, DK, GW]) for p in range(2)]
        logits, work, work2 = (ph.sb(n, [P, NT, E]) for n in ("logits", "work", "work2"))
        hot = [ph.sb(f"hot{k}", [P, NT, E]) for k in range(2)]
        best, rank, place, first_row, valid, row, share = (
            [ph.sb(f"{n}{k}", [P, NT]) for k in range(2)]
            for n in ("best", "rank", "place", "first_row", "valid", "row", "share"))
        totals, scan = ph.sb("totals", [P, E, NT]), ph.sb("scan", [P, E, NT])
        scatter_row = ph.sb("scatter_row", [P, NT, 2], I32)
        stage_row = [ph.sb(f"stage_row{p}", [P, 2], I32) for p in range(FLIGHT)]
        stage_x = [ph.sb(f"stage_x{p}", [P, D]) for p in range(FLIGHT)]
        ZW = 2048
        zeros = ph.sb("zeros", [P, ZW]) if first else None
        pT = [ph.ps(f"pT{p}", [P, DK, GW]) for p in range(2)]
        pL = [ph.ps(f"pL{p}", [P, GT, E]) for p in range(2)]

        gate_loaded, zeros_ready, zeroed = ph.sem("gate_loaded"), ph.sem("zeros_ready"), ph.sem("zeroed")
        xn_ready, xT_in_psum, xnT_ready, logits_in_psum, logits_ready = (
            ph.sem(n) for n in ("xn_ready", "xT_in_psum", "xnT_ready", "logits_in_psum", "logits_ready"))
        step, gap_ready, ratio_ready, hot_ready, counts_in_psum = (
            ph.sem(n) for n in ("step", "gap_ready", "ratio_ready", "hot_ready", "counts_in_psum"))
        staged, scattered, turn = ph.sem("staged"), ph.pool_dma_sems("scattered", FLIGHT), ph.sem("turn")
        block = memory.enter_context(nc.Block())

        @block.sync
        def _(sp):
            sp.dma_start(gw[:], gate_w.rearrange("(k p) e -> p k e", p=P)).then_inc(gate_loaded, 16)
            sp.dma_start(gb[:], gate_b.partition_broadcast(P)).then_inc(gate_loaded, 16)
            if first:
                sp.wait_ge(zeros_ready, 1)
                flat = xe[0:E * C, :].rearrange("r d -> (r d)")
                whole, rest = divmod(E * C * D, P * ZW)
                for z in range(whole):
                    sp.dma_start(flat[z * P * ZW:(z + 1) * P * ZW].rearrange("(p f) -> p f", p=P),
                                 zeros[:]).then_inc(zeroed, 16)
                sp.dma_start(flat[whole * P * ZW:].rearrange("(p f) -> p f", p=P),
                             zeros[:, 0:rest // P]).then_inc(zeroed, 16)
                sp.wait_ge(zeroed, 16 * (whole + 1))

        @block.vector
        def _(dve):
            dve.sem_inc(xn_ready, LEAD)
            dve.sem_inc(logits_ready, LEAD)
            dve.sem_inc(staged, LEAD)
            if first:
                nc.vector.memset(zeros[:], 0.0).then_inc(zeros_ready, 1)
            dve.wait_ge(gate_loaded, 32)

            def normalise(g, p):
                dve.wait_ge(xT_in_psum, after(g - 2))
                for j in range(GT):
                    t = GT * g + j
                    nc.vector.tensor_scalar(xn[p][:, j:j + 1, :], x_res[:, at(t), :], mean[:, at(t)],
                                            rstd[:, at(t)], ALU.subtract, ALU.mult).then_inc(xn_ready, 1)

            def group(g, p, last_of_all=False):
                if not last_of_all:
                    normalise(g + 1, 1 - p)
                dve.wait_ge(logits_in_psum, after(g))
                nc.vector.tensor_tensor(logits[:, at(GT * g, GT), :], pL[p][:], spread(gb[:], 1, GT),
                                        ALU.add).then_inc(logits_ready, 1)

            normalise(0, 0)
            with dve.Fori(0, G // 2 - 1) as i:
                for p in range(2):
                    group(2 * i + p, p)
            group(G - 2, 0)
            group(G - 1, 1, last_of_all=True)
            dve.wait_ge(logits_ready, after(G - 1))

            link = chain(dve, step)
            rev = spread(cst["rev"][:], 1, NT)
            for k, src in ((0, logits), (1, work2)):
                link(nc.vector.reduce_max(best[k][:], src[:], AX.X))
                link(nc.vector.tensor_tensor(work[:], src[:], spread(best[k][:], 2, E), ALU.is_equal))
                link(nc.vector.tensor_tensor(work[:], work[:], rev, ALU.mult))
                link(nc.vector.reduce_max(rank[k][:], work[:], AX.X))
                link(nc.vector.tensor_tensor(hot[k][:], rev, spread(rank[k][:], 2, E), ALU.is_equal))
                if k == 0:
                    link(nc.vector.scalar_tensor_tensor(out=work2[:], in0=hot[0][:], scalar=-1e38, in1=src[:],
                                                        op0=ALU.mult, op1=ALU.add))
            nc.vector.tensor_tensor(work[:], hot[0][:], hot[1][:], ALU.add).then_inc(hot_ready, 1)
            link(nc.vector.tensor_tensor(share[1][:], best[1][:], best[0][:], ALU.subtract))
            dve.sem_inc(gap_ready, 1)
            dve.wait_ge(ratio_ready, 1)
            link(nc.vector.tensor_scalar(share[0][:], valid[0][:], 1.0, None, ALU.add))
            link(nc.vector.reciprocal(share[0][:], share[0][:]))
            link(nc.vector.tensor_tensor(share[1][:], valid[0][:], share[0][:], ALU.mult))

            dve.wait_ge(counts_in_psum, 1)
            link(nc.vector.tensor_copy(totals[:], pT_view(pT[1], NT, E).rearrange("p t e -> p e t")))
            link(nc.vector.tensor_tensor_scan(scan[:].rearrange("p e t -> p (e t)"),
                                              cst["keep"][:].rearrange("p e t -> p (e t)"),
                                              totals[:].rearrange("p e t -> p (e t)"), 0.0, ALU.mult, ALU.add))
            link(nc.vector.tensor_tensor(totals[:], scan[:], totals[:], ALU.subtract))
            link(nc.vector.tensor_tensor(work2[:], pT_view(pT[0], NT, E), totals[:].rearrange("p e t -> p t e"),
                                         ALU.add))
            for k in range(2):
                link(nc.vector.tensor_tensor(work[:], work2[:], hot[k][:], ALU.mult))
                link(nc.vector.reduce_sum(place[k][:], work[:], AX.X))
                link(nc.vector.tensor_scalar(first_row[k][:], rank[k][:], -float(C), float(E * C), ALU.mult, ALU.add))
                link(nc.vector.tensor_scalar(valid[k][:], place[k][:], float(C), None, ALU.is_lt))
                link(nc.vector.scalar_tensor_tensor(out=gather_row[:, :, k], in0=place[k][:], scalar=float(C - 1),
                                                    in1=first_row[k][:], op0=ALU.min, op1=ALU.add))
                link(nc.vector.tensor_tensor(row[k][:], place[k][:], first_row[k][:], ALU.add))
                link(nc.vector.tensor_tensor(row[k][:], row[k][:], cst["dump"][:, k, :], ALU.subtract))
                link(nc.vector.tensor_tensor(row[k][:], row[k][:], valid[k][:], ALU.mult))
                link(nc.vector.tensor_tensor(scatter_row[:, :, k], row[k][:], cst["dump"][:, k, :], ALU.add))
                link(nc.vector.scalar_tensor_tensor(out=weight[:, :, k], in0=share[k][:], scalar=0.5,
                                                    in1=valid[k][:], op0=ALU.mult, op1=ALU.mult))
            def stage(i):
                for p in range(FLIGHT):
                    t = FLIGHT * i + p
                    if not (isinstance(i, int) and i == 0):
                        dve.wait_ge(scattered[p], sw_landed(i - 1, 2))
                    nc.vector.tensor_copy(stage_row[p][:], scatter_row[:, at(t), :].rearrange("p a k -> p (a k)")
                                          ).then_inc(staged, 1)
                    nc.vector.tensor_scalar(stage_x[p][:], x_res[:, at(t), :].rearrange("p a d -> p (a d)"),
                                            mean[:, at(t)], rstd[:, at(t)], ALU.subtract,
                                            ALU.mult).then_inc(staged, 1)

            turns(dve, NT // FLIGHT, stage)

        @block.scalar
        def _(act):
            act.sem_inc(xnT_ready, LEAD)
            with act.Fori(0, G // 2) as i:
                for p in range(2):
                    g = 2 * i + p
                    act.wait_ge(xT_in_psum, after(g))
                    act.wait_ge(logits_in_psum, after(g - 2))
                    nc.scalar.activation(xnT[p][:], pT[p][:], ACT.Copy).then_inc(xnT_ready, 1)
            act.wait_ge(gap_ready, 1)
            nc.scalar.activation(valid[0][:], share[1][:], ACT.Exp).then_inc(ratio_ready, 1)

        @block.tensor
        def _(pe):
            pe.sem_inc(xT_in_psum, LEAD)
            pe.sem_inc(logits_in_psum, LEAD)
            pe.wait_ge(gate_loaded, 32)

            def transposes(g, p):
                pe.wait_ge(xn_ready, after(GT * g + GT - 1))
                pe.wait_ge(xnT_ready, after(g - 2))
                for j in range(GT):
                    for k in range(DK):
                        last = nc.tensor.transpose(pT[p][:, k, j * P:(j + 1) * P],
                                                   xn[p][:, j, k * P:(k + 1) * P], ident[:])
                last.then_inc(xT_in_psum, 1)

            def group(g, p, last_of_all=False):
                if not last_of_all:
                    transposes(g + 1, 1 - p)
                pe.wait_ge(xnT_ready, after(g))
                pe.wait_ge(logits_ready, after(g - 2))
                for j in range(GT):
                    for k in range(DK):
                        last = nc.tensor.matmul(pL[p][:, j, :], xnT[p][:, k, j * P:(j + 1) * P], gw[:, k, :],
                                                start=(k == 0), stop=(k == DK - 1))
                last.then_inc(logits_in_psum, 1)

            transposes(0, 0)
            with pe.Fori(0, G // 2 - 1) as i:
                for p in range(2):
                    group(2 * i + p, p)
            group(G - 2, 0)
            group(G - 1, 1, last_of_all=True)
            pe.wait_ge(hot_ready, 1)
            for m, src in ((0, cst["lower"]), (1, cst["ones"])):
                for h in range(NT * E // 512):
                    last = nc.tensor.matmul(pT_view(pT[m], NT, E)[:, h * 512 // E:(h + 1) * 512 // E, :], src[:],
                                            work[:, h * 512 // E:(h + 1) * 512 // E, :], start=True, stop=True)
            last.then_inc(counts_in_psum, 1)

        @block.gpsimd
        def _(pool):
            if first:
                pool.wait_ge(zeroed, 16 * (math.ceil(E * C * D / (P * ZW))))
            with pool.Fori(0, NT // FLIGHT) as i:
                for p in range(FLIGHT):
                    t = FLIGHT * i + p
                    pool.wait_ge(staged, after(2 * t + 1))
                    pool.sem_inc(turn, 1)
                    for k in range(2):
                        pool.indirect_dma_start(
                            out=xe, out_offset=bass.IndirectOffsetOnAxis(ap=stage_row[p][:, k:k + 1], axis=0),
                            in_=stage_x[p][:], in_offset=None).then_inc(scattered[p], 16)
            for p in range(FLIGHT):
                pool.wait_ge(scattered[p], sw_landed(NT // FLIGHT - 1, 2))


def pT_view(bank_pair, NT, E):
    return bank_pair[:].rearrange("p a b -> p (a b)").rearrange("p (t e) -> p t e", e=E)


def moe_experts(nc, tag, E, C, F, xe, ye, cst, w1, b1, w2, b2):
    ident = cst["ident"]
    FK = F // P
    tiles = [(j * P, min(P, C - j * P)) for j in range(math.ceil(C / P))]
    NJ = len(tiles)
    whole = C // P
    with ExitStack() as memory:
        ph = Phase(nc, memory, tag)
        w1s, w2s = ph.sb("w1s", [P, DK, F]), ph.sb("w2s", [P, FK, D])
        NR = 4
        h = ph.sb("h", [P, NR, C])
        w1h, w1l = ([ph.sb(f"w1{n}{p}", [P, DK, F], F32R) for p in range(2)] for n in "hl")
        w2h, w2l = ([ph.sb(f"w2{n}{p}", [P, FK, D], F32R) for p in range(2)] for n in "hl")
        xTh, xTl = ([ph.sb(f"xT{n}{p}", [P, DK, C], F32R) for p in range(2)] for n in "hl")
        hTh, hTl = ([ph.sb(f"hT{n}{p}", [P, FK, C], F32R) for p in range(2)] for n in "hl")
        CUTS = FK + 2
        b2s = [ph.sb(f"b2s{p}", [P, D]) for p in range(2)]
        b1r, b1T = ph.sb("b1r", [E, F]), ph.sb("b1T", [P, FK, E])
        xr = [ph.sb(f"xr{p}", [P, NJ, D]) for p in range(2)]
        yo = [ph.sb(f"yo{p}", [P, NJ, D]) for p in range(2)]
        pX = ph.ps("pX", [P, DK, 512])
        NH = 4
        pH = ph.ps("pH", [P, NH, 512])
        pY = ph.ps("pY", [P, DK, 512])
        yT = ph.sb("yT", [P, DK, C])
        y_rows = pX[:].rearrange("p k c -> p (k c)")

        b1_loaded, b1_in_psum, b1_ready = ph.sem("b1_loaded"), ph.sem("b1_in_psum"), ph.sem("b1_ready")
        w1_loaded, w2_loaded = ph.sem("w1_loaded"), ph.sem("w2_loaded")
        b2_loaded, x_loaded = ph.sems("b2_loaded"), ph.sems("x_loaded")
        stored = ph.pool_dma_sems("stored")
        xT_in_psum, xT_ready, h_in_psum, h_ready, y_in_psum, y_ready = (
            ph.sem(n) for n in ("xT_in_psum", "xT_ready", "h_in_psum", "h_ready", "y_in_psum", "y_ready"))
        yT_ready, yr_in_psum = ph.sem("yT_ready"), ph.sem("yr_in_psum")
        high_cut, w1_split, w2_split, x_split, h_split = (
            ph.sem(n) for n in ("high_cut", "w1_split", "w2_split", "x_split", "h_split"))
        block = memory.enter_context(nc.Block())

        @block.sync
        def _(sp):
            for s in (w1_loaded, w2_loaded, *b2_loaded):
                sp.sem_inc(s, 16)
            for p in range(2):
                sp.sem_inc(x_loaded[p], 32)
            sp.dma_start(b1r[:], b1).then_inc(b1_loaded, 16)
            with sp.Fori(0, E // 2) as i:
                for p in range(2):
                    e = 2 * i + p
                    sp.wait_ge(xT_in_psum, after(e - 2))
                    sp.dma_start(xr[p][:, 0:whole, :],
                                 xe[at(e * C, whole * P), :].rearrange("(j q) d -> q j d", q=P)
                                 ).then_inc(x_loaded[p], 16)
                    sp.dma_start(xr[p][0:C - whole * P, whole, :], xe[at(e * C + whole * P, C - whole * P), :]
                                 ).then_inc(x_loaded[p], 16)
                    sp.wait_ge(w1_split, after(e - 1))
                    sp.dma_start(w1s[:], w1[at(e), :, :].rearrange("a (k q) f -> q (a k) f", q=P)
                                 ).then_inc(w1_loaded, 16)
                    sp.wait_ge(w2_split, after(e - 1))
                    sp.dma_start(w2s[:], w2[at(e), :, :].rearrange("a (k q) d -> q (a k) d", q=P)
                                 ).then_inc(w2_loaded, 16)
                    sp.wait_ge(y_ready, after(NJ * (e - 1) - 1))
                    sp.dma_start(b2s[p][:], b2[at(e), :].rearrange("a d -> (a d)").partition_broadcast(P)
                                 ).then_inc(b2_loaded[p], 16)

        def transpose_queue(pe, e, i, p):
            pe.wait_ge(x_loaded[p], landed(i, 2))
            pe.wait_ge(x_split, after(e - 1))
            pe.wait_ge(y_ready, after(NJ * (e - 1) - 1))
            for j, (at_row, n) in enumerate(tiles):
                for k in range(DK):
                    last = nc.tensor.transpose(pX[:, k, at_row:at_row + n], xr[p][0:n, j, k * P:(k + 1) * P],
                                               ident[0:n, 0:n])
            last.then_inc(xT_in_psum, 1)

        @block.tensor
        def _(pe):
            for s in (xT_in_psum, h_in_psum, y_in_psum, yr_in_psum):
                pe.sem_inc(s, LEAD)
            pe.wait_ge(b1_loaded, 16)
            for f in range(FK):
                last = nc.tensor.transpose(pH[:, 0, f * E:(f + 1) * E], b1r[:, f * P:(f + 1) * P], ident[0:E, 0:E])
            last.then_inc(b1_in_psum, 1)
            transpose_queue(pe, 0, 0, 0)
            pe.wait_ge(b1_ready, 1)

            def transpose_back(e, last_of_all=False):
                pe.wait_ge(yT_ready, after(DK * e + DK - 1))
                pe.wait_ge(x_split, after(e if last_of_all else e + 1))
                for j, (at_row, n) in enumerate(tiles):
                    for m in range(DK):
                        last = nc.tensor.transpose(y_rows[0:n, j * D + m * P:j * D + (m + 1) * P],
                                                   yT[:, m, at_row:at_row + n], ident[:])
                last.then_inc(yr_in_psum, 1)

            def expert(i, p, last_of_all=False):
                e = 2 * i + p
                pe.wait_ge(w1_split, after(e))
                pe.wait_ge(x_split, after(e))
                for f in range(FK):
                    pe.wait_ge(h_ready, after(FK * e + f - NH))
                    cols = slice(f * P, (f + 1) * P)
                    for k in range(DK):
                        last = split_matmul(nc, pH[:, f % NH, 0:C], (w1h[p][:, k, cols], w1l[p][:, k, cols]),
                                            (xTh[p][:, k, :], xTl[p][:, k, :]), k == 0, k == DK - 1)
                    last.then_inc(h_in_psum, 1)
                    if f == 2 and not (isinstance(e, int) and e == 0):
                        transpose_back(e - 1)
                if not last_of_all:
                    transpose_queue(pe, e + 1, i + p, 1 - p)
                pe.wait_ge(w2_split, after(e))
                for m in range(DK):
                    pe.wait_ge(yT_ready, after(DK * (e - 1) + m))
                    cols = slice(m * P, (m + 1) * P)
                    for f in range(FK):
                        if m == 0:
                            pe.wait_ge(h_split, after(FK * e + f))
                        last = split_matmul(nc, pY[:, m, 0:C], (w2h[p][:, f, cols], w2l[p][:, f, cols]),
                                            (hTh[p][:, f, :], hTl[p][:, f, :]), f == 0, f == FK - 1)
                    last.then_inc(y_in_psum, 1)

            expert(0, 0)
            expert(0, 1)
            with pe.Fori(1, E // 2 - 1) as i:
                for p in range(2):
                    expert(i, p)
            expert(E // 2 - 1, 0)
            expert(E // 2 - 1, 1, last_of_all=True)
            transpose_back(E - 1, last_of_all=True)

        @block.scalar
        def _(act):
            act.sem_inc(xT_ready, LEAD)
            act.sem_inc(h_ready, LEAD)
            act.sem_inc(yT_ready, LEAD)
            act.wait_ge(b1_in_psum, 1)
            nc.scalar.activation(b1T[:], pH[:, 0, 0:FK * E].rearrange("p (f e) -> p f e", e=E), ACT.Copy
                                 ).then_inc(b1_ready, 1)

            def copy_xT(e, p):
                act.wait_ge(xT_in_psum, after(e))
                act.wait_ge(h_in_psum, after(FK * (e - 1) - 1))
                nc.scalar.activation(xTh[p][:], pX[:, :, 0:C], ACT.Copy).then_inc(xT_ready, 1)

            copy_xT(0, 0)
            act.wait_ge(b1_ready, 1)

            def expert(i, p, last_of_all=False):
                e = 2 * i + p
                for f in range(FK):
                    act.wait_ge(h_in_psum, after(FK * e + f))
                    act.wait_ge(h_split, after(FK * e + f - NR))
                    nc.scalar.activation(h[:, f % NR, :], pH[:, f % NH, 0:C], ACT.Gelu,
                                         bias=b1T[:, f, at(e)]).then_inc(h_ready, 1)
                if not last_of_all:
                    copy_xT(e + 1, 1 - p)
                for m in range(DK):
                    act.wait_ge(y_in_psum, after(DK * e + m))
                    act.wait_ge(yr_in_psum, after(e - 1))
                    nc.scalar.activation(yT[:, m, :], pY[:, m, 0:C], ACT.Copy).then_inc(yT_ready, 1)

            with act.Fori(0, E // 2 - 1) as i:
                for p in range(2):
                    expert(i, p)
            expert(E // 2 - 1, 0)
            expert(E // 2 - 1, 1, last_of_all=True)

        @block.vector
        def _(dve):
            for s in (y_ready, high_cut, w1_split, x_split, h_split):
                dve.sem_inc(s, LEAD)

            def split(high, low, whole, cut, done):
                cut_high(nc.vector, high, whole).then_inc(high_cut, 1)
                dve.wait_ge(high_cut, after(cut))
                cut_low(nc.vector, low, whole, high).then_inc(done, 1)

            def split_w1(e, p):
                dve.wait_ge(w1_loaded, landed(e))
                dve.wait_ge(h_in_psum, after(FK * (e - 1) - 1))
                split(w1h[p][:], w1l[p][:], w1s[:], CUTS * e, w1_split)

            def split_x(e, p):
                dve.wait_ge(xT_ready, after(e))
                cut_low(nc.vector, xTl[p][:], pX[:, :, 0:C], xTh[p][:]).then_inc(x_split, 1)

            def cut_w2(e, p):
                dve.wait_ge(w2_loaded, landed(e))
                dve.wait_ge(y_in_psum, after(DK * (e - 1) - 1))
                cut_high(nc.vector, w2h[p][:], w2s[:]).then_inc(high_cut, 1)

            split_w1(0, 0)
            split_x(0, 0)
            cut_w2(0, 0)

            def take_y(i, p):
                e = 2 * i + p
                dve.wait_ge(b2_loaded[p], landed(i))
                if not (isinstance(i, int) and i == 0):
                    dve.wait_ge(stored[p], sw_landed(i - 1, 2))
                dve.wait_ge(yr_in_psum, after(e))
                for j, (_, n) in enumerate(tiles):
                    nc.vector.tensor_tensor(yo[p][0:n, j, :], y_rows[0:n, j * D:(j + 1) * D], b2s[p][0:n, :],
                                            ALU.add).then_inc(y_ready, 1)

            def expert(i, p, last_of_all=False):
                e = 2 * i + p
                for f in range(FK):
                    dve.wait_ge(h_ready, after(FK * e + f))
                    if f == 0:
                        dve.wait_ge(y_in_psum, after(DK * (e - 1) - 1))
                    split(hTh[p][:, f, :], hTl[p][:, f, :], h[:, f % NR, :], CUTS * e + 2 + f, h_split)
                    if f == 3 and not (isinstance(e, int) and e == 0):
                        take_y(i - 1 + p, 1 - p)
                if not last_of_all:
                    split_w1(e + 1, 1 - p)
                    split_x(e + 1, 1 - p)
                    cut_w2(e + 1, 1 - p)

            for i in range(2):
                for p in range(2):
                    expert(i, p)
            with dve.Fori(2, E // 2 - 1) as i:
                for p in range(2):
                    expert(i, p)
            expert(E // 2 - 1, 0)
            expert(E // 2 - 1, 1, last_of_all=True)
            take_y(E // 2 - 1, 1)

        @block.gpsimd
        def _(pool):
            pool.sem_inc(w2_split, LEAD)

            def low_w2(e, p):
                pool.wait_ge(high_cut, after(CUTS * e + 1))
                cut_low(nc.gpsimd, w2l[p][:], w2s[:], w2h[p][:]).then_inc(w2_split, 1)

            def store(e, p):
                pool.wait_ge(y_ready, after(NJ * e + NJ - 1))
                pool.dma_start(ye[at(e * C, whole * P), :].rearrange("(j q) d -> q j d", q=P),
                               yo[p][:, 0:whole, :]).then_inc(stored[p], 16)
                pool.dma_start(ye[at(e * C + whole * P, C - whole * P), :],
                               yo[p][0:C - whole * P, whole, :]).then_inc(stored[p], 16)

            low_w2(0, 0)
            with pool.Fori(0, E // 2 - 1) as i:
                for p in range(2):
                    low_w2(2 * i + p + 1, 1 - p)
                    store(2 * i + p, p)
            low_w2(E - 1, 1)
            store(E - 2, 0)
            store(E - 1, 1)
            for p in range(2):
                pool.wait_ge(stored[p], sw_landed(E // 2 - 1, 2))


def moe_combine(nc, tag, T, x_res, ye, gather_row, weight, stats):
    NT = T // P
    with ExitStack() as memory:
        ph = Phase(nc, memory, tag)
        row = [ph.sb(f"row{p}", [P, 2], I32) for p in range(FLIGHT)]
        got = [ph.sb(f"got{p}", [P, 2, D]) for p in range(FLIGHT)]
        staged, gathered, added, turn = ph.sem("staged"), ph.pool_dma_sems("gathered", FLIGHT), ph.sem("added"), ph.sem("turn")
        block = memory.enter_context(nc.Block())

        @block.scalar
        def _(act):
            act.sem_inc(staged, LEAD)

            def stage(i):
                for p in range(FLIGHT):
                    t = FLIGHT * i + p
                    if not (isinstance(i, int) and i == 0):
                        act.wait_ge(gathered[p], sw_landed(i - 1, 2))
                    nc.scalar.activation(row[p][:], gather_row[:, at(t), :].rearrange("p a k -> p (a k)"), ACT.Copy
                                         ).then_inc(staged, 1)

            turns(act, NT // FLIGHT, stage)

        @block.gpsimd
        def _(pool):
            with pool.Fori(0, NT // FLIGHT) as i:
                for p in range(FLIGHT):
                    t = FLIGHT * i + p
                    pool.wait_ge(staged, after(t))
                    pool.wait_ge(added, after(2 * (t - FLIGHT) + 1))
                    pool.sem_inc(turn, 1)
                    for k in range(2):
                        pool.indirect_dma_start(
                            out=got[p][:, k, :], out_offset=None, in_=ye,
                            in_offset=bass.IndirectOffsetOnAxis(ap=row[p][:, k:k + 1], axis=0)
                        ).then_inc(gathered[p], 16)

        @block.vector
        def _(dve):
            dve.sem_inc(added, LEAD)
            with dve.Fori(0, NT // FLIGHT) as i:
                for p in range(FLIGHT):
                    t = FLIGHT * i + p
                    dve.wait_ge(gathered[p], sw_landed(i, 2))
                    for k in range(2):
                        if k:
                            dve.wait_ge(added, after(2 * t))
                        nc.vector.scalar_tensor_tensor(
                            out=x_res[:, at(t), :], in0=got[p][:, k:k + 1, :],
                            scalar=weight[:, at(t), k:k + 1].rearrange("p a k -> p (a k)"),
                            in1=x_res[:, at(t), :], op0=ALU.mult, op1=ALU.add).then_inc(added, 1)
                    dve.wait_ge(added, after(2 * t + 1))
                    token_stats(nc, stats, x_res, t)


def fold_butterflies(nc, tag, cst, w_exp, b_exp, up_w, up_b, down_w, w_con, b_con, down_b, folded):
    STAGES, PAIRS = up_w.shape[0], up_w.shape[1]
    HID = 2 * PAIRS
    HK = HID // P
    LOW = int(math.log2(P))
    HIGH = STAGES - LOW
    ident = cst["ident"]
    with ExitStack() as memory:
        ph = Phase(nc, memory, tag)
        exp, con = ph.sb("exp", [P, DK, HID]), ph.sb("con", [P, HK, D])
        expT = ph.sb("expT", [P, HK, D])
        bias, bias_cols = ph.sb("bias", [P, HK]), ph.sb("bias_cols", [P, HK, P])
        eye_u, eye_d = ph.sb("eye_u", [P, 1, HID]), ph.sb("eye_d", [P, 1, HID])
        up = ph.sb("up", [P, DK + 1, HID])
        down = ph.sb("down", [P, DK, HID])
        ub = ph.sb("ub", [1, HID])
        bc = [ph.sb(f"bc{k}", [P, D]) for k in range(2)]
        wu = [ph.sb(f"wu{p}", [P, 4 * PAIRS]) for p in range(2)]
        wd = [ph.sb(f"wd{p}", [P, 4 * PAIRS]) for p in range(2)]
        lo_u, hi_u = ph.sb("lo_u", [P, DK + 1, HID]), ph.sb("hi_u", [P, DK + 1, HID])
        lo_d, hi_d = ph.sb("lo_d", [P, DK, HID]), ph.sb("hi_d", [P, DK, HID])
        pD = ph.ps("pD", [P, DK, HID])
        pE = ph.ps("pE", [P, HID])
        pB = ph.ps("pB", [P, HK])
        loaded, up_loaded, down_loaded = ph.sem("loaded"), ph.sems("up_loaded"), ph.sems("down_loaded")
        up_step, down0_step, down1_step = ph.sem("up_step"), ph.sem("down0_step"), ph.sem("down1_step")
        eyes_ready, eye_d_ready, in_psum, psum_read = (
            ph.sem(n) for n in ("eyes_ready", "eye_d_ready", "in_psum", "psum_read"))
        block = memory.enter_context(nc.Block())
        PER = 3
        flat = pD[:].rearrange("p m h -> p (m h)")

        @block.sync
        def _(sp):
            sp.dma_start(con[:], w_con.rearrange("(k p) d -> p k d", p=P)).then_inc(loaded, 16)
            sp.dma_start(bias[:], b_exp.rearrange("(k p) -> p k", p=P), allow_slow_non_contiguous=True
                         ).then_inc(loaded, 16)
            sp.dma_start(ub[:], up_b.rearrange("(a h) -> a h", a=1)).then_inc(loaded, 16)
            sp.dma_start(bc[0][:], b_con.partition_broadcast(P)).then_inc(loaded, 16)
            sp.dma_start(bc[1][:], down_b.partition_broadcast(P)).then_inc(loaded, 16)
            sp.dma_start(exp[:], w_exp.rearrange("(k p) h -> p k h", p=P)).then_inc(loaded, 16)
            for s in range(STAGES):
                if s >= 2:
                    sp.wait_ge(up_step, PER * (s - 1))
                sp.dma_start(wu[s % 2][:], up_w[s].rearrange("n i c -> (n i c)").partition_broadcast(P)
                             ).then_inc(up_loaded[s % 2], 16)
                if s >= 2:
                    if s - 2 < HIGH:
                        sp.wait_ge(down0_step, PER * (s - 1))
                    sp.wait_ge(down1_step, PER * (s - 1))
                sp.dma_start(wd[s % 2][:], down_w[STAGES - 1 - s].rearrange("n i c -> (n i c)").partition_broadcast(P)
                             ).then_inc(down_loaded[s % 2], 16)

        def stage(eng, y, w, lo, hi, s, rows, step, transposed, base):
            stride = 2 ** s
            order = "p (n j c i) -> p c n i j" if transposed else "p (n j i c) -> p c n i j"
            wv = w[:].rearrange(order, j=stride, i=2, c=2)
            for half, product in ((0, lo), (1, hi)):
                for r in range(rows):
                    mine = y[:, r, :].rearrange("p (n two j) -> p two n j", two=2, j=stride)[:, half]
                    ins = eng.tensor_tensor(product[:, r, :].rearrange("p (n i j) -> p n i j", i=2, j=stride),
                                            wv[:, half], spread(mine, 2, 2), ALU.mult)
                ins.then_inc(step, 1)
            eng.wait_ge(step, base + 2)
            eng.tensor_tensor(y, lo, hi, ALU.add).then_inc(step, 1)
            eng.wait_ge(step, base + 3)

        def eye(eng, out):
            return eng.tensor_copy(out[:].rearrange("p a (n j) -> p (a n) j", j=P), spread(ident[:], 1, HK))

        @block.vector
        def _(dve):
            eye(nc.vector, eye_u).then_inc(eyes_ready, 1)
            dve.wait_ge(loaded, 16 * 6)
            nc.vector.tensor_copy(bias_cols[:], spread(bias[:], 2, P)).then_inc(eyes_ready, 1)
            dve.wait_ge(eyes_ready, 2)
            for s in range(STAGES):
                dve.wait_ge(up_loaded[s % 2], 16 * (s // 2 + 1))
                if s < LOW:
                    stage(nc.vector, eye_u[:], wu[s % 2], lo_u[:, 0:1, :], hi_u[:, 0:1, :], s, 1, up_step, False,
                          PER * s)
                else:
                    if s == LOW:
                        dve.wait_ge(psum_read, 4)
                    stage(nc.vector, up[:], wu[s % 2], lo_u[:], hi_u[:], s, DK + 1, up_step, False, PER * s)
                if s < HIGH:
                    dve.wait_ge(psum_read, 1)
                    dve.wait_ge(down_loaded[s % 2], 16 * (s // 2 + 1))
                    stage(nc.vector, down[:, 0:1, :], wd[s % 2], lo_d[:, 0:1, :], hi_d[:, 0:1, :], STAGES - 1 - s, 1,
                          down0_step, True, PER * s)
            nc.vector.tensor_tensor(bc[0][:], bc[0][:], bc[1][:], ALU.add).then_inc(up_step, 1)
            nc.vector.tensor_copy(folded["w_up"][:], up[:, 0:DK, :])
            dve.wait_ge(up_step, PER * STAGES + 1)
            nc.vector.tensor_scalar(folded["b_down"][:], bc[0][:], 0.5, None, ALU.mult)

        @block.gpsimd
        def _(pool):
            eye(nc.gpsimd, eye_d).then_inc(eye_d_ready, 1)
            pool.wait_ge(eye_d_ready, 1)
            pool.wait_ge(psum_read, 1)
            for s in range(STAGES):
                pool.wait_ge(down_loaded[s % 2], 16 * (s // 2 + 1))
                y = down[:, 1:2, :] if s < HIGH else eye_d[:]
                stage(nc.gpsimd, y, wd[s % 2], lo_d[:, 1:2, :], hi_d[:, 1:2, :], STAGES - 1 - s, 1,
                      down1_step, True, PER * s)

        @block.tensor
        def _(pe):
            pe.wait_ge(loaded, 16 * 6)
            for k in range(HK):
                for m in range(DK):
                    last = nc.tensor.transpose(pD[:, m, k * P:(k + 1) * P], con[:, k, m * P:(m + 1) * P], ident[:])
            last.then_inc(in_psum, 1)
            pe.wait_ge(psum_read, 1)
            for k in range(HK):
                for m in range(DK):
                    last = nc.tensor.transpose(flat[:, k * D + m * P:k * D + (m + 1) * P],
                                               exp[:, m, k * P:(k + 1) * P], ident[:])
            last.then_inc(in_psum, 1)
            pe.wait_ge(psum_read, 2)
            pe.wait_ge(up_step, PER * LOW)
            pe.wait_ge(eyes_ready, 2)
            for k in range(HK):
                cols = slice(k * P, (k + 1) * P)
                for m in range(DK):
                    nc.tensor.matmul(pD[:, m, cols], expT[:, k, m * P:(m + 1) * P], eye_u[:, 0, cols],
                                     start=True, stop=True)
                last = nc.tensor.matmul(pE[:, cols], bias_cols[:, k, :], eye_u[:, 0, cols], start=True, stop=True)
            last.then_inc(in_psum, 1)
            pe.wait_ge(psum_read, 4)
            pe.wait_ge(down0_step, PER * HIGH)
            pe.wait_ge(down1_step, PER * HIGH)
            for k in range(HK):
                for m in range(DK):
                    last = nc.tensor.transpose(flat[:, k * D + m * P:k * D + (m + 1) * P],
                                               down[:, m, k * P:(k + 1) * P], ident[:])
            last.then_inc(in_psum, 1)
            pe.wait_ge(up_step, PER * STAGES)
            for k in range(HK):
                cols = slice(k * P, (k + 1) * P)
                nc.tensor.matmul(pB[:, k:k + 1], up[0:1, DK, cols], cst["ones"][0:1, 0:1], start=True, stop=False)
                last = nc.tensor.matmul(pB[:, k:k + 1], ub[0:1, cols], cst["ones"][0:1, 0:1], start=False, stop=True)
            last.then_inc(in_psum, 1)
            pe.wait_ge(psum_read, 5)
            pe.wait_ge(down1_step, PER * STAGES)
            for k in range(HK):
                last = nc.tensor.matmul(flat[:, k * D:(k + 1) * D], eye_d[:, 0, k * P:(k + 1) * P], con[:, k, :],
                                        start=True, stop=True)
            last.then_inc(in_psum, 1)

        @block.scalar
        def _(act):
            def copy(count, out, source, scale=1.0):
                act.wait_ge(in_psum, count)
                nc.scalar.activation(out, source, ACT.Copy, scale=scale).then_inc(psum_read, 1)

            copy(1, down[:], pD[:])
            copy(2, expT[:].rearrange("p k d -> p (k d)"), flat)
            copy(3, up[:, 0:DK, :], pD[:])
            copy(3, up[:, DK, :], pE[:])
            copy(4, con[:].rearrange("p k d -> p (k d)"), flat)
            copy(5, folded["b_up"][:], pB[:])
            copy(6, folded["w_down"][:].rearrange("p k d -> p (k d)"), flat, 0.5)
            act.wait_ge(psum_read, 7)


def butterfly_ffn(nc, tag, T, x_res, mean, rstd, cst, folded, stats, moves=(), out=None):
    NT, G = T // P, T // GW
    w_up, b_up, w_down, b_down = (folded[n] for n in ("w_up", "b_up", "w_down", "b_down"))
    HK = w_down.shape[1]
    ident = cst["ident"]
    NH = 4
    with ExitStack() as memory:
        ph = Phase(nc, memory, tag)
        xn = [ph.sb(f"xn{p}", [P, GT, D]) for p in range(2)]
        w_up_h, w_up_l = (ph.sb(f"w_up_{n}", w_up.shape, F32R) for n in "hl")
        w_down_h, w_down_l = (ph.sb(f"w_down_{n}", w_down.shape, F32R) for n in "hl")
        xTh, xTl = ([ph.sb(f"xT{n}{p}", [P, DK, GW], F32R) for p in range(2)] for n in "hl")
        hTh, hTl = ([ph.sb(f"hT{n}{p}", [P, HK, GW], F32R) for p in range(2)] for n in "hl")
        NR = 4
        h = ph.sb("h", [P, NR, GW])
        CUTS = HK
        pX, pH, pY = ph.ps("pX", [P, DK, GW]), ph.ps("pH", [P, NH, GW]), ph.ps("pY", [P, 2, 512])
        xn_ready, xT_in_psum, xnT_ready, h_in_psum, h_ready, y_in_psum, y_added, biased = (
            ph.sem(n) for n in ("xn_ready", "xT_in_psum", "xnT_ready", "h_in_psum", "h_ready", "y_in_psum",
                                "y_added", "biased"))
        high_cut, x_split, h_split, w_cut, moved = (
            ph.sem(n) for n in ("high_cut", "x_split", "h_split", "w_cut", "moved"))
        block = memory.enter_context(nc.Block())

        @block.sync
        def _(sp):
            for to, source in moves:
                sp.dma_start(to, source).then_inc(moved, 16)
            if moves:
                sp.wait_ge(moved, 16 * len(moves))
            if out is not None:
                for g in range(G):
                    sp.wait_ge(biased, after(GT * g + GT - 1))
                    sp.dma_start(out[:, g * GW:(g + 1) * GW, :].rearrange("a (t p) d -> p (a t) d", p=P),
                                 x_res[:, g * GT:(g + 1) * GT, :]).then_inc(moved, 16)
                sp.wait_ge(moved, 16 * G)

        @block.vector
        def _(dve):
            dve.sem_inc(xn_ready, LEAD)
            dve.sem_inc(y_added, LEAD)
            dve.sem_inc(biased, LEAD)
            for s in (high_cut, x_split, h_split):
                dve.sem_inc(s, LEAD)

            def split_x(g, p):
                dve.wait_ge(xnT_ready, after(g))
                dve.wait_ge(h_in_psum, after(HK * (g - 1) - 1))
                cut_low(nc.vector, xTl[p][:], pX[:], xTh[p][:]).then_inc(x_split, 1)

            def normalise(g, p):
                dve.wait_ge(xT_in_psum, after(g - 2))
                for j in range(GT):
                    t = GT * g + j
                    nc.vector.tensor_scalar(xn[p][:, j:j + 1, :], x_res[:, at(t), :], mean[:, at(t)],
                                            rstd[:, at(t)], ALU.subtract, ALU.mult).then_inc(xn_ready, 1)

            def group(i, p, last_of_all=False):
                g = 2 * i + p
                if not last_of_all:
                    normalise(g + 1, 1 - p)
                dve.wait_ge(y_in_psum, after(GT * (g - 1) - 1))
                for f in range(HK):
                    dve.wait_ge(h_ready, after(HK * g + f))
                    cut_high(nc.vector, hTh[p][:, f, :], h[:, f % NR, :]).then_inc(high_cut, 1)
                    dve.wait_ge(high_cut, after(CUTS * g + f))
                    cut_low(nc.vector, hTl[p][:, f, :], h[:, f % NR, :], hTh[p][:, f, :]).then_inc(h_split, 1)
                for j in range(GT):
                    t = GT * g + j
                    if j == 1 and not last_of_all:
                        split_x(g + 1, 1 - p)
                    dve.wait_ge(y_in_psum, after(t))
                    nc.vector.tensor_tensor(x_res[:, at(t), :], x_res[:, at(t), :], pY[:, j % 2:j % 2 + 1, 0:D],
                                            ALU.add).then_inc(y_added, 1)
                    dve.wait_ge(y_added, after(t))
                    nc.vector.tensor_tensor(x_res[:, at(t), :], x_res[:, at(t), :], spread(b_down[:], 1, 1),
                                            ALU.add).then_inc(biased, 1)
                    if stats is not None and j:
                        dve.wait_ge(biased, after(t - 1))
                        token_stats(nc, stats, x_res, t - 1)
                if stats is not None:
                    dve.wait_ge(biased, after(GT * g + GT - 1))
                    token_stats(nc, stats, x_res, GT * g + GT - 1)

            normalise(0, 0)
            cut_high(nc.vector, w_up_h[:], w_up[:]).then_inc(w_cut, 1)
            dve.wait_ge(w_cut, 1)
            cut_low(nc.vector, w_up_l[:], w_up[:], w_up_h[:]).then_inc(w_cut, 1)
            split_x(0, 0)
            cut_high(nc.vector, w_down_h[:], w_down[:]).then_inc(w_cut, 1)
            with dve.Fori(0, G // 2 - 1) as i:
                for p in range(2):
                    group(i, p)
            group(G // 2 - 1, 0)
            group(G // 2 - 1, 1, last_of_all=True)

        @block.gpsimd
        def _(pool):
            pool.wait_ge(w_cut, 3)
            cut_low(nc.gpsimd, w_down_l[:], w_down[:], w_down_h[:]).then_inc(w_cut, 1)

        def transpose_group(pe, g, p):
            pe.wait_ge(xn_ready, after(GT * g + GT - 1))
            pe.wait_ge(x_split, after(g - 1))
            for j in range(GT):
                for k in range(DK):
                    last = nc.tensor.transpose(pX[:, k, j * P:(j + 1) * P], xn[p][:, j, k * P:(k + 1) * P], ident[:])
            last.then_inc(xT_in_psum, 1)

        @block.tensor
        def _(pe):
            for s in (xT_in_psum, h_in_psum, y_in_psum):
                pe.sem_inc(s, LEAD)
            transpose_group(pe, 0, 0)
            pe.wait_ge(w_cut, 2)

            def group(i, p, last_of_all=False):
                g = 2 * i + p
                pe.wait_ge(x_split, after(g))
                for f in range(HK):
                    pe.wait_ge(h_ready, after(HK * g + f - NH))
                    cols = slice(f * P, (f + 1) * P)
                    for k in range(DK):
                        last = split_matmul(nc, pH[:, f % NH, :], (w_up_h[:, k, cols], w_up_l[:, k, cols]),
                                            (xTh[p][:, k, :], xTl[p][:, k, :]), k == 0, k == DK - 1)
                    last.then_inc(h_in_psum, 1)
                if not last_of_all:
                    transpose_group(pe, g + 1, 1 - p)
                if isinstance(g, int) and g == 0:
                    pe.wait_ge(w_cut, 4)
                for j in range(GT):
                    pe.wait_ge(y_added, after(GT * g + j - 2))
                    rows = slice(j * P, (j + 1) * P)
                    for f in range(HK):
                        if j == 0:
                            pe.wait_ge(h_split, after(HK * g + f))
                        last = split_matmul(nc, pY[:, j % 2, 0:D], (hTh[p][:, f, rows], hTl[p][:, f, rows]),
                                            (w_down_h[:, f, :], w_down_l[:, f, :]), f == 0, f == HK - 1)
                    last.then_inc(y_in_psum, 1)

            group(0, 0)
            group(0, 1)
            with pe.Fori(1, G // 2 - 1) as i:
                for p in range(2):
                    group(i, p)
            group(G // 2 - 1, 0)
            group(G // 2 - 1, 1, last_of_all=True)

        @block.scalar
        def _(act):
            act.sem_inc(xnT_ready, LEAD)
            act.sem_inc(h_ready, LEAD)

            def copy_xnT(g, p):
                act.wait_ge(xT_in_psum, after(g))
                act.wait_ge(h_in_psum, after(HK * (g - 1) - 1))
                nc.scalar.activation(xTh[p][:], pX[:], ACT.Copy).then_inc(xnT_ready, 1)

            def group(i, p, last_of_all=False):
                g = 2 * i + p
                for f in range(HK):
                    act.wait_ge(h_in_psum, after(HK * g + f))
                    act.wait_ge(h_split, after(HK * g + f - NR))
                    nc.scalar.activation(h[:, f % NR, :], pH[:, f % NH, :], ACT.Gelu,
                                         bias=b_up[:, f:f + 1]).then_inc(h_ready, 1)
                if not last_of_all:
                    copy_xnT(g + 1, 1 - p)

            copy_xnT(0, 0)
            with act.Fori(0, G // 2 - 1) as i:
                for p in range(2):
                    group(i, p)
            group(G // 2 - 1, 0)
            group(G // 2 - 1, 1, last_of_all=True)


def linear_attention(nc, tag, T, H, BD, x_res, mean, rstd, cst, qkv_w, qkv_b, out_w, out_b,
                     stats):
    G = T // GW
    HT = P // BD
    VW = 2 * BD
    HQ = P // VW
    EPS = 1e-6
    ident = cst["ident"]
    NM = 2 * DK
    with ExitStack() as memory:
        ph = Phase(nc, memory, tag)
        wqkv, wout = ph.sb("wqkv", [P, DK, 3 * D]), ph.sb("wout", [P, DK, D])
        b_rows, b_cols, b_cols1 = ph.sb("b_rows", [NM, P]), ph.sb("b_cols", [P, NM]), ph.sb("b_cols1", [P, NM])
        b_value, b_out = ph.sb("b_value", [P, D]), ph.sb("b_out", [P, D])
        xn = [ph.sb(f"xn{p}", [P, GT, D]) for p in range(2)]
        wh, wl = (ph.sb(f"wqkv_{n}", [P, DK, 3 * D], F32R) for n in "hl")
        xTh, xTl = ([ph.sb(f"xT{n}{p}", [P, DK, GW], F32R) for p in range(2)] for n in "hl")
        low = [ph.sb(f"low{m}", [P, GW]) for m in range(2)]
        qk = [ph.sb(f"qk{p}", [P, NM, GW]) for p in range(2)]
        q_of = [ph.sb(f"q_of{p}", [P, DK, 2, GW]) for p in range(2)]
        v1 = [ph.sb(f"v1{p}", [P, H, VW]) for p in range(2)]
        kt = [ph.sb(f"kt{p}", [P, D]) for p in range(2)]
        scores = [ph.sb(f"scores{p}", [P, H, P]) for p in range(2)]
        state, added = ph.sb("state", [P, DK, HT * VW]), ph.sb("added", [P, DK, HT * VW])
        ctxT = ph.sb("ctxT", [P, H // HQ, P])
        denom = ph.sb("denom", [P, H])
        o = ph.sb("o", [P, H, BD])
        oT = ph.sb("oT", [P, DK, P])
        y = ph.sb("y", [P, D])

        pF = ph.ps("pF", [P, 2, GW])
        pS = ph.ps("pS", [P, 2, GW])
        pV, pC, pU, pO = (ph.ps(n, [P, 512]) for n in ("pV", "pC", "pU", "pO"))

        w_loaded, b_in_psum, bias_ready, setup = (ph.sem(n) for n in ("w_loaded", "b_in_psum", "bias_ready", "setup"))
        xn_ready, xT_in_psum, xnT_ready = (ph.sem(n) for n in ("xn_ready", "xT_in_psum", "xnT_ready"))
        f_in_psum, low_ready, exp_ready, f_ready, q_split = (
            ph.sem(n) for n in ("f_in_psum", "low_ready", "exp_ready", "f_ready", "q_split"))
        vk_in_psum, vk_ready, s_in_psum, s_ready, c_in_psum, u_in_psum = (
            ph.sem(n) for n in ("vk_in_psum", "vk_ready", "s_in_psum", "s_ready", "c_in_psum", "u_in_psum"))
        w_split, x_split = ph.sem("w_split"), ph.sem("x_split")
        cT_ready, ctx_in_psum = ph.sem("cT_ready"), ph.sem("ctx_in_psum")
        state_step, denom_step, o_step, oT_in_psum, oT_ready, y_in_psum, y_read, y_added = (
            ph.sem(n) for n in ("state_step", "denom_step", "o_step", "oT_in_psum", "oT_ready", "y_in_psum", "y_read", "y_added"))
        block = memory.enter_context(nc.Block())

        def all_steps(eng, step):
            for j in range(GT):
                step(0, 0, j, before=(j >= 1), second=(j >= 2))
            for j in range(GT):
                step(1, 1, j)
            with eng.Fori(1, G // 2 - 1) as i:
                for p in range(2):
                    for j in range(GT):
                        step(2 * i + p, p, j)
            for j in range(GT):
                step(G - 2, 0, j)
            for j in range(GT):
                step(G - 1, 1, j, following=False)
            step(G, 0, 0, main=False, following=False)
            step(G, 0, 1, main=False, before=False, following=False)

        @block.sync
        def _(sp):
            sp.dma_start(wqkv[:], qkv_w.rearrange("(k p) n -> p k n", p=P)).then_inc(w_loaded, 16)
            sp.dma_start(wout[:], out_w.rearrange("(k p) n -> p k n", p=P)).then_inc(w_loaded, 16)
            sp.dma_start(b_rows[:], qkv_b[0:2 * D].rearrange("(m p) -> m p", p=P)).then_inc(w_loaded, 16)
            sp.dma_start(b_value[:], qkv_b[2 * D:3 * D].partition_broadcast(P)).then_inc(w_loaded, 16)
            sp.dma_start(b_out[:], out_b.partition_broadcast(P)).then_inc(w_loaded, 16)

        @block.tensor
        def _(pe):
            for s in (xT_in_psum, f_in_psum, vk_in_psum, s_in_psum, c_in_psum, u_in_psum, ctx_in_psum, oT_in_psum,
                      y_in_psum):
                pe.sem_inc(s, LEAD)
            pe.wait_ge(w_loaded, 16 * 5)
            nc.tensor.transpose(pV[:, 0:NM], b_rows[:], ident[0:NM, 0:NM]).then_inc(b_in_psum, 1)
            pe.wait_ge(bias_ready, 2)

            def transposes(g, p):
                pe.wait_ge(xn_ready, after(GT * g + GT - 1))
                pe.wait_ge(f_ready, after(NM * g - 1))
                for k in range(DK):
                    for j in range(GT):
                        last = nc.tensor.transpose(pF[:, k, j * P:(j + 1) * P], xn[p][:, j, k * P:(k + 1) * P],
                                                   ident[:])
                last.then_inc(xT_in_psum, 1)

            def features(g, p, m):
                cols = slice(m * P, (m + 1) * P)
                pe.wait_ge(x_split, after(g))
                pe.wait_ge(f_ready, after(NM * g + m - 2))
                for k in range(DK):
                    last = split_matmul(nc, pF[:, m % 2, :], (wh[:, k, cols], wl[:, k, cols]),
                                        (xTh[p][:, k, :], xTl[p][:, k, :]), k == 0, k == DK - 1)
                last.then_inc(f_in_psum, 1)

            def front(g, p, when):
                for at_point, m in (((1, "mid"), 0), ((1, "end"), 1), ((2, "mid"), 2), ((2, "end"), 3)):
                    if when == at_point:
                        features(g, p, m)
                if when == (0, "end"):
                    transposes(g, p)

            def values_keys(c, p, j):
                chunk = slice(j * P, (j + 1) * P)
                if j == 0:
                    pe.wait_ge(f_ready, after(NM // GT * c + NM - 1))
                pe.wait_ge(vk_ready, after(2 * c - 1))
                for k in range(DK):
                    split_matmul(nc, pV[:, 0:D], (xTh[p][:, k, chunk], xTl[p][:, k, chunk]),
                                 (wh[:, k, 2 * D:3 * D], wl[:, k, 2 * D:3 * D]), k == 0, k == DK - 1)
                for k in range(DK):
                    last = nc.tensor.transpose(pV[:, D + k * P:D + (k + 1) * P], qk[p][:, DK + k, chunk], ident[:])
                last.then_inc(vk_in_psum, 1)

            def score_pair(c, p, j, pair):
                chunk = slice(j * P, (j + 1) * P)
                if j == 0 and pair == 0:
                    pe.wait_ge(q_split, after(2 * DK // GT * c + 2 * DK - 1))
                pe.wait_ge(s_ready, after(H // 4 * c + 2 * pair - 1))
                for k in range(DK):
                    for s in (2 * pair, 2 * pair + 1):
                        rows = slice(2 * BD * s, 2 * BD * (s + 1))
                        last = nc.tensor.matmul(pS[:, s % 2, k * 2 * P:(k + 1) * 2 * P],
                                                qk[p][rows, DK + k, chunk], q_of[p][rows, k, :, chunk],
                                                start=True, stop=True)
                        if k == DK - 1:
                            last.then_inc(s_in_psum, 1)

            def context(c, p, j, k):
                b, chunk, width = j % 2, slice(j * P, (j + 1) * P), HT * VW
                if k == 0:
                    pe.wait_ge(state_step, after(2 * c - 1))
                    pe.wait_ge(o_step, after(c - 1))
                    pe.wait_ge(s_ready, after(H // 4 * c + H // 4 - 1))
                    pe.wait_ge(vk_ready, after(2 * c + 1))
                for half in range(HT // HQ):
                    q = HT // HQ * k + half
                    tokens = slice(q * P, (q + 1) * P)
                    nc.tensor.matmul(pC[:, tokens], state[:, k, half * P:(half + 1) * P], qk[p][:, k, chunk],
                                     start=True, stop=False)
                    for hh in range(HQ):
                        last = nc.tensor.matmul(pC[hh * VW:(hh + 1) * VW, tokens], v1[b][:, HQ * q + hh, :],
                                                scores[b][:, HQ * q + hh, :], start=False, stop=True)
                if k == DK - 1:
                    last.then_inc(c_in_psum, 1)
                    pe.wait_ge(state_step, after(2 * c - 2))
                    for m in range(DK):
                        last = nc.tensor.matmul(pU[:, m * width:(m + 1) * width], kt[b][:, m * P:(m + 1) * P],
                                                v1[b][:, m * HT:(m + 1) * HT, :].rearrange("p h e -> p (h e)"),
                                                start=True, stop=True)
                    last.then_inc(u_in_psum, 1)

            def transpose_context(c):
                pe.wait_ge(cT_ready, after(c))
                for q in range(H // HQ):
                    last = nc.tensor.transpose(pC[:, q * P:(q + 1) * P], ctxT[:, q, :], ident[:])
                last.then_inc(ctx_in_psum, 1)

            def transpose_output(c):
                pe.wait_ge(o_step, after(c))
                pe.wait_ge(y_read, after(c - 1))
                for k in range(DK):
                    last = nc.tensor.transpose(pO[:, k * P:(k + 1) * P],
                                               o[:].rearrange("p h e -> p (h e)")[:, k * P:(k + 1) * P], ident[:])
                last.then_inc(oT_in_psum, 1)

            def project_output(c):
                pe.wait_ge(oT_ready, after(c))
                for k in range(DK):
                    last = nc.tensor.matmul(pO[:, D:2 * D], oT[:, k, :], wout[:, k, :],
                                            start=(k == 0), stop=(k == DK - 1))
                last.then_inc(y_in_psum, 1)

            def step(g, p, j, main=True, before=True, second=True, following=True):
                c = GT * g + j
                last_p, last_j = (p, j - 1) if j else (1 - p, GT - 1)
                if main:
                    values_keys(c, p, j)
                    score_pair(c, p, j, 0)
                if before:
                    context(c - 1, last_p, last_j, 0)
                if second:
                    transpose_output(c - 2)
                if following:
                    front(g + 1, 1 - p, (j, "mid"))
                if main:
                    score_pair(c, p, j, 1)
                if before:
                    context(c - 1, last_p, last_j, 1)
                if second:
                    project_output(c - 2)
                if before:
                    transpose_context(c - 1)
                if following:
                    front(g + 1, 1 - p, (j, "end"))

            transposes(0, 0)
            pe.wait_ge(w_split, 2)
            for m in range(NM):
                features(0, 0, m)
            all_steps(pe, step)

        @block.scalar
        def _(act):
            for s in (xnT_ready, exp_ready, oT_ready, cT_ready):
                act.sem_inc(s, LEAD)
            act.wait_ge(b_in_psum, 1)
            nc.scalar.activation(b_cols[:], pV[:, 0:NM], ACT.Copy).then_inc(bias_ready, 1)

            def copy_xnT(g, p):
                act.wait_ge(xT_in_psum, after(g))
                act.wait_ge(vk_in_psum, after(GT * (g - 1) - 1))
                nc.scalar.activation(xTh[p][:], pF[:], ACT.Copy).then_inc(xnT_ready, 1)

            def exponential(g, m):
                act.wait_ge(low_ready, after(NM * g + m))
                nc.scalar.activation(low[m % 2][:], low[m % 2][:], ACT.Exp).then_inc(exp_ready, 1)

            def step(g, p, j, main=True, before=True, second=True, following=True):
                c = GT * g + j
                if second:
                    act.wait_ge(oT_in_psum, after(c - 2))
                    act.wait_ge(y_in_psum, after(c - 3))
                    nc.scalar.activation(oT[:], pO[:, 0:D].rearrange("p (k t) -> p k t", k=DK), ACT.Copy
                                         ).then_inc(oT_ready, 1)
                if following and j in (1, 2):
                    exponential(g + 1, 2 * j - 2)
                if before:
                    act.wait_ge(c_in_psum, after(c - 1))
                    act.wait_ge(ctx_in_psum, after(c - 2))
                    nc.scalar.activation(ctxT[:].rearrange("p q t -> p (q t)"), pC[:], ACT.Copy
                                         ).then_inc(cT_ready, 1)
                if following and j == 0:
                    copy_xnT(g + 1, 1 - p)
                if following and j in (1, 2):
                    exponential(g + 1, 2 * j - 1)

            copy_xnT(0, 0)
            for m in range(NM):
                exponential(0, m)
            all_steps(act, step)

        @block.gpsimd
        def _(pool):
            pool.sem_inc(y_added, LEAD)
            with pool.Fori(0, G // 2) as i:
                for p in range(2):
                    for j in range(GT):
                        c = GT * (2 * i + p) + j
                        pool.wait_ge(y_read, after(c))
                        nc.gpsimd.tensor_tensor(x_res[:, at(c), :], x_res[:, at(c), :], spread(y[:], 1, 1), ALU.add
                                                ).then_inc(y_added, 1)

        @block.vector
        def _(dve):
            for s in (x_split, xn_ready, low_ready, f_ready, q_split, vk_ready, s_ready, state_step, denom_step, o_step, y_read):
                dve.sem_inc(s, LEAD)
            for b in range(2):
                nc.vector.memset(v1[b][:, :, BD:BD + 1], 1.0).then_inc(setup, 1)
                nc.vector.memset(v1[b][:, :, BD + 1:VW], 0.0).then_inc(setup, 1)
            nc.vector.memset(state[:], 0.0).then_inc(setup, 1)
            dve.wait_ge(bias_ready, 1)
            nc.vector.tensor_scalar(b_cols1[:], b_cols[:], 1.0, None, ALU.add).then_inc(bias_ready, 1)
            dve.wait_ge(bias_ready, 2)
            dve.wait_ge(setup, 5)
            dve.wait_ge(w_loaded, 16 * 5)

            def normalise(g, p):
                dve.wait_ge(xT_in_psum, after(g - 2))
                for j in range(GT):
                    t = GT * g + j
                    nc.vector.tensor_scalar(xn[p][:, j:j + 1, :], x_res[:, at(t), :], mean[:, at(t)],
                                            rstd[:, at(t)], ALU.subtract, ALU.mult).then_inc(xn_ready, 1)

            def split_x(g, p):
                dve.wait_ge(xnT_ready, after(g))
                dve.wait_ge(vk_in_psum, after(GT * (g - 1) - 1))
                cut_low(nc.vector, xTl[p][:], pF[:], xTh[p][:]).then_inc(x_split, 1)

            def lower_part(g, m):
                dve.wait_ge(f_in_psum, after(NM * g + m))
                dve.wait_ge(f_ready, after(NM * g + m - 2))
                nc.vector.tensor_scalar(low[m % 2][:], pF[:, m % 2, :], b_cols[:, m:m + 1], 0.0,
                                        ALU.add, ALU.min).then_inc(low_ready, 1)

            def feature_map(g, p, m):
                if m == 0:
                    dve.wait_ge(u_in_psum, after(GT * (g - 1) - 1))
                dve.wait_ge(exp_ready, after(NM * g + m))
                nc.vector.scalar_tensor_tensor(out=qk[p][:, m, :], in0=pF[:, m % 2, :],
                                               scalar=b_cols1[:, m:m + 1], in1=low[m % 2][:],
                                               op0=ALU.add, op1=ALU.max).then_inc(f_ready, 1)

            def split_heads(g, p, k):
                dve.wait_ge(f_ready, after(NM * g + k))
                for odd in range(2):
                    nc.vector.tensor_scalar(q_of[p][:, k, odd, :], qk[p][:, k, :], cst["parity"][:, odd:odd + 1],
                                            None, ALU.mult).then_inc(q_split, 1)

            def front(g, p, when):
                if when == (0, 0):
                    normalise(g, p)
                if when == (1, 0):
                    split_x(g, p)
                if when == (1, 2):
                    lower_part(g, 0)
                if when == (1, 3):
                    feature_map(g, p, 0)
                    lower_part(g, 1)
                if when == (2, 1):
                    feature_map(g, p, 1)
                if when == (2, 2):
                    lower_part(g, 2)
                if when == (2, 3):
                    feature_map(g, p, 2)
                    lower_part(g, 3)
                if when == (3, 1):
                    feature_map(g, p, 3)
                if when == (3, 2):
                    split_heads(g, p, 0)
                if when == (3, 3):
                    split_heads(g, p, 1)

            def values_keys(c, b):
                dve.wait_ge(vk_in_psum, after(c))
                dve.wait_ge(u_in_psum, after(c - 2))
                nc.vector.tensor_tensor(v1[b][:, :, 0:BD], pV[:, 0:D].rearrange("p (h e) -> p h e", e=BD),
                                        b_value[:].rearrange("p (h e) -> p h e", e=BD), ALU.add
                                        ).then_inc(vk_ready, 1)
                nc.vector.tensor_copy(kt[b][:], pV[:, D:2 * D]).then_inc(vk_ready, 1)

            def masked_scores(c, b, pair):
                for s in (2 * pair, 2 * pair + 1):
                    dve.wait_ge(s_in_psum, after(H // 4 * c + s))
                    if s == 0:
                        dve.wait_ge(c_in_psum, after(c - 2))
                    nc.vector.tensor_tensor(
                        scores[b][:].rearrange("p (k h) t -> p k h t", k=DK)[:, :, 2 * s:2 * s + 2, :],
                        pS[:, s % 2, :].rearrange("p (k h t) -> p k h t", k=DK, t=P),
                        spread(spread(cst["causal"][:], 1, 2), 1, DK), ALU.mult).then_inc(s_ready, 1)

            def next_state(c):
                dve.wait_ge(u_in_psum, after(c))
                own = spread(spread(cst["head_block"][:, :, 0], 2, VW), 1, DK)
                nc.vector.tensor_tensor(added[:].rearrange("p k (h e) -> p k h e", e=VW),
                                        pU[:].rearrange("p (k h e) -> p k h e", k=DK, e=VW), own, ALU.mult
                                        ).then_inc(state_step, 1)
                dve.wait_ge(state_step, after(2 * c))
                nc.vector.tensor_tensor(state[:], state[:], added[:], ALU.add).then_inc(state_step, 1)

            def normed_context(c):
                dve.wait_ge(ctx_in_psum, after(c))
                dve.wait_ge(oT_in_psum, after(c - 1))
                ctxv = pC[:].rearrange("p (h e) -> p h e", e=VW)
                nc.vector.tensor_scalar(denom[:], ctxv[:, :, BD], EPS, None, ALU.add).then_inc(denom_step, 1)
                dve.wait_ge(denom_step, after(2 * c))
                nc.vector.reciprocal(denom[:], denom[:]).then_inc(denom_step, 1)
                dve.wait_ge(denom_step, after(2 * c + 1))
                nc.vector.tensor_tensor(o[:], ctxv[:, :, 0:BD], spread(denom[:], 2, BD), ALU.mult
                                        ).then_inc(o_step, 1)

            def take_output(c):
                dve.wait_ge(y_in_psum, after(c))
                dve.wait_ge(y_added, after(c - 1))
                nc.vector.tensor_tensor(y[:], pO[:, D:2 * D], b_out[:], ALU.add).then_inc(y_read, 1)

            def step(g, p, j, main=True, before=True, second=True, following=True):
                c = GT * g + j
                if second and not (isinstance(c, int) and c < 3):
                    dve.wait_ge(y_added, after(c - 3))
                    token_stats(nc, stats, x_res, c - 3)
                if following:
                    front(g + 1, 1 - p, (j, 0))
                if main:
                    values_keys(c, j % 2)
                    masked_scores(c, j % 2, 0)
                if following:
                    front(g + 1, 1 - p, (j, 1))
                if main:
                    masked_scores(c, j % 2, 1)
                if following:
                    front(g + 1, 1 - p, (j, 2))
                if before:
                    next_state(c - 1)
                if second:
                    take_output(c - 2)
                if before:
                    normed_context(c - 1)
                if following:
                    front(g + 1, 1 - p, (j, 3))

            normalise(0, 0)
            cut_high(nc.vector, wh[:], wqkv[:]).then_inc(w_split, 1)
            dve.wait_ge(w_split, 1)
            cut_low(nc.vector, wl[:], wqkv[:], wh[:]).then_inc(w_split, 1)
            split_x(0, 0)
            for m in range(NM):
                lower_part(0, m)
                feature_map(0, 0, m)
            for k in range(DK):
                split_heads(0, 0, k)
            all_steps(dve, step)
            dve.wait_ge(y_added, after(GT * G - 1))
            token_stats(nc, stats, x_res, GT * G - 1)


def window_weights(nc, ph, tag, H, BD, cst, a):
    W = a["L1_attn_rel_pos_emb"].shape[0]
    FT = 2 * BD
    HG = P // FT
    NG = H // HG
    HT = P // BD
    res = {"features": ph.sb("features", [P, DK, H * FT]), "offset": ph.sb("offset", [P, W]),
           "reduce": ph.sb("reduce", [P, HG, 2, HG, HG]), "value": ph.sb("value", [P, DK, D]),
           "proj": ph.sb("proj", [P, NG, D]), "half_damage_b": ph.sb("half_damage_b", [P, 1])}
    with ExitStack() as memory:
        t = Phase(nc, memory, tag)
        disp, val_rows = t.sb("disp", [P, DK, D]), t.sb("val_rows", [P, DK, D])
        proj_rows = t.sb("proj_rows", [P, DK, H, FT])
        strain = t.sb("strain", [P, HT, FT])
        place_w, place = t.sb("place_w", [BD, HG, 2, BD]), t.sb("place", [BD, W])
        fused_b, last_w = t.sb("fused_b", [P, 1]), t.sb("last_w", [P, 1])
        reduced = t.sb("reduced", [P, 2, HG])
        pW = t.ps("pW", [P, DK, 512])
        pR = t.ps("pR", [P, 2, 512])
        pP = t.ps("pP", [P, 2, 512])
        pO = t.ps("pO", [P, 512])
        cleared, loaded, made, in_psum = t.sem("cleared"), t.sem("loaded"), t.sem("made"), t.sem("in_psum")
        block = memory.enter_context(nc.Block())

        @block.sync
        def _(sp):
            sp.dma_start(disp[:], a["L1_attn_W_disp"].rearrange("(k p) d -> p k d", p=P)).then_inc(loaded, 16)
            sp.dma_start(val_rows[:], a["L1_attn_W_val"].rearrange("(k p) d -> p k d", p=P)).then_inc(loaded, 16)
            sp.dma_start(res["half_damage_b"][:], a["L1_attn_damage_out_b"].partition_broadcast(P)).then_inc(loaded, 16)
            sp.dma_start(place[:], a["L1_attn_rel_pos_emb"].rearrange("w b -> b w"),
                             allow_slow_non_contiguous=True).then_inc(loaded, 16)
            for h in range(HG):
                sp.dma_start(fused_b[h * FT:(h + 1) * FT, :], a["L1_attn_strain_fused_b"].rearrange("(f a) -> f a", a=1),
                             allow_slow_non_contiguous=True).then_inc(loaded, 16)
                for half, name in ((0, "L1_attn_bond_out_w"), (1, "L1_attn_damage_out_w")):
                    rows = slice(h * FT + half * BD, h * FT + (half + 1) * BD)
                    sp.dma_start(last_w[rows, :], a[name].rearrange("a b -> b a"),
                             allow_slow_non_contiguous=True).then_inc(loaded, 16)
            sp.wait_ge(cleared, 3)
            for h in range(HT):
                sp.dma_start(strain[h * BD:(h + 1) * BD, h, :], a["L1_attn_strain_fused_w"].rearrange("f b -> b f"),
                             allow_slow_non_contiguous=True).then_inc(loaded, 16)
            for h in range(HG):
                sp.dma_start(place_w[:, h, 0, :], a["L1_attn_pos_proj_w"].rearrange("f b -> b f"),
                             allow_slow_non_contiguous=True).then_inc(loaded, 16)
            for k in range(DK):
                sp.dma_start(proj_rows[:, k, :, 0:BD], a["L1_attn_c_proj_w"][k * P:(k + 1) * P, :].rearrange(
                    "p (h e) -> p h e", e=BD)).then_inc(loaded, 16)

        n_loads = 4 + 3 * HG + HT + HG + DK

        @block.vector
        def _(dve):
            nc.vector.memset(strain[:], 0.0).then_inc(cleared, 1)
            nc.vector.memset(place_w[:], 0.0).then_inc(cleared, 1)
            nc.vector.memset(proj_rows[:], 0.0).then_inc(cleared, 1)
            nc.vector.memset(res["reduce"][:], 0.0).then_inc(made, 1)
            dve.wait_ge(loaded, 16 * n_loads)
            own = cst["head_block"][:, :, 0].rearrange("p (h two) -> p two h", two=2)
            nc.vector.tensor_scalar(reduced[:], own, last_w[:], None, ALU.mult).then_inc(made, 1)
            nc.vector.tensor_scalar(res["half_damage_b"][:], res["half_damage_b"][:], 0.5, None, ALU.mult)
            dve.wait_ge(made, 2)
            for k in range(HG):
                nc.vector.tensor_copy(res["reduce"][:, k, :, :, k], reduced[:])
            dve.wait_ge(in_psum, 1)
            nc.vector.tensor_scalar(res["offset"][:], pO[:, 0:W], fused_b[:], None, ALU.add)

        @block.tensor
        def _(pe):
            pe.wait_ge(loaded, 16 * n_loads)
            nc.tensor.matmul(pO[:, 0:W], place_w[:].rearrange("b h two f -> b (h two f)"), place[:],
                             start=True, stop=True).then_inc(in_psum, 1)
            for k in range(DK):
                for m in range(DK):
                    nc.tensor.matmul(pW[:, m, k * HT * FT:(k + 1) * HT * FT], disp[:, k, m * P:(m + 1) * P],
                                     strain[:].rearrange("p h f -> p (h f)"), start=True, stop=True)
                    nc.tensor.transpose(pR[:, 0, m * D + k * P:m * D + (k + 1) * P], val_rows[:, k, m * P:(m + 1) * P],
                                        cst["ident"][:])
                for q in range(NG):
                    last = nc.tensor.transpose(
                        pP[:, q // 2, (q % 2) * D + k * P:(q % 2) * D + (k + 1) * P],
                        proj_rows[:, k, q * HG:(q + 1) * HG, :].rearrange("p h f -> p (h f)"), cst["ident"][:])
            last.then_inc(in_psum, 1)

        @block.scalar
        def _(act):
            act.wait_ge(in_psum, 2)
            nc.scalar.activation(res["features"][:], pW[:], ACT.Copy)
            nc.scalar.activation(res["value"][:].rearrange("p k d -> p (k d)"), pR[:, 0, :], ACT.Copy)
            nc.scalar.activation(res["proj"][:].rearrange("p q d -> p (q d)"),
                                 pP[:].rearrange("p a b -> p (a b)"), ACT.Copy)
    return res


def window_attention(nc, tag, T, H, BD, x_res, mean, rstd, cst, a):
    G = T // GW
    W = a["L1_attn_rel_pos_emb"].shape[0]
    FT = 2 * BD
    HG = P // FT
    NG = H // HG
    KW = HG
    NW = W // KW
    RING = 4
    HP = H // 2
    DVE_TOKENS = 292
    BAND = 2 * P
    PITCH = 3 * P
    LEFT = PITCH // 2
    SOFT, EXPS, PROB, WIDE = 2 * KW, 5 * KW, 6 * KW, W // 2
    COPY_LAG = 4
    ident = cst["ident"]
    band_dram = nc.dram_tensor(f"{tag}_band", [2, P, H, PITCH], F32)
    band = band_dram.ap()
    with ExitStack() as memory:
        ph = Phase(nc, memory, tag)
        wt = window_weights(nc, ph, tag + "_w", H, BD, cst, a)
        xn = ph.sb("xn", [P, GT, D])
        xnT = ph.sb("xnT", [P, DK, GW])
        feat = [ph.sb(f"feat{p}", [P, NG, W + GW]) for p in range(2)]
        val = [ph.sb(f"val{p}", [P, GT, H, FT]) for p in range(2)]
        val_before = ph.sb("val_before", [P, H, FT])
        pair = [ph.sb(f"pair{r}", [P, NG, GW]) for r in range(RING)]
        flat = [ph.sb(f"flat{b}", [P, GW]) for b in range(2)]
        damage = ph.sb("damage", [P, GT, NG, HG * KW])
        logit = [ph.sb(f"logit{p}", [P, GT, NW, H, KW]) for p in range(2)]
        top, total = ph.sb("top", [P, H]), ph.sb("total", [P, H])
        prob = ph.sb("prob", [P, H, W])
        wide = [ph.sb(f"wide{b}", [P, H, BAND]) for b in range(2)]
        wideT = [ph.sb(f"wideT{b}", [P, 2, 2, P]) for b in range(2)]
        oT = ph.sb("oT", [P, NG, P])
        pF, pW, pA = (ph.ps(n, [P, 2, 512]) for n in ("pF", "pW", "pA"))
        pL, pO = ph.ps("pL", [P, GT, P]), ph.ps("pO", [P, NG, P])

        names = ("zeros_ready", "band_zeroed", "setup", "xn_ready", "xT_in_psum", "xnT_ready", "f_in_psum", "f_ready",
                 "halo_ready", "before_ready", "v_in_psum", "v_ready", "diff_dve", "diff_pool", "gelu_ready",
                 "reduced", "flat_ready", "l_in_psum", "tanh_ready", "logit_ready", "soft_step", "exp_ready",
                 "masked", "prob_step", "prob_stored", "a_in_psum", "a_ready", "o_in_psum",
                 "oT_ready", "y_in_psum", "y_added", "pool_turn")
        s = {n: ph.sem(n) for n in names}
        wide_loaded = ph.sems("wide_loaded")
        block = memory.enter_context(nc.Block())

        def all_groups(eng, group):
            group(0, 0, True, False, False)
            group(1, 1, True, True, False)
            with eng.Fori(1, G // 2 - 1) as i:
                for p in range(2):
                    group(2 * i + p, p, True, True, True)
            group(G - 2, 0, True, True, True)
            group(G - 1, 1, True, True, True)
            group(G, 0, False, True, True)
            group(G + 1, 1, False, False, True)

        def head_pair(g, p, step, tail, rest):
            if tail and 0 <= step < GT * HP:
                return g - 1, 1 - p, step // HP, step % HP
            if rest and 0 <= step + W < GT * HP:
                step += W
                return g - 2, p, step // HP, step % HP
            return None

        def tile_done(g, p, step, tail, rest):
            found = head_pair(g, p, step - HP, tail, rest)
            return found[:3] if found and found[3] == 0 else None

        @block.sync
        def _(sp):
            sp.wait_ge(s["zeros_ready"], 1)
            third = H * PITCH // 3
            for b in range(2):
                sp.dma_start(band[b].rearrange("p h w -> p (h w)").rearrange("p (c f) -> p c f", f=third),
                             spread(pair[RING - 1][:].rearrange("p g t -> p (g t)")[:, 0:third], 1, 3)
                             ).then_inc(s["band_zeroed"], 16)
            sp.wait_ge(s["band_zeroed"], 32)
            sp.sem_inc(s["prob_stored"], 16)
            for b in range(2):
                sp.sem_inc(wide_loaded[b], 16)
            with sp.Fori(0, T // P // 2) as i:
                for b in range(2):
                    t = 2 * i + b
                    sp.wait_ge(s["prob_step"], after(3 * t + 2))
                    sp.wait_ge(wide_loaded[b], landed(i - 1))
                    sp.dma_start(band[b, :, :, LEFT:LEFT + W], prob[:]).then_inc(s["prob_stored"], 16)
                    sp.wait_ge(s["prob_stored"], landed(t))
                    sp.wait_ge(s["a_in_psum"], after(HP * (t - 1) - 1))
                    skewed = bass.AP(tensor=band_dram, offset=b * P * H * PITCH + LEFT - 1,
                                     ap=[[H * PITCH - 1, P], [PITCH, H], [1, BAND - (P - W)]])
                    sp.dma_start(wide[b][:, :, P - W:BAND], skewed).then_inc(wide_loaded[b], 16)

        @block.tensor
        def _(pe):
            for n in ("xT_in_psum", "f_in_psum", "v_in_psum", "reduced", "l_in_psum", "a_in_psum", "o_in_psum",
                      "y_in_psum"):
                pe.sem_inc(s[n], LEAD)

            def transposes(g):
                pe.wait_ge(s["xn_ready"], after(GT * g + GT - 1))
                pe.wait_ge(s["y_added"], after(GT * (g - 2) - 1))
                pe.wait_ge(s["f_ready"], after(NG * g - 1))
                for k in range(DK):
                    for j in range(GT):
                        last = nc.tensor.transpose(pF[:, k, j * P:(j + 1) * P], xn[:, j, k * P:(k + 1) * P], ident[:])
                last.then_inc(s["xT_in_psum"], 1)

            def features(g, m):
                pe.wait_ge(s["xnT_ready"], after(g))
                pe.wait_ge(s["f_ready"], after(NG * g + m - 2))
                for k in range(DK):
                    last = nc.tensor.matmul(pF[:, m % 2, :], wt["features"][:, k, m * P:(m + 1) * P],
                                            xnT[:, k, :], start=(k == 0), stop=(k == DK - 1))
                last.then_inc(s["f_in_psum"], 1)

            def values(g, j):
                pe.wait_ge(s["v_ready"], after(GT * g + j - 2))
                for k in range(DK):
                    last = nc.tensor.matmul(pA[:, j % 2, 0:D], xnT[:, k, j * P:(j + 1) * P],
                                            wt["value"][:, k, :], start=(k == 0), stop=(k == DK - 1))
                last.then_inc(s["v_in_psum"], 1)

            transposes(0)
            for m in range(NG):
                features(0, m)

            def group(g, p, main, tail, rest):
                for st in range(W):
                    slot, k = divmod(st, KW)
                    b = slot % 2
                    wg = NW * g + slot
                    if main:
                        if k == 0:
                            pe.wait_ge(s["flat_ready"], after(wg - 2))
                        pe.wait_ge(s["gelu_ready"], after(W * g + st))
                        for q in range(NG):
                            last = nc.tensor.matmul(
                                pW[q * FT:(q + 1) * FT, b, :],
                                wt["reduce"][:, k].rearrange("p two h k -> p (two h k)"), pair[st % RING][:, q, :],
                                start=(k == 0), stop=(k == KW - 1))
                        last.then_inc(s["reduced"], 1)
                    if k == 1 and (main or (tail and slot == 0)) and not (isinstance(g, int) and wg == 0):
                        pe.wait_ge(s["flat_ready"], after(wg - 1))
                        pe.wait_ge(s["logit_ready"], after(wg - 2))
                        for j in range(GT):
                            last = nc.tensor.transpose(pL[:, j, :], flat[1 - b][:, j * P:(j + 1) * P], ident[:])
                        last.then_inc(s["l_in_psum"], 1)
                    if main and slot == 1:
                        if k == 0:
                            pe.wait_ge(s["a_ready"], after(HP * GT * (g - 1) - 1))
                        values(g, k)
                    if main and not (isinstance(g, int) and g == G - 1):
                        if st == 2 * KW + 3:
                            transposes(g + 1)
                        if 3 <= slot < 3 + NG and k == 3:
                            features(g + 1, slot - 3)
                    item = head_pair(g, p, st - WIDE - 2, tail, rest)
                    if item:
                        gt, own, j, hp = item
                        t = GT * gt + j
                        pe.wait_ge(s["a_ready"], after(HP * t + hp))
                        if hp == 0:
                            pe.wait_ge(s["oT_ready"], after(t - 1))
                            if j == 0:
                                pe.wait_ge(s["before_ready"], after(gt))
                        before = val[own][:, j - 1] if j else val_before
                        for blk, v in ((0, before), (1, val[own][:, j])):
                            for hh in range(2):
                                h = 2 * hp + hh
                                rows = slice((h % HG) * FT, (h % HG + 1) * FT)
                                last = nc.tensor.matmul(pO[rows, h // HG, :], v[:, h, :], wideT[hp % 2][:, hh, blk, :],
                                                        start=(blk == 0), stop=(blk == 1))
                        if hp == HP - 1:
                            last.then_inc(s["o_in_psum"], 1)
                    item = head_pair(g, p, st - WIDE, tail, rest)
                    if item:
                        gt, _, j, hp = item
                        t = GT * gt + j
                        if hp == 0:
                            pe.wait_ge(wide_loaded[j % 2], landed(GT // 2 * gt + j // 2))
                        pe.wait_ge(s["a_ready"], after(HP * t + hp - 2))
                        if j == 0 and hp == 0:
                            pe.wait_ge(s["v_ready"], after(GT * g + GT - 1) if main else after(GT * G - 1))
                        for hh in range(2):
                            for blk in range(2):
                                last = nc.tensor.transpose(
                                    pA[:, hp % 2, (2 * hh + blk) * P:(2 * hh + blk + 1) * P],
                                    wide[j % 2][:, 2 * hp + hh, blk * P:(blk + 1) * P], ident[:])
                        last.then_inc(s["a_in_psum"], 1)
                    item = tile_done(g, p, st - WIDE - 6, tail, rest)
                    if item:
                        gt, _, j = item
                        t = GT * gt + j
                        pe.wait_ge(s["oT_ready"], after(t))
                        pe.wait_ge(s["y_added"], after(t - 2))
                        for q in range(NG):
                            last = nc.tensor.matmul(pF[:, j % 2, 0:D], oT[:, q, :], wt["proj"][:, q, :],
                                                    start=(q == 0), stop=(q == NG - 1))
                        last.then_inc(s["y_in_psum"], 1)

            all_groups(pe, group)

        @block.scalar
        def _(act):
            for n in ("xnT_ready", "f_ready", "gelu_ready", "tanh_ready", "exp_ready", "oT_ready"):
                act.sem_inc(s[n], LEAD)

            def copy_xnT(g):
                act.wait_ge(s["xT_in_psum"], after(g))
                act.wait_ge(s["v_in_psum"], after(GT * g - 1))
                nc.scalar.activation(xnT[:], pF[:], ACT.Copy).then_inc(s["xnT_ready"], 1)

            def copy_features(g, p, m):
                act.wait_ge(s["f_in_psum"], after(NG * g + m))
                nc.scalar.activation(feat[p][:, m, W:W + GW], pF[:, m % 2, :], ACT.Copy).then_inc(s["f_ready"], 1)

            copy_xnT(0)
            for m in range(NG):
                copy_features(0, 0, m)
            act.wait_ge(s["setup"], 6)

            def group(g, p, main, tail, rest):
                for st in range(W):
                    slot, k = divmod(st, KW)
                    wg = NW * g + slot
                    if main:
                        act.wait_ge(s["diff_dve"], after(W * g + st))
                        act.wait_ge(s["diff_pool"], after(W * g + st))
                        nc.scalar.activation(pair[st % RING][:], pair[st % RING][:], ACT.Gelu,
                                             bias=wt["offset"][:, st:st + 1]).then_inc(s["gelu_ready"], 1)
                    if k == 3 and (main or (tail and slot == 0)) and not (isinstance(g, int) and wg == 0):
                        act.wait_ge(s["l_in_psum"], after(wg - 1))
                        act.wait_ge(s["logit_ready"], after(wg - 2))
                        nc.scalar.activation(damage[:], pL[:].rearrange("p j (q two x) -> p j q two x", q=NG, two=2)[:, :, :, 1, :],
                                             ACT.Tanh, scale=0.5, bias=wt["half_damage_b"][:]).then_inc(s["tanh_ready"], 1)
                    if main and not (isinstance(g, int) and g == G - 1):
                        if st == 3 * KW:
                            copy_xnT(g + 1)
                        if 4 <= slot < 4 + NG and k == 1:
                            copy_features(g + 1, 1 - p, slot - 4)
                    if tail and st == EXPS:
                        for j in range(GT):
                            t = GT * (g - 1) + j
                            act.wait_ge(s["soft_step"], after(2 * t + 1))
                            bond = logit[1 - p][:, j].rearrange("p w h k -> p (w h k)")
                            nc.scalar.activation(bond, bond, ACT.Exp).then_inc(s["exp_ready"], 1)
                    item = tile_done(g, p, st - WIDE - 3, tail, rest)
                    if item:
                        gt, _, j = item
                        t = GT * gt + j
                        act.wait_ge(s["o_in_psum"], after(t))
                        act.wait_ge(s["y_in_psum"], after(t - 1))
                        nc.scalar.activation(oT[:], pO[:], ACT.Copy).then_inc(s["oT_ready"], 1)

            all_groups(act, group)

        @block.gpsimd
        def _(pool):
            for n in ("diff_pool", "masked", "halo_ready"):
                pool.sem_inc(s[n], LEAD)
            for p in range(2):
                nc.gpsimd.memset(val[p][:], 0.0).then_inc(s["setup"], 1)
            nc.gpsimd.memset(feat[1][:, :, GW:GW + W], 0.0).then_inc(s["setup"], 1)
            pool.wait_ge(s["setup"], 6)

            def halo(g, p):
                pool.wait_ge(s["f_ready"], after(NG * g - 1))
                pool.wait_ge(s["diff_dve"], after(W * (g - 1) - 1))
                pool.sem_inc(s["pool_turn"], 1)
                nc.gpsimd.tensor_copy(feat[p][:, :, 0:W], feat[1 - p][:, :, GW:GW + W]).then_inc(s["halo_ready"], 1)

            halo(0, 0)

            def group(g, p, main, tail, rest):
                if main:
                    pool.wait_ge(s["f_ready"], after(NG * g + NG - 1))
                    pool.wait_ge(s["halo_ready"], after(g))
                for st in range(W):
                    if main:
                        if isinstance(g, int) and W * g + st == RING - 1:
                            pool.wait_ge(s["band_zeroed"], 32)
                        pool.wait_ge(s["reduced"], after(W * g + st - RING))
                        nc.gpsimd.tensor_tensor(
                            pair[st % RING][:, :, DVE_TOKENS:GW], feat[p][:, :, st + 1 + DVE_TOKENS:st + 1 + GW],
                            feat[p][:, :, W + DVE_TOKENS:W + GW], ALU.subtract).then_inc(s["diff_pool"], 1)
                    if isinstance(g, int) and g == 1 and st == SOFT:
                        pool.wait_ge(s["logit_ready"], after(NW - 1))
                        first = logit[0][:, 0]
                        nc.gpsimd.affine_select(out=first, in_=first, compare_op=ALU.is_ge, fill=-1e30,
                                                base=-(W - 1), pattern=[[KW, NW], [0, H], [1, KW]],
                                                channel_multiplier=1).then_inc(s["masked"], 1)
                    if main and st == W - 2 * KW and not (isinstance(g, int) and g == G - 1):
                        halo(g + 1, 1 - p)

            all_groups(pool, group)

        @block.vector
        def _(dve):
            nc.vector.memset(pair[RING - 1][:], 0.0).then_inc(s["zeros_ready"], 1)
            for n in ("xn_ready", "v_ready", "before_ready", "diff_dve", "flat_ready", "logit_ready", "soft_step", "prob_step",
                      "a_ready", "y_added"):
                dve.sem_inc(s[n], LEAD)

            def normalise(g):
                dve.wait_ge(s["xT_in_psum"], after(g - 1))
                for j in range(GT):
                    t = GT * g + j
                    nc.vector.tensor_scalar(xn[:, j:j + 1, :], x_res[:, at(t), :], mean[:, at(t)],
                                            rstd[:, at(t)], ALU.subtract, ALU.mult).then_inc(s["xn_ready"], 1)

            normalise(0)
            for p in range(2):
                nc.vector.memset(wide[p][:, :, 0:P - W], 0.0).then_inc(s["setup"], 1)
            nc.vector.memset(wideT[0][:], 0.0).then_inc(s["setup"], 1)
            dve.wait_ge(s["setup"], 6)

            def group(g, p, main, tail, rest):
                if main:
                    dve.wait_ge(s["f_ready"], after(NG * g + NG - 1))
                    dve.wait_ge(s["halo_ready"], after(g))
                for st in range(W):
                    slot, k = divmod(st, KW)
                    b = slot % 2
                    wg = NW * g + slot
                    if main:
                        if isinstance(g, int) and W * g + st == RING - 1:
                            dve.wait_ge(s["band_zeroed"], 32)
                        dve.wait_ge(s["reduced"], after(W * g + st - RING))
                        nc.vector.tensor_tensor(
                            pair[st % RING][:, :, 0:DVE_TOKENS], feat[p][:, :, st + 1:st + 1 + DVE_TOKENS],
                            feat[p][:, :, W:W + DVE_TOKENS], ALU.subtract).then_inc(s["diff_dve"], 1)
                    if k == 2 and (main or (tail and slot < 2)) and not (isinstance(g, int) and wg < 2):
                        own, place = (p, slot - 2) if slot >= 2 else (1 - p, NW - 2 + slot)
                        dve.wait_ge(s["tanh_ready"], after(wg - 2))
                        nc.vector.scalar_tensor_tensor(
                            out=logit[own][:, :, place].rearrange("p j (q h) k -> p j q (h k)", q=NG),
                            in0=damage[:], scalar=-5.0,
                            in1=pL[:].rearrange("p j (q two x) -> p j q two x", q=NG, two=2)[:, :, :, 0, :],
                            op0=ALU.mult, op1=ALU.add).then_inc(s["logit_ready"], 1)
                    if k == 3 and (main or (tail and slot == 0)) and not (isinstance(g, int) and wg == 0):
                        dve.wait_ge(s["reduced"], after(KW * wg - 1))
                        dve.wait_ge(s["l_in_psum"], after(wg - 3))
                        nc.vector.tensor_copy(flat[1 - b][:], pW[:, 1 - b, :]).then_inc(s["flat_ready"], 1)
                    if st == 2 * KW - 1:
                        if tail:
                            dve.wait_ge(s["o_in_psum"], after(GT * (g - 2)))
                            dve.wait_ge(s["v_ready"], after(GT * (g - 1) - 1))
                            nc.vector.tensor_copy(val_before[:], val[p][:, GT - 1]).then_inc(s["before_ready"], 1)
                        if main:
                            dve.wait_ge(s["o_in_psum"], after(GT * (g - 1) - 1))
                            dve.wait_ge(s["before_ready"], after(g - 1))
                    if main and slot == 2:
                        dve.wait_ge(s["v_in_psum"], after(GT * g + k))
                        nc.vector.tensor_copy(val[p][:, k, :, 0:BD], pA[:, k % 2, 0:D].rearrange("p (h e) -> p h e", e=BD)
                                              ).then_inc(s["v_ready"], 1)
                    if main and st == KW + 3 and not (isinstance(g, int) and g == G - 1):
                        normalise(g + 1)
                    if tail and SOFT <= st < SOFT + GT * KW and k < 2:
                        j = (st - SOFT) // KW
                        t = GT * (g - 1) + j
                        bond = logit[1 - p][:, j]
                        if k == 0:
                            if isinstance(g, int) and t == 0:
                                dve.wait_ge(s["masked"], after(0))
                            dve.wait_ge(s["logit_ready"], after(NW * g - 1))
                            dve.wait_ge(s["soft_step"], after(2 * t - 1))
                            nc.vector.tensor_reduce(top[:], bond.rearrange("p w h k -> p h w k"), AX.XY, ALU.max
                                                    ).then_inc(s["soft_step"], 1)
                        else:
                            dve.wait_ge(s["soft_step"], after(2 * t))
                            nc.vector.tensor_tensor(bond, bond, spread(spread(top[:], 1, NW), 3, KW), ALU.subtract
                                                    ).then_inc(s["soft_step"], 1)
                    if tail and PROB <= st < PROB + GT * KW and k < 2:
                        j = (st - PROB) // KW
                        t = GT * (g - 1) + j
                        bond = logit[1 - p][:, j]
                        if k == 0:
                            dve.wait_ge(s["exp_ready"], after(t))
                            dve.wait_ge(s["prob_step"], after(3 * t - 1))
                            nc.vector.tensor_reduce(total[:], bond.rearrange("p w h k -> p h w k"), AX.XY, ALU.add
                                                    ).then_inc(s["prob_step"], 1)
                            dve.wait_ge(s["prob_step"], after(3 * t))
                            nc.vector.reciprocal(total[:], total[:]).then_inc(s["prob_step"], 1)
                        else:
                            dve.wait_ge(s["prob_step"], after(3 * t + 1))
                            dve.wait_ge(s["prob_stored"], landed(t - 1))
                            nc.vector.tensor_tensor(prob[:].rearrange("p h (w k) -> p w h k", k=KW), bond,
                                                    spread(spread(total[:], 1, NW), 3, KW), ALU.mult
                                                    ).then_inc(s["prob_step"], 1)
                    item = head_pair(g, p, st - WIDE - COPY_LAG, tail, rest)
                    if item:
                        gt, _, j, hp = item
                        t = GT * gt + j
                        dve.wait_ge(s["a_in_psum"], after(HP * t + hp))
                        nc.vector.tensor_copy(wideT[hp % 2][:].rearrange("p h b t -> p (h b t)"), pA[:, hp % 2, :]
                                              ).then_inc(s["a_ready"], 1)
                    item = tile_done(g, p, st - WIDE - 10, tail, rest)
                    if item:
                        gt, _, j = item
                        t = GT * gt + j
                        dve.wait_ge(s["y_in_psum"], after(t))
                        nc.vector.tensor_tensor(x_res[:, at(t), :], x_res[:, at(t), :], pF[:, j % 2:j % 2 + 1, 0:D],
                                                ALU.add).then_inc(s["y_added"], 1)

            all_groups(dve, group)


def macaron_kernel(nc, a, out):
    x_in = a["L0_attn_x"]
    T = x_in.shape[1]
    NT = T // P
    E, _, F = a["L0_ffn_w1"].shape
    C = math.ceil(T * 2 / E * 1.2)
    H, BD = 16, 16
    xe = nc.dram_tensor("xe", [E * C + 2 * T, D], F32).ap()
    ye = nc.dram_tensor("ye", [E * C, D], F32).ap()
    with ExitStack() as program:
        ph = Phase(nc, program, "all")
        x_res = ph.sb("x_res", [P, NT, D])
        mean, rstd, stats = ph.sb("mean", [P, NT]), ph.sb("rstd", [P, NT]), ph.sb("stats", [P, NT, 6])
        gather_row, weight = ph.sb("gather_row", [P, NT, 2], I32), ph.sb("weight", [P, NT, 2])
        cst = make_constants(nc, ph, NT, E, C, H, BD)

        def layer_norm(tag, taken=True, moves=(), x_in=None):
            layer_norm_stats(nc, tag, x_res, stats, mean, rstd, cst["neg_half"], NT, taken, moves, x_in)

        def experts(tag, first):
            layer_norm(tag + "_ln", taken=not first, x_in=x_in if first else None)
            moe_route(nc, tag + "_route", T, E, C, x_res, mean, rstd, cst, a["L0_ffn_gate_w"],
                      a["L0_ffn_gate_b"], xe, gather_row, weight, first)
            moe_experts(nc, tag + "_experts", E, C, F, xe, ye, cst, a["L0_ffn_w1"], a["L0_ffn_b1"],
                        a["L0_ffn_w2"], a["L0_ffn_b2"])
            moe_combine(nc, tag + "_combine", T, x_res, ye, gather_row, weight, stats)

        experts("moe0", True)
        layer_norm("linear_ln")
        linear_attention(nc, "linear", T, H, BD, x_res, mean, rstd, cst, a["L0_attn_qkv_w"], a["L0_attn_qkv_b"],
                         a["L0_attn_out_w"], a["L0_attn_out_b"], stats)
        experts("moe1", False)

        HID = a["L1_ffn_W_exp"].shape[1]
        shapes = {"w_up": [P, DK, HID], "b_up": [P, HID // P], "w_down": [P, HID // P, D], "b_down": [P, D]}
        stored = {n: nc.dram_tensor(n + "_dram", shape, F32).ap() for n, shape in shapes.items()}

        with ExitStack() as memory:
            fold = Phase(nc, memory, "folded0")
            folded = {n: fold.sb(n, shape) for n, shape in shapes.items()}
            fold_butterflies(nc, "fold", cst, a["L1_ffn_W_exp"], a["L1_ffn_b_exp"], a["L1_ffn_up_weights"],
                             a["L1_ffn_up_bias"], a["L1_ffn_down_weights"], a["L1_ffn_W_con"], a["L1_ffn_b_con"],
                             a["L1_ffn_down_bias"], folded)
            layer_norm("ffn0_ln")
            butterfly_ffn(nc, "ffn0", T, x_res, mean, rstd, cst, folded, stats,
                          [(stored[n], folded[n][:]) for n in shapes])
        layer_norm("window_ln")
        window_attention(nc, "window", T, H, BD, x_res, mean, rstd, cst, a)
        with ExitStack() as memory:
            fold = Phase(nc, memory, "folded1")
            folded = {n: fold.sb(n, shape) for n, shape in shapes.items()}
            layer_norm("ffn1_ln", taken=False, moves=[(folded[n][:], stored[n]) for n in shapes])
            butterfly_ffn(nc, "ffn1", T, x_res, mean, rstd, cst, folded, None, out=out)


def kernel(**inputs):
    import numpy as _np
    import concourse.bacc as _bacc
    from concourse import mybir as _mybir
    from concourse.bass_utils import run_bass_kernel_spmd as _run

    nc = _bacc.Bacc("TRN2", target_bir_lowering=False, num_devices=1)
    arrays, aps = {}, {}
    for name, value in inputs.items():
        a = _np.ascontiguousarray(value)
        arrays[f"in_{name}_dram"] = a
        aps[name] = nc.dram_tensor(f"in_{name}_dram", a.shape, _mybir.dt.from_np(a.dtype), kind="ExternalInput").ap()
    shape = inputs["L0_attn_x"].shape
    out = nc.dram_tensor("out_0_dram", shape, F32, kind="ExternalOutput").ap()
    macaron_kernel(nc, aps, out)
    r = _run(nc, [arrays], core_ids=[0])
    return r.results[0]["out_0_dram"]
```
